# Optimizing a Trainium2 kernel written in Bass

```python
import numpy as np
import jax
import jax.numpy as jnp

def _softmax(x, axis=-1):
    return jax.nn.softmax(x, axis=axis)

def _gelu(x):
    return jax.nn.gelu(x, approximate=True)

def _silu(x):
    return jax.nn.silu(x)

def _sigmoid(x):
    return jax.nn.sigmoid(x)

def _layernorm(x, axis=-1, eps=1e-05):
    m = jnp.mean(x, axis=axis, keepdims=True)
    v = jnp.var(x, axis=axis, keepdims=True)
    return (x - m) / jnp.sqrt(v + eps)

def _scatter_add(tgt, idx, src, axis=0):
    return tgt.at[idx].add(src)

def _segment_sum(src, seg, n):
    return jax.ops.segment_sum(src, seg, n)
kernel_name = 'mk_perceiver_d4_seqx_r4_16a352'

def setup_inputs(seed: int=0):
    np.random.seed(seed)
    _w = jnp.asarray

    def _rec_inputs():
        import jax
        import jax.numpy as jnp
        _rk = jax.random.key(seed)
        x = -0.0005146 + 1 * jax.random.normal(jax.random.fold_in(_rk, 1), (2, 64, 256), jnp.float32)
        _lenS = 64 - jax.random.randint(jax.random.fold_in(_rk, 7), (2,), 0, max(1, 64 // 4) + 1, jnp.int32)
        _lenS2 = 1024 - jax.random.randint(jax.random.fold_in(_rk, 8), (2,), 0, max(1, 1024 // 4) + 1, jnp.int32)
        _ctx_768P = jax.random.normal(jax.random.fold_in(_rk, 11), (2, 16, 192), jnp.float32)
        _ctx_768c = jax.random.dirichlet(jax.random.fold_in(_rk, 511), 0.3 * jnp.ones((16,), jnp.float32), (2, 1024))
        _ctx_768t = jnp.einsum('bsk,bkd->bsd', _ctx_768c, _ctx_768P)
        _ctx_768t = _ctx_768t * jax.lax.rsqrt(jnp.mean(jnp.square(_ctx_768t)) + 1e-12) * 0.953939
        ctx_768 = -0.00040386 + 0.999972 * (_ctx_768t + 0.3 * jax.random.normal(jax.random.fold_in(_rk, 611), (2, 1024, 192), jnp.float32))
        _validS = jnp.arange(64)[None, :] < _lenS[:, None]
        _validS2 = jnp.arange(1024)[None, :] < _lenS2[:, None]
        _causal = jnp.tril(jnp.ones((64, 64), dtype=bool))
        mask_BxS2_bk0 = jnp.logical_not(jnp.broadcast_to(_validS2[:, :], (2, 1024)))
        return (x, ctx_768, mask_BxS2_bk0)
    x, ctx_768, mask_BxS2_bk0 = _rec_inputs()

    def _L0_xattn_setup():
        import jax, jax.numpy as jnp
        import numpy as np
        DIM_IN, DIM_LAT, DIM_HEAD = (192, 256, 64)
        INNER = max(DIM_LAT, DIM_IN)
        HEADS = INNER // DIM_HEAD
        SCALE = DIM_HEAD ** (-0.5)
        RMS_EPS = 1e-08
        LN_EPS = 1e-05

        def layernorm(x, g, b):
            mu = jnp.mean(x, axis=-1, keepdims=True)
            var = jnp.mean((x - mu) ** 2, axis=-1, keepdims=True)
            return (x - mu) * jax.lax.rsqrt(var + LN_EPS) * g + b

        def rmsnorm(x, gamma):
            norm = jnp.sqrt(jnp.sum(x * x, axis=-1, keepdims=True)) * x.shape[-1] ** (-0.5)
            return x / jnp.maximum(norm, RMS_EPS) * gamma
        key = jax.random.key(seed)
        ks = jax.random.split(key, 12)
        b, n, m = (4, 1024, 128)
        x = jax.random.normal(ks[0], (b, n, DIM_IN), jnp.float32)
        latents = jax.random.normal(ks[1], (b, m, DIM_LAT), jnp.float32)
        mask = jax.random.randint(ks[2], (b, n), 0, 2).astype(bool)
        s = lambda k, sh, fan: jax.random.normal(k, sh, jnp.float32) * fan ** (-0.5)
        return {'x': x, 'latents': latents, 'mask': mask, 'ln_x_g': jnp.ones((DIM_IN,), jnp.float32), 'ln_x_b': jnp.zeros((DIM_IN,), jnp.float32), 'ln_l_g': jnp.ones((DIM_LAT,), jnp.float32), 'ln_l_b': jnp.zeros((DIM_LAT,), jnp.float32), 'qn_g': jnp.ones((DIM_HEAD,), jnp.float32), 'kn_g': jnp.ones((DIM_HEAD,), jnp.float32), 'Wq': s(ks[3], (INNER, DIM_LAT), DIM_LAT), 'Wkv': s(ks[4], (2 * INNER, DIM_IN), DIM_IN), 'Wlkv': s(ks[5], (2 * INNER, DIM_LAT), DIM_LAT), 'Wo': s(ks[6], (DIM_LAT, INNER), INNER), 'bo': jnp.zeros((DIM_LAT,), jnp.float32)}
    _L0_xattn_all = _L0_xattn_setup()
    _L0_xattn_in = {k: v for k, v in _L0_xattn_all.items() if k in ('ln_x_g', 'ln_x_b', 'ln_l_g', 'ln_l_b', 'qn_g', 'kn_g', 'Wq', 'Wkv', 'Wlkv', 'Wo', 'bo')}
    del _L0_xattn_all

    def _L0_attn_setup():
        import jax, jax.numpy as jnp
        import numpy as np
        DIM = 256
        DIM_HEAD = 64
        HEADS = 8
        INNER = DIM_HEAD * HEADS
        SCALE = DIM_HEAD ** (-0.5)
        COS_SCALE = 1.0

        def layer_norm(x, w, b, eps=1e-05):
            mu = jnp.mean(x, axis=-1, keepdims=True)
            var = jnp.var(x, axis=-1, keepdims=True)
            return (x - mu) * jax.lax.rsqrt(var + eps) * w + b
        key = jax.random.key(seed)
        ks = jax.random.split(key, 6)
        x = jax.random.normal(ks[0], (4, 512, DIM), dtype=jnp.float32)
        Wq = jax.random.normal(ks[1], (DIM, INNER), dtype=jnp.float32) * DIM ** (-0.5)
        Wkv = jax.random.normal(ks[2], (DIM, 2 * DIM_HEAD), dtype=jnp.float32) * DIM ** (-0.5)
        Wo = jax.random.normal(ks[3], (INNER, DIM), dtype=jnp.float32) * INNER ** (-0.5)
        norm_w = jnp.ones((DIM,), jnp.float32)
        norm_b = jnp.zeros((DIM,), jnp.float32)
        out_norm_w = jnp.ones((DIM,), jnp.float32)
        out_norm_b = jnp.zeros((DIM,), jnp.float32)
        return {'x': x, 'Wq': Wq, 'Wkv': Wkv, 'Wo': Wo, 'norm_w': norm_w, 'norm_b': norm_b, 'out_norm_w': out_norm_w, 'out_norm_b': out_norm_b}
    _L0_attn_all = _L0_attn_setup()
    _L0_attn_in = {k: v for k, v in _L0_attn_all.items() if k in ('Wq', 'Wkv', 'Wo', 'norm_w', 'norm_b', 'out_norm_w', 'out_norm_b')}
    del _L0_attn_all

    def _L0_ffn_setup():
        import jax, jax.numpy as jnp
        import numpy as np
        HIDDEN = 256
        NUM_EXPERTS = 8
        TOP_K = 2
        key = jax.random.key(seed)
        k_x, k_r, k_w1, k_w2 = jax.random.split(key, 4)
        x = jax.random.normal(k_x, (4, 512, HIDDEN), dtype=jnp.float32)
        router_w = jax.random.normal(k_r, (NUM_EXPERTS, HIDDEN), dtype=jnp.float32) * HIDDEN ** (-0.5)
        w1 = jax.random.normal(k_w1, (NUM_EXPERTS, HIDDEN, 2 * HIDDEN), dtype=jnp.float32) * HIDDEN ** (-0.5)
        w2 = jax.random.normal(k_w2, (NUM_EXPERTS, 2 * HIDDEN, HIDDEN), dtype=jnp.float32) * (2 * HIDDEN) ** (-0.5)
        return {'x': x, 'router_w': router_w, 'w1': w1, 'w2': w2}
    _L0_ffn_all = _L0_ffn_setup()
    _L0_ffn_in = {k: v for k, v in _L0_ffn_all.items() if k in ('router_w', 'w1', 'w2')}
    del _L0_ffn_all

    def _L1_xattn_setup():
        import jax, jax.numpy as jnp
        import numpy as np
        QUERY_DIM = 256
        KEY_DIM = 192
        NUM_HEADS = 16
        HEAD_DIM = QUERY_DIM // NUM_HEADS
        SCALE = HEAD_DIM ** (-0.5)
        key = jax.random.key(seed)
        ks = jax.random.split(key, 11)
        B, Nq, Nk = (4, 1024, 256)
        s_q = QUERY_DIM ** (-0.5)
        s_k = KEY_DIM ** (-0.5)
        return {'query': jax.random.normal(ks[0], (B, Nq, QUERY_DIM), jnp.float32), 'key': jax.random.normal(ks[1], (B, Nk, KEY_DIM), jnp.float32), 'value': jax.random.normal(ks[2], (B, Nk, KEY_DIM), jnp.float32), 'Wq': jax.random.normal(ks[3], (QUERY_DIM, QUERY_DIM), jnp.float32) * s_q, 'bq': jnp.zeros((QUERY_DIM,), jnp.float32), 'Wk': jax.random.normal(ks[4], (KEY_DIM, QUERY_DIM), jnp.float32) * s_k, 'bk': jnp.zeros((QUERY_DIM,), jnp.float32), 'Wv': jax.random.normal(ks[5], (KEY_DIM, QUERY_DIM), jnp.float32) * s_k, 'bv': jnp.zeros((QUERY_DIM,), jnp.float32), 'Wo': jax.random.normal(ks[6], (QUERY_DIM, QUERY_DIM), jnp.float32) * s_q, 'bo': jnp.zeros((QUERY_DIM,), jnp.float32)}
    _L1_xattn_all = _L1_xattn_setup()
    _L1_xattn_in = {k: v for k, v in _L1_xattn_all.items() if k in ('Wq', 'bq', 'Wk', 'bk', 'Wv', 'bv', 'Wo', 'bo')}
    del _L1_xattn_all

    def _L1_attn_setup():
        import jax, jax.numpy as jnp
        import numpy as np
        B, L, D = (8, 1024, 256)
        K = 32
        key = jax.random.key(seed)
        kx, kw, kb = jax.random.split(key, 3)
        x = jax.random.normal(kx, (B, L, D), dtype=jnp.float32)
        W = jax.random.normal(kw, (K, D), dtype=jnp.float32) * 0.02
        b = jax.random.normal(kb, (K,), dtype=jnp.float32) * 0.02
        return {'x': x, 'W': W, 'b': b}
    _L1_attn_all = _L1_attn_setup()
    _L1_attn_in = {k: v for k, v in _L1_attn_all.items() if k in ('W', 'b')}
    del _L1_attn_all

    def _L1_ffn_setup():
        import jax, jax.numpy as jnp
        import numpy as np
        B, S, D, E, F, TOP_K = (4, 512, 256, 8, 1024, 2)
        key = jax.random.key(seed)
        k0, k1, k2, k3 = jax.random.split(key, 4)
        init = lambda k, shape, fan: (jax.random.normal(k, shape, jnp.float32) / np.sqrt(fan)).astype(jnp.float32)
        return {'x': jax.random.normal(k0, (B, S, D), jnp.float32), 'gate_w': init(k1, (D, E), D), 'w1': init(k2, (E, D, F), D), 'b1': jnp.zeros((E, F), jnp.float32), 'w2': init(k3, (E, F, D), F), 'b2': jnp.zeros((E, D), jnp.float32)}
    _L1_ffn_all = _L1_ffn_setup()
    _L1_ffn_in = {k: v for k, v in _L1_ffn_all.items() if k in ('gate_w', 'w1', 'b1', 'w2', 'b2')}
    del _L1_ffn_all

    def _L2_xattn_setup():
        import jax, jax.numpy as jnp
        import numpy as np
        HEADS = 16
        DIM_HEAD = 64
        QUERY_DIM = 256
        CONTEXT_DIM = 192
        INNER = HEADS * DIM_HEAD
        SCALE = DIM_HEAD ** (-0.5)
        key = jax.random.key(seed)
        ks = jax.random.split(key, 7)
        B, Sq, Skv = (4, 512, 512)
        x = jax.random.normal(ks[0], (B, Sq, QUERY_DIM), dtype=jnp.float32)
        context = jax.random.normal(ks[1], (B, Skv, CONTEXT_DIM), dtype=jnp.float32)
        w_q = jax.random.normal(ks[2], (QUERY_DIM, INNER), dtype=jnp.float32) / np.sqrt(QUERY_DIM)
        w_k = jax.random.normal(ks[3], (CONTEXT_DIM, INNER), dtype=jnp.float32) / np.sqrt(CONTEXT_DIM)
        w_v = jax.random.normal(ks[4], (CONTEXT_DIM, INNER), dtype=jnp.float32) / np.sqrt(CONTEXT_DIM)
        w_o = jax.random.normal(ks[5], (INNER, QUERY_DIM), dtype=jnp.float32) / np.sqrt(INNER)
        b_o = jax.random.normal(ks[6], (QUERY_DIM,), dtype=jnp.float32) * 0.02
        return {'x': x, 'context': context, 'w_q': w_q, 'w_k': w_k, 'w_v': w_v, 'w_o': w_o, 'b_o': b_o}
    _L2_xattn_all = _L2_xattn_setup()
    _L2_xattn_in = {k: v for k, v in _L2_xattn_all.items() if k in ('w_q', 'w_k', 'w_v', 'w_o', 'b_o')}
    del _L2_xattn_all

    def _L2_attn_setup():
        import jax, jax.numpy as jnp
        import numpy as np
        DIM = 256
        HEADS = 16
        HD = DIM // HEADS
        HID = 4 * DIM
        TPF = 1374
        LR = 0.1
        NS_ITERS = 5
        TTT_STEPS = 2
        B, S = (2, 4)
        SN = S * TPF

        def _newton_schulz(G, iters=NS_ITERS):
            a, b, c = (3.4445, -4.775, 2.0315)
            X = G / (jnp.linalg.norm(G) + 1e-07)
            transposed = G.shape[0] > G.shape[1]
            if transposed:
                X = X.T
            for _ in range(iters):
                A = X @ X.T
                X = a * X + (b * A + c * (A @ A)) @ X
            return X.T if transposed else X

        def _muon_update(p, g):
            return p - LR * _newton_schulz(g)
        key = jax.random.key(seed)
        ks = jax.random.split(key, 8)
        inp = {'x': jax.random.normal(ks[0], (B, SN, DIM), jnp.float32), 'qkv_w': jax.random.normal(ks[1], (DIM, 3 * DIM), jnp.float32) * DIM ** (-0.5), 'qkv_b': jnp.zeros((3 * DIM,), jnp.float32), 'qn_scale': jnp.ones((HD,), jnp.float32), 'qn_bias': jnp.zeros((HD,), jnp.float32), 'kn_scale': jnp.ones((HD,), jnp.float32), 'kn_bias': jnp.zeros((HD,), jnp.float32), 'ttt_gate': jax.random.normal(ks[2], (DIM, HID), jnp.float32) * DIM ** (-0.5), 'ttt_val': jax.random.normal(ks[3], (DIM, HID), jnp.float32) * DIM ** (-0.5), 'ttt_proj': jax.random.normal(ks[4], (HID, DIM), jnp.float32) * HID ** (-0.5), 'proj_w': jax.random.normal(ks[5], (DIM, DIM), jnp.float32) * DIM ** (-0.5), 'proj_b': jnp.zeros((DIM,), jnp.float32)}
        return inp
    _L2_attn_all = _L2_attn_setup()
    _L2_attn_in = {k: v for k, v in _L2_attn_all.items() if k in ('qkv_w', 'qkv_b', 'qn_scale', 'qn_bias', 'kn_scale', 'kn_bias', 'ttt_gate', 'ttt_val', 'ttt_proj', 'proj_w', 'proj_b')}
    del _L2_attn_all

    def _L2_ffn_setup():
        import jax, jax.numpy as jnp
        import numpy as np
        from jax import lax
        DIM = 256
        HID = 512
        E = 8
        K = 2
        B, T = (2, 128)
        key = jax.random.key(seed)
        ks = jax.random.split(key, 5)
        scale = 1.0 / np.sqrt(DIM)
        x = jax.random.normal(ks[0], (B, T, DIM), dtype=jnp.float32)
        router_w = jax.random.normal(ks[1], (E, DIM), dtype=jnp.float32) * scale
        w_gate = jax.random.normal(ks[2], (E, HID, DIM), dtype=jnp.float32) * scale
        w_up = jax.random.normal(ks[3], (E, HID, DIM), dtype=jnp.float32) * scale
        w_down = jax.random.normal(ks[4], (E, DIM, HID), dtype=jnp.float32) * (1.0 / np.sqrt(HID))
        return {'x': x, 'router_w': router_w, 'w_gate': w_gate, 'w_up': w_up, 'w_down': w_down}
    _L2_ffn_all = _L2_ffn_setup()
    _L2_ffn_in = {k: v for k, v in _L2_ffn_all.items() if k in ('router_w', 'w_gate', 'w_up', 'w_down')}
    del _L2_ffn_all

    def _L3_xattn_setup():
        import jax, jax.numpy as jnp
        import numpy as np
        IMAGE_DIM = 256
        TEXT_DIM = 192
        NUM_HEADS = 16
        HEAD_DIM = IMAGE_DIM // NUM_HEADS
        key = jax.random.key(seed)
        ks = jax.random.split(key, 14)
        B, N, M = (4, 1024, 128)
        s_img = 1.0 / np.sqrt(IMAGE_DIM)
        s_txt = 1.0 / np.sqrt(TEXT_DIM)
        s_ff = 1.0 / np.sqrt(2 * IMAGE_DIM)
        return {'x': jax.random.normal(ks[0], (B, N, IMAGE_DIM), jnp.float32), 'y': jax.random.normal(ks[1], (B, M, TEXT_DIM), jnp.float32), 'Wq': jax.random.normal(ks[2], (IMAGE_DIM, IMAGE_DIM), jnp.float32) * s_img, 'bq': jax.random.normal(ks[3], (IMAGE_DIM,), jnp.float32) * s_img, 'Wk': jax.random.normal(ks[4], (TEXT_DIM, IMAGE_DIM), jnp.float32) * s_txt, 'bk': jax.random.normal(ks[5], (IMAGE_DIM,), jnp.float32) * s_txt, 'Wv': jax.random.normal(ks[6], (TEXT_DIM, IMAGE_DIM), jnp.float32) * s_txt, 'bv': jax.random.normal(ks[7], (IMAGE_DIM,), jnp.float32) * s_txt, 'W1': jax.random.normal(ks[8], (IMAGE_DIM, 2 * IMAGE_DIM), jnp.float32) * s_img, 'b1': jax.random.normal(ks[9], (2 * IMAGE_DIM,), jnp.float32) * s_img, 'W2': jax.random.normal(ks[10], (2 * IMAGE_DIM, IMAGE_DIM), jnp.float32) * s_ff, 'b2': jax.random.normal(ks[11], (IMAGE_DIM,), jnp.float32) * s_ff}
    _L3_xattn_all = _L3_xattn_setup()
    _L3_xattn_in = {k: v for k, v in _L3_xattn_all.items() if k in ('Wq', 'bq', 'Wk', 'bk', 'Wv', 'bv', 'W1', 'b1', 'W2', 'b2')}
    del _L3_xattn_all

    def _L3_attn_setup():
        import jax, jax.numpy as jnp
        import numpy as np

        def _parallel_scan_affine(log_a, b):
            T = log_a.shape[1]
            la, bv = (log_a, b)
            stride = 1
            while stride < T:
                la_prev = jnp.roll(la, stride, axis=1).at[:, :stride, :].set(0.0)
                bv_prev = jnp.roll(bv, stride, axis=1).at[:, :stride, :].set(0.0)
                bv = jnp.exp(la) * bv_prev + bv
                la = la + la_prev
                stride *= 2
            return bv
        key = jax.random.key(seed)
        kx, kwz, kwh = jax.random.split(key, 3)
        B, T, D = (4, 1024, 256)
        x = jax.random.normal(kx, (B, T, D), dtype=jnp.float32)
        Wz = jax.random.normal(kwz, (D, D), dtype=jnp.float32) * 0.02
        bz = jnp.zeros((D,), dtype=jnp.float32)
        Wh = jax.random.normal(kwh, (D, D), dtype=jnp.float32) * 0.02
        bh = jnp.zeros((D,), dtype=jnp.float32)
        return {'x': x, 'Wz': Wz, 'bz': bz, 'Wh': Wh, 'bh': bh}
    _L3_attn_all = _L3_attn_setup()
    _L3_attn_in = {k: v for k, v in _L3_attn_all.items() if k in ('Wz', 'bz', 'Wh', 'bh')}
    del _L3_attn_all

    def _L3_ffn_setup():
        import jax, jax.numpy as jnp
        import numpy as np
        NUM_EXPERTS = 8
        TOP_K = 2
        D_MODEL = 256
        D_HID = 1024
        BATCH, SEQ = (2, 512)
        key = jax.random.key(seed)
        ks = jax.random.split(key, 5)
        s = 0.02
        return {'x': jax.random.normal(ks[0], (BATCH, SEQ, D_MODEL), dtype=jnp.float32), 'Wg': jax.random.normal(ks[1], (D_MODEL, NUM_EXPERTS), dtype=jnp.float32) * s, 'bg': jnp.zeros((NUM_EXPERTS,), dtype=jnp.float32), 'W0': jax.random.normal(ks[2], (NUM_EXPERTS, D_MODEL, D_HID), dtype=jnp.float32) * s, 'b0': jnp.zeros((NUM_EXPERTS, D_HID), dtype=jnp.float32), 'W1': jax.random.normal(ks[3], (NUM_EXPERTS, D_MODEL, D_HID), dtype=jnp.float32) * s, 'b1': jnp.zeros((NUM_EXPERTS, D_HID), dtype=jnp.float32), 'W2': jax.random.normal(ks[4], (NUM_EXPERTS, D_HID, D_MODEL), dtype=jnp.float32) * s, 'b2': jnp.zeros((NUM_EXPERTS, D_MODEL), dtype=jnp.float32)}
    _L3_ffn_all = _L3_ffn_setup()
    _L3_ffn_in = {k: v for k, v in _L3_ffn_all.items() if k in ('Wg', 'bg', 'W0', 'b0', 'W1', 'b1', 'W2', 'b2')}
    del _L3_ffn_all
    return {'x': x, 'ctx_768': ctx_768, 'mask_BxS2_bk0': mask_BxS2_bk0, 'L0_xattn_ln_x_g': _L0_xattn_in['ln_x_g'], 'L0_xattn_ln_x_b': _L0_xattn_in['ln_x_b'], 'L0_xattn_ln_l_g': _L0_xattn_in['ln_l_g'], 'L0_xattn_ln_l_b': _L0_xattn_in['ln_l_b'], 'L0_xattn_qn_g': _L0_xattn_in['qn_g'], 'L0_xattn_kn_g': _L0_xattn_in['kn_g'], 'L0_xattn_Wq': _L0_xattn_in['Wq'], 'L0_xattn_Wkv': _L0_xattn_in['Wkv'], 'L0_xattn_Wlkv': _L0_xattn_in['Wlkv'], 'L0_xattn_Wo': _L0_xattn_in['Wo'], 'L0_xattn_bo': _L0_xattn_in['bo'], 'L0_attn_Wq': _L0_attn_in['Wq'], 'L0_attn_Wkv': _L0_attn_in['Wkv'], 'L0_attn_Wo': _L0_attn_in['Wo'], 'L0_attn_norm_w': _L0_attn_in['norm_w'], 'L0_attn_norm_b': _L0_attn_in['norm_b'], 'L0_attn_out_norm_w': _L0_attn_in['out_norm_w'], 'L0_attn_out_norm_b': _L0_attn_in['out_norm_b'], 'L0_ffn_router_w': _L0_ffn_in['router_w'], 'L0_ffn_w1': _L0_ffn_in['w1'], 'L0_ffn_w2': _L0_ffn_in['w2'], 'L1_xattn_Wq': _L1_xattn_in['Wq'], 'L1_xattn_bq': _L1_xattn_in['bq'], 'L1_xattn_Wk': _L1_xattn_in['Wk'], 'L1_xattn_bk': _L1_xattn_in['bk'], 'L1_xattn_Wv': _L1_xattn_in['Wv'], 'L1_xattn_bv': _L1_xattn_in['bv'], 'L1_xattn_Wo': _L1_xattn_in['Wo'], 'L1_xattn_bo': _L1_xattn_in['bo'], 'L1_attn_W': _L1_attn_in['W'], 'L1_attn_b': _L1_attn_in['b'], 'L1_ffn_gate_w': _L1_ffn_in['gate_w'], 'L1_ffn_w1': _L1_ffn_in['w1'], 'L1_ffn_b1': _L1_ffn_in['b1'], 'L1_ffn_w2': _L1_ffn_in['w2'], 'L1_ffn_b2': _L1_ffn_in['b2'], 'L2_xattn_w_q': _L2_xattn_in['w_q'], 'L2_xattn_w_k': _L2_xattn_in['w_k'], 'L2_xattn_w_v': _L2_xattn_in['w_v'], 'L2_xattn_w_o': _L2_xattn_in['w_o'], 'L2_xattn_b_o': _L2_xattn_in['b_o'], 'L2_attn_qkv_w': _L2_attn_in['qkv_w'], 'L2_attn_qkv_b': _L2_attn_in['qkv_b'], 'L2_attn_qn_scale': _L2_attn_in['qn_scale'], 'L2_attn_qn_bias': _L2_attn_in['qn_bias'], 'L2_attn_kn_scale': _L2_attn_in['kn_scale'], 'L2_attn_kn_bias': _L2_attn_in['kn_bias'], 'L2_attn_ttt_gate': _L2_attn_in['ttt_gate'], 'L2_attn_ttt_val': _L2_attn_in['ttt_val'], 'L2_attn_ttt_proj': _L2_attn_in['ttt_proj'], 'L2_attn_proj_w': _L2_attn_in['proj_w'], 'L2_attn_proj_b': _L2_attn_in['proj_b'], 'L2_ffn_router_w': _L2_ffn_in['router_w'], 'L2_ffn_w_gate': _L2_ffn_in['w_gate'], 'L2_ffn_w_up': _L2_ffn_in['w_up'], 'L2_ffn_w_down': _L2_ffn_in['w_down'], 'L3_xattn_Wq': _L3_xattn_in['Wq'], 'L3_xattn_bq': _L3_xattn_in['bq'], 'L3_xattn_Wk': _L3_xattn_in['Wk'], 'L3_xattn_bk': _L3_xattn_in['bk'], 'L3_xattn_Wv': _L3_xattn_in['Wv'], 'L3_xattn_bv': _L3_xattn_in['bv'], 'L3_xattn_W1': _L3_xattn_in['W1'], 'L3_xattn_b1': _L3_xattn_in['b1'], 'L3_xattn_W2': _L3_xattn_in['W2'], 'L3_xattn_b2': _L3_xattn_in['b2'], 'L3_attn_Wz': _L3_attn_in['Wz'], 'L3_attn_bz': _L3_attn_in['bz'], 'L3_attn_Wh': _L3_attn_in['Wh'], 'L3_attn_bh': _L3_attn_in['bh'], 'L3_ffn_Wg': _L3_ffn_in['Wg'], 'L3_ffn_bg': _L3_ffn_in['bg'], 'L3_ffn_W0': _L3_ffn_in['W0'], 'L3_ffn_b0': _L3_ffn_in['b0'], 'L3_ffn_W1': _L3_ffn_in['W1'], 'L3_ffn_b1': _L3_ffn_in['b1'], 'L3_ffn_W2': _L3_ffn_in['W2'], 'L3_ffn_b2': _L3_ffn_in['b2']}

def reference(x, ctx_768, mask_BxS2_bk0, L0_xattn_ln_x_g, L0_xattn_ln_x_b, L0_xattn_ln_l_g, L0_xattn_ln_l_b, L0_xattn_qn_g, L0_xattn_kn_g, L0_xattn_Wq, L0_xattn_Wkv, L0_xattn_Wlkv, L0_xattn_Wo, L0_xattn_bo, L0_attn_Wq, L0_attn_Wkv, L0_attn_Wo, L0_attn_norm_w, L0_attn_norm_b, L0_attn_out_norm_w, L0_attn_out_norm_b, L0_ffn_router_w, L0_ffn_w1, L0_ffn_w2, L1_xattn_Wq, L1_xattn_bq, L1_xattn_Wk, L1_xattn_bk, L1_xattn_Wv, L1_xattn_bv, L1_xattn_Wo, L1_xattn_bo, L1_attn_W, L1_attn_b, L1_ffn_gate_w, L1_ffn_w1, L1_ffn_b1, L1_ffn_w2, L1_ffn_b2, L2_xattn_w_q, L2_xattn_w_k, L2_xattn_w_v, L2_xattn_w_o, L2_xattn_b_o, L2_attn_qkv_w, L2_attn_qkv_b, L2_attn_qn_scale, L2_attn_qn_bias, L2_attn_kn_scale, L2_attn_kn_bias, L2_attn_ttt_gate, L2_attn_ttt_val, L2_attn_ttt_proj, L2_attn_proj_w, L2_attn_proj_b, L2_ffn_router_w, L2_ffn_w_gate, L2_ffn_w_up, L2_ffn_w_down, L3_xattn_Wq, L3_xattn_bq, L3_xattn_Wk, L3_xattn_bk, L3_xattn_Wv, L3_xattn_bv, L3_xattn_W1, L3_xattn_b1, L3_xattn_W2, L3_xattn_b2, L3_attn_Wz, L3_attn_bz, L3_attn_Wh, L3_attn_bh, L3_ffn_Wg, L3_ffn_bg, L3_ffn_W0, L3_ffn_b0, L3_ffn_W1, L3_ffn_b1, L3_ffn_W2, L3_ffn_b2):
    import jax
    import jax.numpy as jnp

    def _L0_xattn_ref(x, latents, mask, ln_x_g, ln_x_b, ln_l_g, ln_l_b, qn_g, kn_g, Wq, Wkv, Wlkv, Wo, bo):
        import jax, jax.numpy as jnp
        import numpy as np
        DIM_IN, DIM_LAT, DIM_HEAD = (192, 256, 64)
        INNER = max(DIM_LAT, DIM_IN)
        HEADS = INNER // DIM_HEAD
        SCALE = DIM_HEAD ** (-0.5)
        RMS_EPS = 1e-08
        LN_EPS = 1e-05

        def layernorm(x, g, b):
            mu = jnp.mean(x, axis=-1, keepdims=True)
            var = jnp.mean((x - mu) ** 2, axis=-1, keepdims=True)
            return (x - mu) * jax.lax.rsqrt(var + LN_EPS) * g + b

        def rmsnorm(x, gamma):
            norm = jnp.sqrt(jnp.sum(x * x, axis=-1, keepdims=True)) * x.shape[-1] ** (-0.5)
            return x / jnp.maximum(norm, RMS_EPS) * gamma
        b, n, _ = x.shape
        m = latents.shape[1]
        xn = layernorm(x, ln_x_g, ln_x_b)
        ln = layernorm(latents, ln_l_g, ln_l_b)
        q = ln @ Wq.T
        kv = jnp.concatenate([xn @ Wkv.T, ln @ Wlkv.T], axis=1)
        k, v = (kv[..., :INNER], kv[..., INNER:])
        split_heads = lambda t: t.reshape(t.shape[0], t.shape[1], HEADS, DIM_HEAD).transpose(0, 2, 1, 3)
        q, k, v = (split_heads(q), split_heads(k), split_heads(v))
        qn = rmsnorm(q, qn_g) * SCALE
        kn = rmsnorm(k, kn_g)
        attn = jnp.einsum('bhid,bhjd->bhij', qn, kn)
        full_mask = jnp.pad(mask, ((0, 0), (0, m)), constant_values=True)
        attn = jnp.where(full_mask[:, None, None, :], attn, -jnp.finfo(attn.dtype).max)
        attn = jax.nn.softmax(attn, axis=-1)
        out = jnp.einsum('bhij,bhjd->bhid', attn, v)
        out = out.transpose(0, 2, 1, 3).reshape(b, m, INNER)
        return out @ Wo.T + bo

    def _L0_attn_ref(x, Wq, Wkv, Wo, norm_w, norm_b, out_norm_w, out_norm_b):
        import jax, jax.numpy as jnp
        import numpy as np
        DIM = 256
        DIM_HEAD = 64
        HEADS = 8
        INNER = DIM_HEAD * HEADS
        SCALE = DIM_HEAD ** (-0.5)
        COS_SCALE = 1.0

        def layer_norm(x, w, b, eps=1e-05):
            mu = jnp.mean(x, axis=-1, keepdims=True)
            var = jnp.var(x, axis=-1, keepdims=True)
            return (x - mu) * jax.lax.rsqrt(var + eps) * w + b
        b, n, _ = x.shape
        xn = layer_norm(x, norm_w, norm_b)
        q = xn @ Wq
        kv = xn @ Wkv
        k, v = (kv[..., :DIM_HEAD], kv[..., DIM_HEAD:])
        q = q.reshape(b, n, HEADS, DIM_HEAD).transpose(0, 2, 1, 3) * SCALE
        sim = jnp.einsum('bhid,bjd->bhij', q, k) * COS_SCALE
        attn = jax.nn.softmax(sim.astype(jnp.float32), axis=-1).astype(sim.dtype)
        out = jnp.einsum('bhij,bjd->bhid', attn, v)
        out = out.transpose(0, 2, 1, 3).reshape(b, n, INNER)
        out = out @ Wo
        return layer_norm(out, out_norm_w, out_norm_b)

    def _L0_ffn_ref(x, router_w, w1, w2):
        import jax, jax.numpy as jnp
        import numpy as np
        HIDDEN = 256
        NUM_EXPERTS = 8
        TOP_K = 2
        bsz, seq, hidden = x.shape
        tokens = x.reshape(-1, hidden)
        logits = tokens @ router_w.T
        topk_vals, topk_idx = jax.lax.top_k(logits, TOP_K)
        weights = jax.nn.softmax(topk_vals, axis=-1)
        h = jnp.einsum('td,edf->etf', tokens, w1)
        h = jax.nn.gelu(h, approximate=False)
        out_all = jnp.einsum('etf,efd->etd', h, w2)
        out_ted = jnp.transpose(out_all, (1, 0, 2))
        gathered = jnp.take_along_axis(out_ted, topk_idx[:, :, None], axis=1)
        output = jnp.sum(weights[:, :, None] * gathered, axis=1)
        return output.reshape(bsz, seq, hidden)

    def _L1_xattn_ref(query, key, value, Wq, bq, Wk, bk, Wv, bv, Wo, bo):
        import jax, jax.numpy as jnp
        import numpy as np
        QUERY_DIM = 256
        KEY_DIM = 192
        NUM_HEADS = 16
        HEAD_DIM = QUERY_DIM // NUM_HEADS
        SCALE = HEAD_DIM ** (-0.5)
        B, Nq, _ = query.shape
        Nk = key.shape[1]
        q = (query @ Wq + bq).reshape(B, Nq, NUM_HEADS, HEAD_DIM).transpose(0, 2, 1, 3)
        k = (key @ Wk + bk).reshape(B, Nk, NUM_HEADS, HEAD_DIM).transpose(0, 2, 1, 3)
        v = (value @ Wv + bv).reshape(B, Nk, NUM_HEADS, HEAD_DIM).transpose(0, 2, 1, 3)
        attn = jnp.einsum('bhqd,bhkd->bhqk', q, k) * SCALE
        attn = jax.nn.softmax(attn, axis=-1)
        out = jnp.einsum('bhqk,bhkd->bhqd', attn, v)
        out = out.transpose(0, 2, 1, 3).reshape(B, Nq, QUERY_DIM)
        return out @ Wo + bo

    def _L1_attn_ref(x, W, b):
        import jax, jax.numpy as jnp
        import numpy as np
        B, L, D = (8, 1024, 256)
        K = 32
        logits = jnp.einsum('bld,kd->blk', x, W) + b
        w = jax.nn.softmax(logits, axis=-1)
        Bn, Ln, Dn = x.shape
        Kn = w.shape[-1]
        xp = jnp.pad(x, ((0, 0), (0, Kn - 1), (0, 0)))
        out = jnp.zeros_like(x)
        for d in range(Kn):
            out = out + w[:, :, d:d + 1] * xp[:, d:d + Ln]
        return out

    def _L1_ffn_ref(x, gate_w, w1, b1, w2, b2):
        import jax, jax.numpy as jnp
        import numpy as np
        B, S, D, E, F, TOP_K = (4, 512, 256, 8, 1024, 2)
        b, s, d = x.shape
        e = gate_w.shape[1]
        xf = x.reshape(-1, d)
        t = xf.shape[0]
        logits = xf @ gate_w
        top_w, top_idx = jax.lax.top_k(logits, TOP_K)
        top_w = jax.nn.softmax(top_w.astype(jnp.float32), axis=-1).astype(x.dtype)
        combine = jnp.zeros((t, e), x.dtype).at[jnp.arange(t)[:, None], top_idx].add(top_w)
        h = jax.nn.gelu(jnp.einsum('td,edf->tef', xf, w1) + b1, approximate=False)
        y = jnp.einsum('tef,efd->ted', h, w2) + b2
        out = jnp.einsum('ted,te->td', y, combine)
        return out.reshape(b, s, d)

    def _L2_xattn_ref(x, context, w_q, w_k, w_v, w_o, b_o):
        import jax, jax.numpy as jnp
        import numpy as np
        HEADS = 16
        DIM_HEAD = 64
        QUERY_DIM = 256
        CONTEXT_DIM = 192
        INNER = HEADS * DIM_HEAD
        SCALE = DIM_HEAD ** (-0.5)
        B, Sq, _ = x.shape
        Skv = context.shape[1]
        q = (x @ w_q).reshape(B, Sq, HEADS, DIM_HEAD).transpose(0, 2, 1, 3)
        k = (context @ w_k).reshape(B, Skv, HEADS, DIM_HEAD).transpose(0, 2, 1, 3)
        v = (context @ w_v).reshape(B, Skv, HEADS, DIM_HEAD).transpose(0, 2, 1, 3)
        sim = jnp.einsum('bhid,bhjd->bhij', q, k) * SCALE
        attn = jax.nn.softmax(sim, axis=-1)
        out = jnp.einsum('bhij,bhjd->bhid', attn, v)
        out = out.transpose(0, 2, 1, 3).reshape(B, Sq, INNER)
        return out @ w_o + b_o

    def _L2_attn_ref(x, qkv_w, qkv_b, qn_scale, qn_bias, kn_scale, kn_bias, ttt_gate, ttt_val, ttt_proj, proj_w, proj_b):
        import jax, jax.numpy as jnp
        import numpy as np
        DIM = 256
        HEADS = 16
        HD = DIM // HEADS
        HID = 4 * DIM
        TPF = 1374
        LR = 0.1
        NS_ITERS = 5
        TTT_STEPS = 2
        B, S = (2, 4)
        SN = S * TPF

        def _newton_schulz(G, iters=NS_ITERS):
            a, b, c = (3.4445, -4.775, 2.0315)
            X = G / (jnp.linalg.norm(G) + 1e-07)
            transposed = G.shape[0] > G.shape[1]
            if transposed:
                X = X.T
            for _ in range(iters):
                A = X @ X.T
                X = a * X + (b * A + c * (A @ A)) @ X
            return X.T if transposed else X

        def _muon_update(p, g):
            return p - LR * _newton_schulz(g)
        Bx, SNx, _ = x.shape
        qkv = x @ qkv_w + qkv_b
        q, k, v = jnp.split(qkv, 3, axis=-1)
        q = q.reshape(Bx, SNx, HEADS, HD)
        k = k.reshape(Bx, SNx, HEADS, HD)
        q = q / (jnp.linalg.norm(q, axis=-1, keepdims=True) + 1e-06) * qn_scale + qn_bias
        k = k / (jnp.linalg.norm(k, axis=-1, keepdims=True) + 1e-06) * kn_scale + kn_bias
        q_ttt = q.reshape(-1, DIM)
        k_ttt = k.reshape(-1, DIM)
        v_ttt = v.reshape(-1, DIM)
        theta = {'gate': ttt_gate, 'val': ttt_val, 'proj': ttt_proj}

        def loss_fn(p):
            h = jax.nn.swish(k_ttt @ p['gate']) * (k_ttt @ p['val'])
            pred = h @ p['proj']
            return jnp.mean((pred - v_ttt) ** 2)
        for _ in range(TTT_STEPS):
            grads = jax.grad(loss_fn)(theta)
            theta = {kk: _muon_update(theta[kk], grads[kk]) for kk in theta}
        h_q = jax.nn.swish(q_ttt @ theta['gate']) * (q_ttt @ theta['val'])
        o = h_q @ theta['proj'] @ proj_w + proj_b
        return o.reshape(Bx, SNx, DIM)

    def _L2_ffn_ref(x, router_w, w_gate, w_up, w_down):
        import jax, jax.numpy as jnp
        import numpy as np
        from jax import lax
        DIM = 256
        HID = 512
        E = 8
        K = 2
        B, T = (2, 128)
        Bb, Tt, D = x.shape
        N = Bb * Tt
        xf = x.reshape(N, D)
        logits = xf @ router_w.T
        routing = jax.nn.softmax(logits, axis=-1)
        top_w, top_i = lax.top_k(routing, K)
        top_w = top_w / jnp.sum(top_w, axis=-1, keepdims=True)
        combine = jnp.zeros((N, E), dtype=x.dtype)
        combine = combine.at[jnp.arange(N)[:, None], top_i].add(top_w)
        g = jnp.einsum('nd,ehd->neh', xf, w_gate)
        u = jnp.einsum('nd,ehd->neh', xf, w_up)
        h = jax.nn.silu(g) * u
        y = jnp.einsum('neh,edh->ned', h, w_down)
        out = jnp.einsum('ned,ne->nd', y, combine)
        return out.reshape(Bb, Tt, D)

    def _L3_xattn_ref(x, y, Wq, bq, Wk, bk, Wv, bv, W1, b1, W2, b2):
        import jax, jax.numpy as jnp
        import numpy as np
        IMAGE_DIM = 256
        TEXT_DIM = 192
        NUM_HEADS = 16
        HEAD_DIM = IMAGE_DIM // NUM_HEADS
        B, N, _ = x.shape
        M = y.shape[1]
        q = (x @ Wq + bq).reshape(B, N, NUM_HEADS, HEAD_DIM)
        k = (y @ Wk + bk).reshape(B, M, NUM_HEADS, HEAD_DIM)
        v = (y @ Wv + bv).reshape(B, M, NUM_HEADS, HEAD_DIM)
        scale = 1.0 / np.sqrt(HEAD_DIM)
        scores = jnp.einsum('bnhd,bmhd->bhnm', q, k) * scale
        attn = jax.nn.softmax(scores, axis=-1)
        out = jnp.einsum('bhnm,bmhd->bnhd', attn, v).reshape(B, N, IMAGE_DIM)
        h = jax.nn.relu(out @ W1 + b1)
        return h @ W2 + b2

    def _L3_attn_ref(x, Wz, bz, Wh, bh):
        import jax, jax.numpy as jnp
        import numpy as np

        def _parallel_scan_affine(log_a, b):
            T = log_a.shape[1]
            la, bv = (log_a, b)
            stride = 1
            while stride < T:
                la_prev = jnp.roll(la, stride, axis=1).at[:, :stride, :].set(0.0)
                bv_prev = jnp.roll(bv, stride, axis=1).at[:, :stride, :].set(0.0)
                bv = jnp.exp(la) * bv_prev + bv
                la = la + la_prev
                stride *= 2
            return bv
        z = jax.nn.sigmoid(jnp.einsum('btd,ed->bte', x, Wz) + bz)
        h_tilde = jnp.einsum('btd,ed->bte', x, Wh) + bh
        log_a = jnp.log(1.0 - z + 1e-08)
        b = z * h_tilde
        h_out = _parallel_scan_affine(log_a, b)
        return h_out

    def _L3_ffn_ref(x, Wg, bg, W0, b0, W1, b1, W2, b2):
        import jax, jax.numpy as jnp
        import numpy as np
        NUM_EXPERTS = 8
        TOP_K = 2
        D_MODEL = 256
        D_HID = 1024
        BATCH, SEQ = (2, 512)
        n, s, d = x.shape
        gate_logits = x @ Wg + bg
        top_vals, top_idx = jax.lax.top_k(gate_logits, TOP_K)
        w = jax.nn.softmax(top_vals, axis=-1)
        combine = jnp.sum(jax.nn.one_hot(top_idx, NUM_EXPERTS, dtype=x.dtype) * w[..., None], axis=-2)
        xf = x.reshape(n * s, d)
        h = jnp.einsum('td,edh->eth', xf, W0) + b0[:, None, :]
        g = jax.nn.silu(jnp.einsum('td,edh->eth', xf, W1) + b1[:, None, :])
        y = jnp.einsum('eth,ehd->etd', h * g, W2) + b2[:, None, :]
        out = jnp.einsum('te,etd->td', combine.reshape(n * s, NUM_EXPERTS), y)
        return out.reshape(n, s, d)
    x = x + _L0_xattn_ref(ctx_768, _layernorm(x, axis=-1), mask_BxS2_bk0, L0_xattn_ln_x_g, L0_xattn_ln_x_b, L0_xattn_ln_l_g, L0_xattn_ln_l_b, L0_xattn_qn_g, L0_xattn_kn_g, L0_xattn_Wq, L0_xattn_Wkv, L0_xattn_Wlkv, L0_xattn_Wo, L0_xattn_bo)
    x = x + _L0_attn_ref(_layernorm(x, axis=-1), L0_attn_Wq, L0_attn_Wkv, L0_attn_Wo, L0_attn_norm_w, L0_attn_norm_b, L0_attn_out_norm_w, L0_attn_out_norm_b)
    x = x + _L0_ffn_ref(_layernorm(x, axis=-1), L0_ffn_router_w, L0_ffn_w1, L0_ffn_w2)
    x = x + _L1_xattn_ref(_layernorm(x, axis=-1), ctx_768, ctx_768, L1_xattn_Wq, L1_xattn_bq, L1_xattn_Wk, L1_xattn_bk, L1_xattn_Wv, L1_xattn_bv, L1_xattn_Wo, L1_xattn_bo)
    x = x + _L1_attn_ref(_layernorm(x, axis=-1), L1_attn_W, L1_attn_b)
    x = x + _L1_ffn_ref(_layernorm(x, axis=-1), L1_ffn_gate_w, L1_ffn_w1, L1_ffn_b1, L1_ffn_w2, L1_ffn_b2)
    x = x + _L2_xattn_ref(_layernorm(x, axis=-1), ctx_768, L2_xattn_w_q, L2_xattn_w_k, L2_xattn_w_v, L2_xattn_w_o, L2_xattn_b_o)
    x = x + _L2_attn_ref(_layernorm(x, axis=-1), L2_attn_qkv_w, L2_attn_qkv_b, L2_attn_qn_scale, L2_attn_qn_bias, L2_attn_kn_scale, L2_attn_kn_bias, L2_attn_ttt_gate, L2_attn_ttt_val, L2_attn_ttt_proj, L2_attn_proj_w, L2_attn_proj_b)
    x = x + _L2_ffn_ref(_layernorm(x, axis=-1), L2_ffn_router_w, L2_ffn_w_gate, L2_ffn_w_up, L2_ffn_w_down)
    x = x + _L3_xattn_ref(_layernorm(x, axis=-1), ctx_768, L3_xattn_Wq, L3_xattn_bq, L3_xattn_Wk, L3_xattn_bk, L3_xattn_Wv, L3_xattn_bv, L3_xattn_W1, L3_xattn_b1, L3_xattn_W2, L3_xattn_b2)
    x = x + _L3_attn_ref(_layernorm(x, axis=-1), L3_attn_Wz, L3_attn_bz, L3_attn_Wh, L3_attn_bh)
    x = x + _L3_ffn_ref(_layernorm(x, axis=-1), L3_ffn_Wg, L3_ffn_bg, L3_ffn_W0, L3_ffn_b0, L3_ffn_W1, L3_ffn_b1, L3_ffn_W2, L3_ffn_b2)
    return x

_drawn_inputs = setup_inputs


def setup_inputs(seed=0):
    import zlib

    import numpy as np

    out = dict(_drawn_inputs(seed))
    spreads = {'L0_xattn_ln_x_g': (1.0, 0.2),
     'L0_xattn_ln_x_b': (0.0, 0.1),
     'L0_xattn_ln_l_g': (1.0, 0.2),
     'L0_xattn_ln_l_b': (0.0, 0.1),
     'L0_xattn_qn_g': (1.0, 0.2),
     'L0_xattn_kn_g': (1.0, 0.2),
     'L0_xattn_bo': (0.0, 0.1),
     'L0_attn_norm_w': (1.0, 0.2),
     'L0_attn_norm_b': (0.0, 0.1),
     'L0_attn_out_norm_w': (1.0, 0.2),
     'L0_attn_out_norm_b': (0.0, 0.1),
     'L1_xattn_bq': (0.0, 0.1),
     'L1_xattn_bk': (0.0, 0.8),
     'L1_xattn_bv': (0.0, 0.1),
     'L1_xattn_bo': (0.0, 0.1),
     'L1_ffn_b1': (0.0, 0.287),
     'L1_ffn_b2': (0.0, 0.1),
     'L2_attn_qkv_b': (0.0, 0.8),
     'L2_attn_qn_scale': (1.0, 0.6),
     'L2_attn_qn_bias': (0.0, 0.624),
     'L2_attn_kn_scale': (1.0, 0.6),
     'L2_attn_kn_bias': (0.0, 0.8),
     'L2_attn_proj_b': (0.0, 0.1),
     'L3_attn_bz': (0.0, 0.8),
     'L3_attn_bh': (0.0, 0.1),
     'L3_ffn_bg': (0.0, 0.383),
     'L3_ffn_b0': (0.0, 0.8),
     'L3_ffn_b1': (0.0, 0.8),
     'L3_ffn_b2': (0.0, 0.27)}
    factors = {'L1_attn_b': 6.328,
     'L2_xattn_b_o': 3.439,
     'L3_xattn_bq': 8.0,
     'L3_xattn_bk': 8.0,
     'L3_xattn_b1': 3.093,
     'L3_xattn_b2': 2.949,
     'L3_attn_Wz': 6.871,
     'L3_ffn_W0': 5.297,
     'L3_ffn_W1': 5.356,
     'L3_ffn_W2': 5.129}
    for name, (base, spread) in spreads.items():
        noise = np.random.default_rng([zlib.crc32(name.encode()), seed]).standard_normal(out[name].shape)
        drawn = base * np.exp(spread * noise) if base else spread * noise
        out[name] = jnp.asarray(drawn.astype(out[name].dtype))
    for name, factor in factors.items():
        out[name] = (out[name] * factor).astype(out[name].dtype)
    return out
```

```python
from contextlib import ExitStack

import concourse.bass as bass
from concourse import mybir

F32 = mybir.dt.float32
U32 = mybir.dt.uint32
U8 = mybir.dt.uint8
ALU = mybir.AluOpType
ACT = mybir.ActivationFunctionType
AX = mybir.AxisListType

P = 128
B, LQ = 2, 64
D = 256
C = D // P
KEYS = 1024
CD = 192
CB = CD - P
KT = B * KEYS // P
KTB = KEYS // P
E = 8
SLOTS = 4
FU = 512
FC = FU // P
UNIT = 3 * 1024
LN_EPS = 1e-5
NEG = -3.0e38
MASKED = -1.0e30

COLS = {}
for _name, _n in (("l0x_lg", 2), ("l0x_lb", 2), ("l0x_xg", 2), ("l0x_xb", 2), ("l0x_qg", 1), ("l0x_kg", 1),
                  ("l0a_w", 2), ("l0a_b", 2), ("l1x_bq", 2), ("l1x_bk", 2), ("l1x_bv", 2),
                  ("l3x_bq", 2), ("l3x_bk", 2), ("l3x_bv", 2), ("l3x_b1", 4), ("l3a_bz", 2), ("l3a_bh", 2),
                  ("l1f_b1", 64), ("l3f_b0", 64), ("l3f_b1", 64)):
    COLS[_name] = (sum(n for _, n in COLS.values()), _n)
NCOLS = sum(n for _, n in COLS.values())

ROWS = {}
for _name, _n in (("l0x_bo", D), ("l0a_ow", D), ("l0a_ob", D), ("l1x_bo", D), ("l1a_b", 32), ("l2x_bo", D),
                  ("l2a_pb", D), ("l3x_b2", D), ("l3f_bg", E)):
    ROWS[_name] = (sum(n for _, n in ROWS.values()), _n)
NROWS = sum(n for _, n in ROWS.values())

LATE = {"qkvb": (0, 3 * D), "qs": (768, 16), "qb": (784, 16), "ks": (800, 16), "kb": (816, 16)}
NLATE = 832

CONSTS = {"ident": (0, 128), "ones": (128, 128), "iota": (256, 8), "par": (264, 2), "bits": (266, 6),
          "nhalf": (272, 72), "phalf": (344, 32),
          "head": (376, 8)}
NCONST = 384

ROUTER = 4 * 16

def table(*items):
    out, at = {}, 0
    for name, n in items:
        out[name] = (at, n)
        at += n
    return out, at

L0X, L0X_N = table(("wq", 2 * D), ("wkv", 2 * 2 * D), ("wlkv", 2 * 2 * D), ("wo", 2 * D))
L0A, L0A_N = table(("wq", 2 * 512), ("wk", 2 * P), ("wv", 2 * 64), ("wo", 4 * D))
L1X, L1X_N = table(("wq", 2 * D), ("wk", 2 * D), ("wv", 2 * D), ("wo", 2 * D), ("l1a_w", 2 * 32))
L2X, L2X_N = table(("wq", 2 * 1024), ("wk", 8 * CD), ("wv", 2 * 1024), ("wo", 8 * D))
L2A, L2A_N = table(("qkv", 2 * 768), ("gate", 2 * 1024), ("val", 2 * 1024), ("proj", 8 * D),
                   ("projt", 2 * 1024), ("pw", 2 * D))
L3X, L3X_N = table(("wq", 2 * D), ("wk", 2 * D), ("wv", 2 * D), ("w1", 2 * 512), ("w2", 4 * D))
L3A, L3A_N = table(("wz", 2 * D), ("wh", 2 * D))

ATT_BASE = {"l0x": 0, "l1x": 4, "l2x": 20, "l3x": 36}
OPT_BASE = {"l0x": 0, "l2x": 4}
MOE_BASE = (0, 8, 24, 32)
MOE_UNITS = (8, 16, 8, 16)



class Views:
    pass


class Own:

    def __init__(self, eng, sem):
        self.eng, self.sem, self.n = eng, sem, 0

    def __call__(self, ins):
        ins.then_inc(self.sem, 1)
        self.n += 1

    def wait(self):
        self.eng.wait_ge(self.sem, self.n)


def perceiver_kernel(nc, x_in, ctx_in, ctxt_in, mask_in, cols_in, rows_in, late_in, e8_in, const_in, router_in,
                     l0x_in, l0a_in, l1x_in, l2x_in, l2a_in, l3x_in, l3a_in, m0_in, m1_in, m2_in, m3_in, out,
                     stages=12):
    with ExitStack() as ctx:
        def sb(name, shape, dt=F32):
            return ctx.enter_context(nc.sbuf_tensor(name, shape, dt))

        def sem(name):
            return ctx.enter_context(nc.semaphore(name))

        class S:
            (in_x, in_const, in_ctx, in_cols, in_l0x, in_mask) = (
                sem(n) for n in "in_x in_const in_ctx in_cols in_l0x in_mask".split())
            (in_rows, in_router, in_e8, in_l0a, moe_y, out_psum) = (
                sem(n) for n in "in_rows in_router in_e8 in_l0a moe_y out_psum".split())
            (in_l1x, in_ctxt, in_l2x, conv_y, in_l2a, in_late) = (
                sem(n) for n in "in_l1x in_ctxt in_l2x conv_y in_l2a in_late".split())
            (in_l3x, in_l3a, x_done, stored, ln_var, ln_rstd) = (
                sem(n) for n in "in_l3x in_l3a x_done stored ln_var ln_rstd".split())
            (cln_var, cln_rstd, ss_ready, ss_rstd, t_ss, t_norm) = (
                sem(n) for n in "cln_var cln_rstd ss_ready ss_rstd t_ss t_norm".split())
            (t_nrm, t_nrmp, att_max, att_pt, att_exp, att_o) = (
                sem(n) for n in "t_nrm t_nrmp att_max att_pt att_exp att_o".split())
            (att_pta, top_gap, top_exp, moe_up, moe_h, moe_g) = (
                sem(n) for n in "att_pta top_gap top_exp moe_up moe_h moe_g".split())
            (xn_psum, xn_act, kv_psum, kv_k, kv_v, kt_psum) = (
                sem(n) for n in "xn_psum xn_act kv_psum kv_k kv_v kt_psum".split())
            (kt_act, sa_max, sa_exp, c_psum, c_act, conv_max) = (
                sem(n) for n in "kt_act sa_max sa_exp c_psum c_act conv_max".split())
            (conv_exp, h1_psum, h1_act, t_a, t_sig, t_back) = (
                sem(n) for n in "conv_exp h1_psum h1_act t_a t_sig t_back".split())
            (t_backc, n_u, n_uc, n_w, n_wc, n_e) = (
                sem(n) for n in "t_backc n_u n_uc n_w n_wc n_e".split())
            (n_ec, m_h, m_hc, g_psum, g_z, t_qkv) = (
                sem(n) for n in "n_ec m_h m_hc g_psum g_z t_qkv".split())
            (t_qk, t_kqt, t_kqtc, t_gram, t_gramc, t_b) = (
                sem(n) for n in "t_qk t_kqt t_kqtc t_gram t_gramc t_b".split())
            (t_h, t_x, t_xc, t_z, t_zc, t_pred) = (
                sem(n) for n in "t_h t_x t_xc t_z t_zc t_pred".split())
            (t_e, t_et, t_etc, t_sh, t_dh, t_da) = (
                sem(n) for n in "t_e t_et t_etc t_sh t_dh t_da".split())
            (t_s, t_tr, t_trp, n_mc, n_ba, n_p) = (
                sem(n) for n in "t_s t_tr t_trp n_mc n_ba n_p".split())
            (n_pc, n_m, t_r, t_rc, t_o, t_oc) = (
                sem(n) for n in "n_pc n_m t_r t_rc t_o t_oc".split())
            (dve_own, xh_ready, xt_psum, xt_ready, att_on, att_ptd) = (
                sem(n) for n in "dve_own xh_ready xt_psum xt_ready att_on att_ptd".split())
            (opt_psum, opt_ready, att_s, router_psum, comb_ready, moe_acc) = (
                sem(n) for n in "opt_psum opt_ready att_s router_psum comb_ready moe_acc".split())
            (combt_psum, combt_ready, b2_psum, xn_ready, xn_dve, q_psum) = (
                sem(n) for n in "combt_psum combt_ready b2_psum xn_ready xn_dve q_psum".split())
            (kv_ss, q_norm, khat_ready, qt_psum, qbd_ready, kt_dve) = (
                sem(n) for n in "kv_ss q_norm khat_ready qt_psum qbd_ready kt_dve".split())
            (sa_qkv, sa_q, sa_s, sa_norm, sa_pt, sa_ptc) = (
                sem(n) for n in "sa_qkv sa_q sa_s sa_norm sa_pt sa_ptc".split())
            (sa_ot, sa_otc, c_dve, q16_psum, q16_ready, o16_psum) = (
                sem(n) for n in "sa_ot sa_otc c_dve q16_psum q16_ready o16_psum".split())
            (o16_ready, conv_s, conv_a, conv_at, conv_atc, qa_psum) = (
                sem(n) for n in "o16_ready conv_s conv_a conv_at conv_atc qa_psum".split())
            (qa_ready, h1_dve, ot_psum, ot_ready, g_scan, g_back) = (
                sem(n) for n in "qa_ready h1_dve ot_psum ot_ready g_scan g_back".split())

        slot_full = [ctx.enter_context(nc.semaphore(f"slot_full{i}")) for i in range(SLOTS)]

        ring = sb("ring", [P, SLOTS, UNIT])
        wa = sb("wa", [P, L2A_N])
        wb = sb("wb", [P, L2X_N])
        ctxn = sb("ctxn", [P, KT * CD])
        ctxt = sb("ctxt", [P, C * B * KEYS])
        scr = sb("scr", [P, 11520])
        cols = sb("cols", [P, NCOLS])
        rows = sb("rows", [P, NROWS])
        cst = sb("cst", [P, NCONST])
        router = sb("router", [P, ROUTER])
        e8 = sb("e8", [E, 2 * D])
        x = sb("x", [P, D])
        xh = sb("xh", [P, D])
        xt = sb("xt", [P, C, P])
        sm = sb("sm", [P, 256])
        ps01 = ctx.enter_context(nc.psum_tensor("ps01", [P, 1024], F32))
        ps23 = ctx.enter_context(nc.psum_tensor("ps23", [P, 1024], F32))
        ps45 = ctx.enter_context(nc.psum_tensor("ps45", [P, 1024], F32))
        ps6 = ctx.enter_context(nc.psum_tensor("ps6", [P, 512], F32))
        ps7 = ctx.enter_context(nc.psum_tensor("ps7", [P, 512], F32))
        halves = [ps01[:, 0:512], ps01[:, 512:1024], ps23[:, 0:512], ps23[:, 512:1024],
                  ps45[:, 0:512], ps45[:, 512:1024]]

        def carve(tensor, at, *shape):
            n = 1
            for s in shape:
                n *= s
            v = tensor[:, at:at + n]
            names = "abcd"[:len(shape)]
            if len(shape) > 1:
                v = v.rearrange(f"p ({' '.join(names)}) -> p {' '.join(names)}",
                                **{k: s for k, s in zip(names, shape)})
            return v

        def weight(tensor, tab, name, *shape):
            at, n = tab[name]
            return carve(tensor, at, *shape)

        def col(name, i=0):
            at, _ = COLS[name]
            return cols[:, at + i:at + i + 1]

        def row(name):
            at, n = ROWS[name]
            return rows[:, at:at + n]

        ident, ones = cst[:, 0:128], cst[:, 128:256]
        iota8, parity, bits = cst[:, 256:264], cst[:, 264:266], cst[:, 266:272]
        nhalf, phalf, head8 = cst[:, 272:344], cst[:, 344:376], cst[:, 376:384]
        stat, mv, ve, rstd = sm[:, 0:6], sm[:, 6:8], sm[:, 8:9], sm[:, 9:10]


        NK = KEYS + P
        a, w, q = L0X_N, L0A_N, Views()
        xnt = carve(ctxt, 0, C, B * KEYS)
        q.kt, q.v = carve(scr, 0, C, (KT + 1) * P), carve(scr, 4352, KT + 1, D)
        q.sc, q.qbd, q.sq = carve(scr, 8704, 2, NK), carve(scr, 11008, B, C, P), carve(wb, w + 2 * NK + 2048, 2, D)
        q.knat, q.pt = carve(wa, a, KT + 1, D), carve(wa, a + 4352, 2, NK)
        q.stats, q.mv = carve(wa, a + 6656, KT, 6), carve(wa, a + 6752, KT, 2)
        q.cve, q.crs = carve(wa, a + 6784, KT), carve(wa, a + 6800, KT)
        q.ss, q.rs = carve(wa, a + 6816, 72), carve(wa, a + 6888, 72)
        q.mask, q.mask8 = carve(wb, w, B, NK), wb[:, w + 2 * NK:w + 2 * NK + 512].bitcast(U8)
        q.xn = carve(wb, w + 2 * NK + 512, 8, CD)
        gain = sm[:, 40:41]
        att = Views()
        att.nmax = sm[:, 16:18]
        att.rsum = sm[:, 18:20]
        att.rinv = sm[:, 20:22]
        att.mx = sm[:, 22:24]

        late = ctxn

        r0 = Views()
        r0.qbd = carve(scr, 0, B, 4, P)
        r0.kt = carve(scr, 1024, P)
        r0.v = carve(scr, 1152, 64)
        r0.p = carve(scr, 1216, 4, B, LQ)
        r0.pt = carve(scr, 1728, 4, P)
        r0.ot = carve(scr, 2240, 4, P)
        r0.o = carve(scr, 2752, D)
        r0.mx = sm[:, 48:56]
        r0.sum = sm[:, 56:64]
        r0.rinv = sm[:, 64:72]
        n16 = Views()
        n16.kt = carve(scr, 0, C, B * KEYS)
        n16.v = carve(scr, 4096, KT, D)
        n16.p = carve(scr, 8192, 2, KEYS)
        n16.pt = carve(wa, 4224, 2, KEYS)
        n16.qt = carve(wa, 6272, C, P)
        n16.qbd = carve(wa, 2176, C, B, 8, LQ)
        n16.o = carve(wa, 6528, C, B, P)
        n16.ot = carve(wa, 7040, C, P)
        n16.tmp = carve(wa, 7296, C, P)
        n16.h = carve(wa, 7552, 4, P)
        n64 = Views()
        n64.qt = carve(scr, 0, 8, P)
        n64.opa = carve(scr, 0, B, 16, LQ)
        n64.qa = carve(scr, 2048, B, 16, LQ)
        n64.qb = carve(scr, 4096, B, 16, LQ)
        n64.opb = carve(scr, 4096, B, 16, LQ)
        n64.p = carve(scr, 6144, 2, KEYS)
        n64.pt = carve(scr, 8192, 2, KEYS)
        n64.o = carve(scr, 10240, 2, CD)
        n64.ot = carve(scr, 6144, 8, P)
        cv = Views()
        cv.w = carve(scr, 0, 32)
        cv.a = carve(scr, 64, 2, LQ)
        cv.b = carve(scr, 192, LQ)
        cv.nb = sm[:, 80:86]
        cv.full = carve(scr, 256, P)
        cv.at = carve(scr, 384, P)
        cv.mx = sm[:, 72:73]
        cv.sum = sm[:, 73:74]
        cv.rs = sm[:, 74:75]
        mo = Views()
        mo.g = carve(scr, 0, 2, FU)
        mo.h = carve(scr, 1024, 2, FU)
        mo.lg = sm[:, 96:104]
        mo.top = sm[:, 104:112]
        mo.idx = sm[:, 112:120].bitcast(U32)
        mo.idxf = sm[:, 120:128]
        mo.gap = sm[:, 128:130]
        mo.ex = sm[:, 130:132]
        mo.z = sm[:, 132:133]
        mo.rz = sm[:, 133:134]
        mo.wt = sm[:, 134:136]
        mo.c0 = sm[:, 136:144]
        mo.c1 = sm[:, 144:152]
        mo.comb = sm[:, 152:160]
        mo.combt = carve(scr, 2048, P)
        gr = Views()
        gr.e = carve(scr, 0, C, P)
        gr.z = carve(scr, 256, C, P)
        gr.a = carve(scr, 512, C, P)
        gr.b = carve(scr, 768, C, P)
        gr.h = carve(scr, 1024, C, P)
        gr.t = carve(scr, 1280, C, P)

        tt = Views()
        tt.qkv = carve(scr, 0, 3, D)
        tt.kqt = carve(scr, 768, 2, C, P)
        tt.gram = carve(scr, 1280, 2, P)
        tt.s = carve(scr, 1536, 8, P)
        tt.g = carve(scr, 2560, 8, P)
        tt.tb = carve(scr, 3584, 8, P)
        tt.w = carve(scr, 4608, 8, P)
        tt.h = carve(scr, 5632, 2, 8, P)
        tt.en = carve(scr, 7680, 2, D)
        tt.et = carve(scr, 8192, 2, C, P)
        tt.m = [[carve(scr, 8704 + (s * 3 + c) * 2 * P, 2, P) for c in range(3)] for s in range(2)]
        tt.sh = carve(scr, 10240, 2, P)
        tt.sgv = carve(scr, 10496, 2, P)
        tt.tmp = carve(scr, 10752, 6, P)
        tt.hn = carve(wb, L3X_N, 2, 8, P)
        tt.dan = carve(wb, L3X_N + 2048, 2, 8, P)
        tt.dbn = [carve(wa, 0, 8, P), carve(ctxn, 0, 8, P)]
        tt.u = [carve(ctxn, 1024 + c * 640, P) for c in range(3)]
        tt.wm = [carve(ctxn, 1152 + c * 640, P) for c in range(3)]
        tt.e = [carve(ctxn, 1280 + c * 640, 2, P) for c in range(3)]
        tt.pt = [carve(ctxn, 1536 + c * 640, P) for c in range(3)]
        tt.ai = xh[:, 0:P]
        tt.ss = sm[:, 160:192]
        tt.nr = sm[:, 192:224]
        tt.tr = sm[:, 224:227]
        tt.n2 = sm[:, 227:230]
        tt.n = sm[:, 230:233]
        tt.rn = sm[:, 233:236]
        NS_A, NS_B, NS_C, NS_ITERS, LR = 3.4445, -4.775, 2.0315, 5, 0.1
        block = ctx.enter_context(nc.Block())

        @block.sync
        def _(sp):
            sp.dma_start(x[:], x_in).then_inc(S.in_x, 16)
            sp.dma_start(cst[:], const_in).then_inc(S.in_const, 16)
            sp.dma_start(ctxn[:], ctx_in).then_inc(S.in_ctx, 16)
            sp.dma_start(cols[:], cols_in).then_inc(S.in_cols, 16)
            sp.dma_start(wa[:, 0:L0X_N], l0x_in).then_inc(S.in_l0x, 16)
            sp.dma_start(q.mask8, mask_in.partition_broadcast(P)).then_inc(S.in_mask, 16)
            sp.dma_start(rows[:], rows_in.partition_broadcast(P)).then_inc(S.in_rows, 16)
            sp.dma_start(router[:], router_in).then_inc(S.in_router, 16)
            sp.dma_start(e8[:], e8_in).then_inc(S.in_e8, 16)
            sp.dma_start(wb[:, 0:L0A_N], l0a_in).then_inc(S.in_l0a, 16)

            def units(m, source, first, n):
                width = source.shape[2]

                def lot(it):
                    for s in range(SLOTS):
                        if MOE_BASE[m] + first > 0:
                            sp.wait_ge(S.moe_y, MOE_BASE[m] - SLOTS + s + 1 + it * SLOTS)
                        k = it * SLOTS + s
                        unit = source[k] if isinstance(it, int) else \
                            source[bass.ds(k, 1)].rearrange("o p w -> (o p) w")
                        sp.dma_start(ring[:, s, 0:width], unit).then_inc(slot_full[s], 16)

                lots = range(first // SLOTS, (first + n) // SLOTS)
                if len(lots) == 1:
                    lot(lots[0])
                else:
                    with sp.Fori(lots[0], lots[-1] + 1) as it:
                        lot(it)

            units(0, m0_in, 0, 4)
            if stages > 1:
                sp.wait_ge(S.out_psum, 1)
                sp.dma_start(wa[:, 0:L1X_N], l1x_in).then_inc(S.in_l1x, 16)
                sp.dma_start(ctxt[:], ctxt_in).then_inc(S.in_ctxt, 16)
                sp.wait_ge(S.out_psum, 2)
                sp.dma_start(wb[:], l2x_in).then_inc(S.in_l2x, 16)
            if stages > 2:
                units(0, m0_in, 4, 4)
            if stages > 5:
                units(1, m1_in, 0, 4)
                sp.wait_ge(S.conv_y, 1)
                sp.dma_start(wa[:, 0:L2A_N], l2a_in).then_inc(S.in_l2a, 16)
                units(1, m1_in, 4, 12)
            if stages > 6:
                sp.wait_ge(S.out_psum, 4)
                sp.dma_start(late[:, 0:NLATE], late_in.partition_broadcast(P)).then_inc(S.in_late, 16)
                sp.dma_start(wb[:, 0:L3X_N], l3x_in).then_inc(S.in_l3x, 16)
            if stages > 8:
                units(2, m2_in, 0, 4)
                sp.wait_ge(S.out_psum, 5)
                sp.dma_start(wa[:, 0:L3A_N], l3a_in).then_inc(S.in_l3a, 16)
                units(2, m2_in, 4, 4)
            if stages > 11:
                units(3, m3_in, 0, 4)
                units(3, m3_in, 4, 12)
            if stages < 12:
                sp.wait_ge(S.in_e8, 16)
            sp.wait_ge(S.x_done, 1)
            sp.dma_start(out, x[:]).then_inc(S.stored, 16)
            sp.wait_ge(S.stored, 16)

        @block.gpsimd
        def _(pool):
            pool.wait_ge(S.in_const, 16)

            def norms(first, n):
                for i in range(first, first + n):
                    pool.wait_ge(S.ln_var, i + 1)
                    nc.gpsimd.tensor_tensor(rstd, ve, nhalf[:, 0:1], ALU.pow).then_inc(S.ln_rstd, 1)

            norms(0, 2)
            pool.wait_ge(S.cln_var, 1)
            nc.gpsimd.tensor_tensor(q.crs, q.cve, nhalf[:, 0:KT], ALU.pow).then_inc(S.cln_rstd, 1)
            pool.wait_ge(S.ss_ready, 1)
            nc.gpsimd.tensor_tensor(q.rs, q.ss, nhalf, ALU.pow).then_inc(S.ss_rstd, 1)
            last = 2 if stages == 1 else stages + 3
            norms(2, min(9, last) - 2)
            if stages == 7:
                norms(9, 1)
            if stages > 7:
                norms(9, 2)
                pool.wait_ge(S.t_ss, 1)
                nc.gpsimd.tensor_tensor(tt.nr, tt.ss, phalf, ALU.pow).then_inc(S.t_norm, 1)
                for s in range(2):
                    pool.wait_ge(S.t_nrm, s + 1)
                    nc.gpsimd.tensor_tensor(tt.n, tt.n2, phalf[:, 0:3], ALU.pow).then_inc(S.t_nrmp, 1)
                norms(11, last - 11)

        @block.scalar
        def _(act):
            def attention(stage, n, sc_of, nmax_of, p_of, pt_of):
                base = ATT_BASE[stage]
                for t in range(n + 1):
                    if t < n:
                        act.wait_ge(S.att_max, base + t + 1)
                        if t >= 2:
                            act.wait_ge(S.att_pt, base + t - 1)
                        nc.scalar.activation(p_of(t), sc_of(t), ACT.Exp, bias=att.nmax[:, t % 2:t % 2 + 1],
                                             accum_out=att.rsum[:, t % 2:t % 2 + 1]).then_inc(S.att_exp, 1)
                    if t >= 1:
                        act.wait_ge(S.att_pt, base + t)
                        if t >= 3:
                            act.wait_ge(S.att_o, base + t - 2)
                        nc.scalar.copy(pt_of(t - 1)[:, 0:512], ps45[:, 0:512]).then_inc(S.att_pta, 1)

            def mixture(m):
                base, nu = MOE_BASE[m], MOE_UNITS[m]
                act.wait_ge(S.top_gap, m + 1)
                nc.scalar.activation(mo.ex, mo.gap, ACT.Exp, accum_out=mo.z).then_inc(S.top_exp, 1)
                func = ACT.Gelu if m < 2 else ACT.Silu
                bias = (None, "l1f_b1", None, "l3f_b1")[m]

                def lot(it):
                    for s in range(SLOTS):
                        first = isinstance(it, int) and it == 0
                        k, par = it * SLOTS + s, s % 2
                        act.wait_ge(S.moe_up, base + s + 1 + it * SLOTS)
                        if m < 2:
                            if not (first and s < 2):
                                act.wait_ge(S.moe_y, base + s - 1 + it * SLOTS)
                            dst, done = mo.h, S.moe_h
                        else:
                            if not (first and s < 2):
                                act.wait_ge(S.moe_h, base + s - 1 + it * SLOTS)
                            dst, done = mo.g, S.moe_g
                        up = halves[par]
                        if bias is None:
                            nc.scalar.activation(dst[:, par, :], up, func).then_inc(done, 1)
                        else:
                            for fc in range(FC):
                                c = COLS[bias][0] + fc + s * FC + it * (SLOTS * FC)
                                ins = nc.scalar.activation(dst[:, par, fc * P:(fc + 1) * P], up[:, fc * P:(fc + 1) * P],
                                                           func, bias=cols[:, bass.ds(c, 1)])
                            ins.then_inc(done, 1)

                lot(0)
                if nu // SLOTS == 2:
                    lot(1)
                else:
                    with act.Fori(1, nu // SLOTS) as it:
                        lot(it)

            act.wait_ge(S.in_cols, 16)
            for g in range(KT // 4):
                act.wait_ge(S.xn_psum, g + 1)
                nc.scalar.activation(xnt[0:CB, 1, g * 512:(g + 1) * 512], halves[1][0:CB, :], ACT.Identity,
                                     bias=col("l0x_xb", 1)[0:CB], scale=col("l0x_xg", 1)[0:CB]).then_inc(S.xn_act, 1)
            for j in range(KT + 1):
                act.wait_ge(S.kv_psum, j + 1)
                nc.scalar.copy(q.knat[:, j, :], halves[2 + j % 2][:, 0:D]).then_inc(S.kv_k, 1)
                nc.scalar.copy(q.v[:, j, :], halves[2 + j % 2][:, D:2 * D]).then_inc(S.kv_v, 1)
            for g in range(9):
                if g % 2:
                    n = 2
                    act.wait_ge(S.kt_psum, g + 1)
                    nc.scalar.copy(q.kt[:, :, g * 2 * P:(g * 2 + n) * P],
                                   halves[4 + g % 2].rearrange("p (c k) -> p c k", c=C)).then_inc(S.kt_act, 1)
            attention("l0x", 4, lambda t: q.sc[:, t % 2, :], None, lambda t: q.sc[:, t % 2, :],
                      lambda t: q.pt[:, t % 2, :])
            if stages > 1:
                act.wait_ge(S.sa_max, 1)
                nc.scalar.activation(r0.p, r0.p, ACT.Exp).then_inc(S.sa_exp, 1)
            if stages > 2:
                mixture(0)

            def context16(i, bk):
                for j in range(1, 16, 2):
                    act.wait_ge(S.c_psum, 16 * i + j + 1)
                    src = halves[j % 4]
                    if j < 8:
                        c, kb = j // 4, j % 4
                        nc.scalar.activation(n16.kt[:, c, kb * 512:(kb + 1) * 512], src, ACT.Identity,
                                             bias=col(bk, c)).then_inc(S.c_act, 1)
                    else:
                        jj = j - 8
                        nc.scalar.copy(n16.v[:, 2 * jj:2 * jj + 2, :], src.rearrange("p (a d) -> p a d", a=2))\
                            .then_inc(S.c_act, 1)

            def scores(t):
                return ps01[:] if t % 2 == 0 else ps23[:]

            if stages > 3:
                context16(0, "l1x_bk")
                attention("l1x", 16, scores, None, lambda t: n16.p[:, t % 2, :], lambda t: n16.pt[:, t % 2, :])
            if stages > 4:
                act.wait_ge(S.conv_max, 1)
                nc.scalar.activation(cv.w, cv.w, ACT.Exp, bias=cv.mx, accum_out=cv.sum).then_inc(S.conv_exp, 1)
            if stages > 5:
                mixture(1)
            if stages > 6:
                for hh in range(2):
                    act.wait_ge(S.h1_psum, hh + 1)
                    for b in range(B):
                        src = ps45[0:CB, :].rearrange("p (a h b q) -> p a h b q", a=2, b=B, q=LQ)[:, :, :, b, :]
                        dst = n64.qb[0:CB, b, 8 * hh:8 * hh + 8, :].rearrange("p (h a) q -> p a h q", a=2)
                        nc.scalar.copy(dst, src).then_inc(S.h1_act, 1)
                attention("l2x", 16, scores, None, lambda t: n64.p[:, t % 2, :], lambda t: n64.pt[:, t % 2, :])
            if stages > 7:
                for s in range(2):
                    act.wait_ge(S.t_a, s + 1)
                    nc.scalar.activation(tt.s, ps01[:].rearrange("p (f k) -> p f k", f=8), ACT.Sigmoid)\
                        .then_inc(S.t_sig, 1)
                    act.wait_ge(S.t_back, 3 * s + 1)
                    nc.scalar.copy(tt.hn[:, s], ps45[:].rearrange("p (f k) -> p f k", f=8)).then_inc(S.t_backc, 1)
                    act.wait_ge(S.t_back, 3 * s + 2)
                    nc.scalar.copy(tt.dan[:, s], ps23[:].rearrange("p (f k) -> p f k", f=8)).then_inc(S.t_backc, 1)
                    act.wait_ge(S.t_back, 3 * s + 3)
                    nc.scalar.copy(tt.dbn[s], ps45[:].rearrange("p (f k) -> p f k", f=8)).then_inc(S.t_backc, 1)
                    with act.Fori(0, NS_ITERS) as it:
                        n0 = 3 * NS_ITERS * s + 1
                        for c in range(3):
                            act.wait_ge(S.n_u, n0 + c + it * 3)
                            nc.scalar.copy(tt.u[c], halves[c][:, 0:P]).then_inc(S.n_uc, 1)
                        for c in range(3):
                            act.wait_ge(S.n_w, n0 + c + it * 3)
                            nc.scalar.copy(tt.wm[c], halves[c][:, P:2 * P]).then_inc(S.n_wc, 1)
                        for c in range(3):
                            act.wait_ge(S.n_e, n0 + c + it * 3)
                            nc.scalar.copy(tt.e[c], halves[c][:, 2 * P:4 * P].rearrange("p (a k) -> p a k", a=2))\
                                .then_inc(S.n_ec, 1)
                act.wait_ge(S.t_a, 3)
                nc.scalar.activation(tt.s, ps01[:].rearrange("p (f k) -> p f k", f=8), ACT.Sigmoid).then_inc(S.t_sig, 1)
            if stages > 8:
                mixture(2)
            if stages > 9:
                context16(1, "l3x_bk")
                attention("l3x", 16, scores, None, lambda t: n16.p[:, t % 2, :], lambda t: n16.pt[:, t % 2, :])
                for f in range(4):
                    act.wait_ge(S.m_h, 1)
                    ins = nc.scalar.activation(n16.h[:, f, :], halves[0][:, f * P:(f + 1) * P], ACT.Relu,
                                               bias=col("l3x_b1", f))
                ins.then_inc(S.m_hc, 1)
            if stages > 10:
                for c in range(C):
                    act.wait_ge(S.g_psum, 1)
                    ins = nc.scalar.activation(gr.z[:, c, :], ps01[:, c * P:(c + 1) * P], ACT.Sigmoid,
                                               bias=col("l3a_bz", c))
                ins.then_inc(S.g_z, 1)
            if stages > 11:
                mixture(3)

        def ttt(dve, own, bc):
            eight = lambda t: t.rearrange("p (f k) -> p f k", f=8)
            dve.wait_ge(S.t_qkv, 1)
            dve.wait_ge(S.in_late, 16)
            lt = lambda name: late[:, LATE[name][0]:LATE[name][0] + LATE[name][1]]
            flat = tt.qkv.rearrange("p a d -> p (a d)")
            own(nc.vector.tensor_tensor(flat, ps01[:, 0:3 * D], lt("qkvb"), ALU.add))
            own.wait()
            qk, sq = flat[:, 0:2 * D], tt.w.rearrange("p f k -> p (f k)")[:, 0:2 * D]
            own(nc.vector.tensor_tensor(sq, qk, qk, ALU.mult))
            own.wait()
            nc.vector.tensor_reduce(tt.ss, sq.rearrange("p (h d) -> p h d", d=16), AX.X, ALU.add).then_inc(S.t_ss, 1)
            dve.wait_ge(S.t_norm, 1)
            own(nc.vector.tensor_scalar(tt.nr, tt.nr, 1e-6, None, ALU.add))
            own.wait()
            own(nc.vector.reciprocal(tt.nr, tt.nr))
            own.wait()
            qk3 = qk.rearrange("p (h d) -> p h d", d=16)
            own(nc.vector.tensor_tensor(qk3, qk3, bc(tt.nr, 16), ALU.mult))
            own.wait()
            for i, (g, b) in enumerate((("qs", "qb"), ("ks", "kb"))):
                half = tt.qkv[:, i, :].rearrange("p (h d) -> p h d", d=16)
                own(nc.vector.tensor_tensor(half, half, lt(g).unsqueeze(1).broadcast_to([P, 16, 16]), ALU.mult))
                own.wait()
                nc.vector.tensor_tensor(half, half, lt(b).unsqueeze(1).broadcast_to([P, 16, 16]), ALU.add)\
                    .then_inc(S.t_qk, 1)
            dve.wait_ge(S.t_kqt, 1)
            nc.vector.tensor_copy(tt.kqt, ps6[:, 0:512].rearrange("p (a c k) -> p a c k", a=2, c=C)).then_inc(S.t_kqtc, 1)
            dve.wait_ge(S.t_gram, 1)
            nc.vector.tensor_copy(tt.gram, ps7[:, 0:2 * P].rearrange("p (a k) -> p a k", a=2)).then_inc(S.t_gramc, 1)
            own(nc.vector.tensor_scalar(tt.ai, ident, NS_A, None, ALU.mult))
            a8, b8, w8 = eight(ps01[:]), eight(ps23[:]), tt.w
            for s in range(2):
                dve.wait_ge(S.t_sig, s + 1)
                own(nc.vector.tensor_tensor(tt.g, tt.s, a8, ALU.mult))
                own.wait()
                dve.wait_ge(S.t_b, s + 1)
                nc.vector.tensor_tensor(tt.h[:, s], tt.g, b8, ALU.mult).then_inc(S.t_h, 1)
                own(nc.vector.scalar_tensor_tensor(w8, tt.g, 1.0, tt.s, ALU.subtract, ALU.mult))
                own.wait()
                own(nc.vector.tensor_tensor(tt.tb, tt.g, w8, ALU.subtract))
                own.wait()
                own(nc.vector.tensor_tensor(tt.tb, tt.tb, b8, ALU.mult))
                if s == 1:
                    dve.wait_ge(S.t_x, 1)
                    nc.vector.tensor_copy(tt.tmp[:, 2], ps7[:, 0:P]).then_inc(S.t_xc, 1)
                    dve.wait_ge(S.t_z, 1)
                    nc.vector.tensor_scalar(tt.tmp[:, 3], ps7[:, P:2 * P], -LR, None, ALU.mult).then_inc(S.t_zc, 1)
                dve.wait_ge(S.t_pred, s + 1)
                own(nc.vector.tensor_tensor(tt.en[:, s], ps6[:, 0:D], tt.qkv[:, 2, :], ALU.subtract))
                own.wait()
                nc.vector.tensor_scalar(tt.en[:, s], tt.en[:, s], 2.0 / (P * D), None, ALU.mult).then_inc(S.t_e, 1)
                dve.wait_ge(S.t_et, s + 1)
                nc.vector.tensor_copy(tt.et[:, s], ps6[:, D:2 * D].rearrange("p (c k) -> p c k", c=C)).then_inc(S.t_etc, 1)
                if s == 1:
                    dve.wait_ge(S.t_x, 2)
                    nc.vector.tensor_copy(tt.tmp[:, 4], ps7[:, 0:P]).then_inc(S.t_xc, 1)
                    dve.wait_ge(S.t_z, 2)
                    nc.vector.tensor_scalar(tt.tmp[:, 5], ps7[:, P:2 * P], -LR, None, ALU.mult).then_inc(S.t_zc, 1)
                dve.wait_ge(S.t_sh, s + 1)
                own(nc.vector.tensor_copy(tt.sh, ps7[:, 2 * P:4 * P].rearrange("p (a k) -> p a k", a=2)))
                dve.wait_ge(S.t_dh, s + 1)
                own.wait()
                own(nc.vector.tensor_tensor(tt.tb, tt.tb, a8, ALU.mult))
                nc.vector.tensor_tensor(tt.w, tt.g, a8, ALU.mult).then_inc(S.t_da, 1)
                dve.wait_ge(S.t_s, s + 1)
                own(nc.vector.tensor_copy(tt.sgv, ps6[:, 0:2 * P].rearrange("p (a k) -> p a k", a=2)))
                own.wait()
                for c, (sc, cc) in enumerate(((tt.sgv[:, 0], tt.gram[:, 0]), (tt.sgv[:, 1], tt.gram[:, 0]),
                                              (tt.sh[:, 0], tt.sh[:, 1]))):
                    ins = nc.vector.tensor_tensor_reduce(tt.tmp[:, c], sc, cc, 1.0, 0.0, ALU.mult, ALU.add,
                                                         tt.tr[:, c:c + 1])
                ins.then_inc(S.t_tr, 1)
                dve.wait_ge(S.t_trp, s + 1)
                nc.vector.tensor_copy(tt.n2, ps7[:, 0:3]).then_inc(S.t_nrm, 1)
                dve.wait_ge(S.t_nrmp, s + 1)
                own(nc.vector.tensor_scalar(tt.n, tt.n, 1e-7, None, ALU.add))
                own.wait()
                own(nc.vector.reciprocal(tt.rn, tt.n))
                own.wait()
                for c in range(3):
                    nc.vector.tensor_scalar(tt.m[s][c], ident.unsqueeze(1).broadcast_to([P, 2, P]), tt.rn[:, c:c + 1],
                                            None, ALU.mult).then_inc(S.n_mc, 1)
                with dve.Fori(0, NS_ITERS) as it:
                    n0 = 3 * NS_ITERS * s + 1
                    for c in range(3):
                        dve.wait_ge(S.n_ec, n0 + c + it * 3)
                        nc.vector.scalar_tensor_tensor(tt.u[c], tt.e[c][:, 1], NS_B, tt.ai, ALU.mult, ALU.add)\
                            .then_inc(S.n_ba, 1)
                    for c in range(3):
                        dve.wait_ge(S.n_p, n0 + c + it * 3)
                        dve.wait_ge(S.n_ba, n0 + c + it * 3)
                        nc.vector.scalar_tensor_tensor(tt.pt[c], halves[3 + c][:, 0:P], NS_C, tt.u[c],
                                                       ALU.mult, ALU.add).then_inc(S.n_pc, 1)
                    for c in range(3):
                        dve.wait_ge(S.n_m, n0 + c + it * 3)
                        nc.vector.tensor_copy(tt.m[s][c], halves[3 + c][:, P:3 * P].rearrange("p (a k) -> p a k", a=2))\
                            .then_inc(S.n_mc, 1)
                if s == 0:
                    dve.wait_ge(S.t_r, 1)
                    nc.vector.tensor_scalar(tt.tmp[:, 0:2], ps6[:, 0:2 * P].rearrange("p (a k) -> p a k", a=2), -LR, None,
                                            ALU.mult).then_inc(S.t_rc, 1)
                else:
                    dve.wait_ge(S.t_r, 2)
                    nc.vector.tensor_scalar(tt.tmp[:, 0:4], ps6[:, 0:4 * P].rearrange("p (a k) -> p a k", a=4), -LR, None,
                                            ALU.mult).then_inc(S.t_rc, 1)
            dve.wait_ge(S.t_sig, 3)
            own(nc.vector.tensor_tensor(tt.g, tt.s, a8, ALU.mult))
            own.wait()
            dve.wait_ge(S.t_b, 3)
            nc.vector.tensor_tensor(tt.tb, tt.g, b8, ALU.mult).then_inc(S.t_h, 1)
            dve.wait_ge(S.t_x, 3)
            nc.vector.tensor_copy(tt.tmp[:, 4:6], ps7[:, 0:2 * P].rearrange("p (a k) -> p a k", a=2)).then_inc(S.t_xc, 1)
            dve.wait_ge(S.t_z, 3)
            nc.vector.tensor_scalar(tt.tmp[:, 0:2], ps7[:, 2 * P:4 * P].rearrange("p (a k) -> p a k", a=2), -LR, None,
                                    ALU.mult).then_inc(S.t_zc, 1)
            dve.wait_ge(S.t_o, 1)
            nc.vector.tensor_copy(tt.et[:, 0], ps45[:, 0:D].rearrange("p (c k) -> p c k", c=C)).then_inc(S.t_oc, 1)

        @block.vector
        def _(dve):
            own = Own(dve, S.dve_own)

            def bc(ap, n):
                return ap.unsqueeze(2).broadcast_to([P, ap.shape[1], n])

            def norm(n, src, dst):
                own(nc.vector.bn_stats(stat, src))
                own.wait()
                own(nc.vector.bn_aggr(mv, stat))
                own.wait()
                nc.vector.tensor_scalar(ve, mv[:, 1:2], LN_EPS, None, ALU.add).then_inc(S.ln_var, 1)
                dve.wait_ge(S.ln_rstd, n + 1)
                nc.vector.tensor_scalar(dst, src, mv[:, 0:1], rstd, ALU.subtract, ALU.mult).then_inc(S.xh_ready, 1)
                dve.wait_ge(S.xh_ready, n + 1)

            def tokens_t(stage, gain=None, bias=None):
                dve.wait_ge(S.xt_psum, stage + 1)
                if gain is None:
                    nc.vector.tensor_copy(xt[:], ps7[:, 0:D].rearrange("p (c k) -> p c k", c=C)).then_inc(S.xt_ready, 1)
                else:
                    own(nc.vector.tensor_scalar(xt[:, 0, :], ps7[:, 0:P], col(gain, 0), col(bias, 0), ALU.mult, ALU.add))
                    own.wait()
                    nc.vector.tensor_scalar(xt[:, 1, :], ps7[:, P:D], col(gain, 1), col(bias, 1), ALU.mult, ALU.add)\
                        .then_inc(S.xt_ready, 1)

            def residual(k, src, bias):
                if k == 1:
                    dve.wait_ge(S.in_rows, 16)
                dve.wait_ge(S.out_psum, k)
                own(nc.vector.tensor_tensor(x[:], x[:], src, ALU.add))
                own.wait()
                if bias is not None:
                    own(nc.vector.tensor_tensor(x[:], x[:], row(bias), ALU.add))
                    own.wait()

            def attention(stage, n, take_max, pt_of, o_of, width, post=None):
                base = ATT_BASE[stage]
                for t in range(n + 2 + (post is not None)):
                    if t < n:
                        take_max(t)
                    if 1 <= t <= n:
                        u = t - 1
                        dve.wait_ge(S.att_exp, base + t)
                        if u >= 2:
                            dve.wait_ge(S.att_on, base + u - 1)
                        own(nc.vector.reciprocal(att.rinv[:, u % 2:u % 2 + 1], att.rsum[:, u % 2:u % 2 + 1]))
                        own.wait()
                        dve.wait_ge(S.att_pt, base + t)
                        if t >= 3:
                            dve.wait_ge(S.att_o, base + t - 2)
                        if stage == "l0x":
                            nc.vector.tensor_copy(pt_of(u)[:, 1024:1152], halves[3][:, 0:P])
                        nc.vector.tensor_copy(pt_of(u)[:, 512:1024], ps45[:, 512:1024]).then_inc(S.att_ptd, 1)
                    if post is not None and 3 <= t:
                        u = t - 3
                        dve.wait_ge(S.opt_psum, OPT_BASE[stage] + u + 1)
                        post(u).then_inc(S.opt_ready, 1)
                    if 2 <= t < n + 2:
                        u = t - 2
                        dve.wait_ge(S.att_o, base + t - 1)
                        nc.vector.tensor_scalar(o_of(u), ps6[:, 0:width],
                                                att.rinv[:, u % 2:u % 2 + 1], None, ALU.mult).then_inc(S.att_on, 1)

            def plain_max(base, scores):
                def take(t):
                    dve.wait_ge(S.att_s, base + t + 1)
                    nc.vector.tensor_reduce(att.nmax[:, t % 2:t % 2 + 1], scores(t), AX.X, ALU.max, negate=True)\
                        .then_inc(S.att_max, 1)
                return take

            def mixture(m):
                base, nu = MOE_BASE[m], MOE_UNITS[m]
                dve.wait_ge(S.router_psum, m + 1)
                if m == 3:
                    own(nc.vector.tensor_tensor(mo.lg, ps7[:, 256:264], row("l3f_bg"), ALU.add))
                else:
                    own(nc.vector.tensor_copy(mo.lg, ps7[:, 256:264]))
                own.wait()
                own(nc.vector.max(mo.top, mo.lg))
                own.wait()
                own(nc.vector.max_index(mo.idx, mo.top, mo.lg))
                nc.vector.tensor_scalar(mo.gap, mo.top[:, 0:2], mo.top[:, 0:1], None, ALU.subtract).then_inc(S.top_gap, 1)
                own.wait()
                own(nc.vector.tensor_copy(mo.idxf, mo.idx))
                dve.wait_ge(S.top_exp, m + 1)
                own(nc.vector.reciprocal(mo.rz, mo.z))
                own.wait()
                own(nc.vector.tensor_scalar(mo.wt, mo.ex, mo.rz, None, ALU.mult))
                own.wait()
                own(nc.vector.tensor_scalar(mo.c0, iota8, mo.idxf[:, 0:1], mo.wt[:, 0:1], ALU.is_equal, ALU.mult))
                own(nc.vector.tensor_scalar(mo.c1, iota8, mo.idxf[:, 1:2], mo.wt[:, 1:2], ALU.is_equal, ALU.mult))
                own.wait()
                nc.vector.tensor_tensor(mo.comb, mo.c0, mo.c1, ALU.add).then_inc(S.comb_ready, 1)
                dve.wait_ge(S.comb_ready, m + 1)

                def add_unit(k_mod, prev_s, it, acc_value):
                    e = prev_s // (nu // E) + it * (SLOTS // (nu // E))
                    dve.wait_ge(S.moe_y, acc_value)
                    if not (isinstance(acc_value, int) and acc_value == 1):
                        dve.wait_ge(S.moe_acc, acc_value - 1)
                    nc.vector.scalar_tensor_tensor(x[:], halves[4 + k_mod][:, 0:D], mo.comb[:, bass.ds(e, 1)], x[:],
                                                   ALU.mult, ALU.add).then_inc(S.moe_acc, 1)

                def lot(it):
                    for s in range(SLOTS):
                        first = isinstance(it, int) and it == 0
                        par = s % 2
                        if m >= 2:
                            dve.wait_ge(S.moe_g, (0, 0, 0, 8)[m] + s + 1 + it * SLOTS)
                            if not (first and s < 2):
                                dve.wait_ge(S.moe_y, base + s - 1 + it * SLOTS)
                            up = halves[2 + par]
                            if m == 2:
                                nc.vector.tensor_tensor(mo.h[:, par, :], mo.g[:, par, :], up, ALU.mult)\
                                    .then_inc(S.moe_h, 1)
                            else:
                                for fc in range(FC):
                                    c = COLS["l3f_b0"][0] + fc + s * FC + it * (SLOTS * FC)
                                    f = slice(fc * P, (fc + 1) * P)
                                    ins = nc.vector.scalar_tensor_tensor(
                                        mo.h[:, par, f], up[:, f], cols[:, bass.ds(c, 1)], mo.g[:, par, f],
                                        ALU.add, ALU.mult)
                                ins.then_inc(S.moe_h, 1)
                        if not (first and s == 0):
                            prev = (s - 1) % SLOTS
                            add_unit(1 - par, prev, it if s else it - 1, base + s + it * SLOTS)

                lot(0)
                if m in (1, 3):
                    dve.wait_ge(S.combt_psum, m // 2 + 1)
                    nc.vector.tensor_copy(mo.combt[0:E, :], ps7[0:E, 264:264 + P]).then_inc(S.combt_ready, 1)
                    dve.wait_ge(S.b2_psum, m // 2 + 1)
                    dve.wait_ge(S.moe_acc, base + SLOTS - 1)
                    own(nc.vector.tensor_tensor(x[:], x[:], ps7[:, 0:D], ALU.add))
                    own.wait()
                if nu // SLOTS == 2:
                    lot(1)
                else:
                    with dve.Fori(1, nu // SLOTS) as it:
                        lot(it)
                add_unit(1, SLOTS - 1, nu // SLOTS - 1, base + nu)
                dve.wait_ge(S.moe_acc, base + nu)

            dve.wait_ge(S.in_x, 16)
            norm(0, x[:], xh[:])
            norm(1, xh[:], xh[:])
            dve.wait_ge(S.in_cols, 16)
            tokens_t(0, "l0x_lg", "l0x_lb")
            own(nc.vector.tensor_tensor(gain, col("l0x_qg"), col("l0x_kg"), ALU.mult))
            own(nc.vector.memset(q.qbd, 0.0))
            dve.wait_ge(S.in_ctx, 16)
            for j in range(KT):
                own(nc.vector.bn_stats(q.stats[:, j, :], ctxn[:, j * CD:(j + 1) * CD]))
            own.wait()
            for j in range(KT):
                own(nc.vector.bn_aggr(q.mv[:, j, :], q.stats[:, j, :]))
            own.wait()
            nc.vector.tensor_scalar(q.cve, q.mv[:, :, 1], LN_EPS, None, ALU.add).then_inc(S.cln_var, 1)
            dve.wait_ge(S.in_mask, 16)
            own(nc.vector.tensor_scalar(q.mask[:, :, 0:KEYS], q.mask8.rearrange("p (b k) -> p b k", b=B),
                                        -MASKED, MASKED, ALU.mult, ALU.add))
            own(nc.vector.memset(q.mask[:, :, KEYS:NK], MASKED))
            own.wait()
            for b in range(B):
                own(nc.vector.memset(q.mask[:, b, KEYS + b * LQ:KEYS + (b + 1) * LQ], 0.0))
            dve.wait_ge(S.cln_rstd, 1)
            for g in range(KT // 4):
                if g >= 2:
                    dve.wait_ge(S.xn_psum, g - 1)
                for i in range(4):
                    j = 4 * g + i
                    ins = nc.vector.tensor_scalar(q.xn[:, j % 8, :], ctxn[:, j * CD:(j + 1) * CD], q.mv[:, j, 0:1],
                                                  q.crs[:, j:j + 1], ALU.subtract, ALU.mult)
                    ins.then_inc(S.xn_ready, 1)
                if g >= 1:
                    dve.wait_ge(S.xn_psum, g)
                    nc.vector.tensor_scalar(xnt[:, 0, (g - 1) * 512:g * 512], halves[0], col("l0x_xg"), col("l0x_xb"),
                                            ALU.mult, ALU.add).then_inc(S.xn_dve, 1)
            dve.wait_ge(S.xn_psum, KT // 4)
            nc.vector.tensor_scalar(xnt[:, 0, KT * P - 512:KT * P], halves[0], col("l0x_xg"), col("l0x_xb"),
                                    ALU.mult, ALU.add).then_inc(S.xn_dve, 1)
            dve.wait_ge(S.q_psum, 1)
            own(nc.vector.tensor_copy(xh[:], ps6[:, 0:D]))
            own.wait()
            own(nc.vector.tensor_tensor(q.kt[:, 0, 0:D], xh[:], xh[:], ALU.mult))
            own.wait()
            own(nc.vector.tensor_reduce(q.ss[:, 68:72], q.kt[:, 0, 0:D].rearrange("p (h d) -> p h d", h=4), AX.X, ALU.add))
            for j in range(KT + 1):
                dve.wait_ge(S.kv_k, j + 1)
                if j >= 2:
                    dve.wait_ge(S.kv_ss, j - 1)
                own(nc.vector.tensor_tensor(q.sq[:, j % 2, :], q.knat[:, j, :], q.knat[:, j, :], ALU.mult))
                own.wait()
                nc.vector.tensor_reduce(q.ss[:, 4 * j:4 * j + 4], q.sq[:, j % 2, :].rearrange("p (h d) -> p h d", h=4),
                                        AX.X, ALU.add).then_inc(S.kv_ss, 1)
            own.wait()
            dve.wait_ge(S.kv_ss, KT + 1)
            nc.vector.tensor_scalar(q.ss, q.ss, 1.0 / 64, 1e-16, ALU.mult, ALU.max).then_inc(S.ss_ready, 1)
            dve.wait_ge(S.ss_rstd, 1)
            nc.vector.tensor_tensor(xh[:].rearrange("p (h d) -> p h d", h=4), xh[:].rearrange("p (h d) -> p h d", h=4),
                                    bc(q.rs[:, 68:72], 64), ALU.mult).then_inc(S.q_norm, 1)
            for j in range(KT + 1):
                kn = q.knat[:, j, :].rearrange("p (h d) -> p h d", h=4)
                nc.vector.tensor_tensor(kn, kn, bc(q.rs[:, 4 * j:4 * j + 4], 64), ALU.mult).then_inc(S.khat_ready, 1)
                if j == 1:
                    dve.wait_ge(S.qt_psum, 1)
                    src = ps6[:, 256:512].rearrange("p (c b k) -> p b c k", c=C, b=B)
                    for i in range(2):
                        for b in range(B):
                            h = slice(64 * i, 64 * i + 64)
                            ins = nc.vector.tensor_scalar(q.qbd[h, b, :, 64 * i:64 * i + 64], src[h, b], gain[h],
                                                          64 ** -0.5, ALU.mult, ALU.mult)
                    ins.then_inc(S.qbd_ready, 1)
                if j % 2 == 1 and j >= 3 and (j // 2 - 1) % 2 == 0:
                    g = j // 2 - 1
                    dve.wait_ge(S.kt_psum, g + 1)
                    nc.vector.tensor_copy(q.kt[:, :, g * 2 * P:(g * 2 + 2) * P],
                                          halves[4 + g % 2].rearrange("p (c k) -> p c k", c=C)).then_inc(S.kt_dve, 1)
            dve.wait_ge(S.kt_psum, 9)
            nc.vector.tensor_copy(q.kt[:, :, 16 * P:17 * P],
                                  halves[4][:, 0:2 * P].rearrange("p (c k) -> p c k", c=C)).then_inc(S.kt_dve, 1)

            def masked_max(t):
                dve.wait_ge(S.att_s, t + 1)
                if t >= 2:
                    dve.wait_ge(S.att_pt, t - 1)
                if t >= 1:
                    dve.wait_ge(S.att_max, t)
                b = t // 2
                own(nc.vector.tensor_tensor_reduce(q.sc[:, t % 2, 0:KEYS], ps01[:], q.mask[:, b, 0:KEYS],
                                                   1.0, NEG, ALU.add, ALU.max, att.mx[:, 0:1]))
                own(nc.vector.tensor_tensor_reduce(q.sc[:, t % 2, KEYS:NK], halves[2][:, 0:P],
                                                   q.mask[:, b, KEYS:NK], 1.0, NEG, ALU.add, ALU.max, att.mx[:, 1:2]))
                own.wait()
                nc.vector.tensor_reduce(att.nmax[:, t % 2:t % 2 + 1], att.mx, AX.X, ALU.max, negate=True)\
                    .then_inc(S.att_max, 1)

            def heads_back(u):
                b, hp = u // 2, u % 2
                for j in range(2):
                    h = slice(64 * j, 64 * j + 64)
                    ins = nc.vector.tensor_copy(xt[h, hp, b * LQ:(b + 1) * LQ], ps7[h, 64 * j:64 * j + 64])
                return ins

            attention("l0x", 4, masked_max, lambda t: q.pt[:, t % 2, :],
                      lambda t: xh[:, (t % 2) * P:(t % 2) * P + P], P, heads_back)
            residual(1, ps6[:, 0:D], "l0x_bo")
            if stages > 1:
                norm(2, x[:], xh[:])
                norm(3, xh[:], xh[:])
                tokens_t(1, "l0a_w", "l0a_b")
                own(nc.vector.memset(r0.qbd, 0.0))
                dve.wait_ge(S.sa_qkv, 1)
                own.wait()
                own(nc.vector.tensor_copy(r0.kt, ps23[:, 0:P]))
                own(nc.vector.tensor_copy(r0.v, ps23[:, P:P + 64]))
                src = ps01[:, 0:512].rearrange("p (h b k) -> p h b k", h=4, b=B)
                for i in range(2):
                    for b in range(B):
                        h = slice(64 * i, 64 * i + 64)
                        ins = nc.vector.tensor_scalar(r0.qbd[h, b, :, 64 * i:64 * i + 64], src[h, :, b, :], 64 ** -0.5,
                                                      None, ALU.mult)
                ins.then_inc(S.sa_q, 1)
                dve.wait_ge(S.sa_s, 1)
                s8 = ps45[:, 0:512].rearrange("p (a k) -> p a k", a=8)
                p8 = r0.p.rearrange("p h b k -> p (h b) k")
                own(nc.vector.tensor_reduce(r0.mx, s8, AX.X, ALU.max))
                own.wait()
                nc.vector.tensor_tensor(p8, s8, bc(r0.mx, LQ), ALU.subtract).then_inc(S.sa_max, 1)
                dve.wait_ge(S.sa_exp, 1)
                own(nc.vector.tensor_reduce(r0.sum, p8, AX.X, ALU.add))
                own.wait()
                own(nc.vector.reciprocal(r0.rinv, r0.sum))
                own.wait()
                nc.vector.tensor_tensor(p8, p8, bc(r0.rinv, LQ), ALU.mult).then_inc(S.sa_norm, 1)
                dve.wait_ge(S.sa_pt, 1)
                nc.vector.tensor_copy(r0.pt, ps01[:, 0:512].rearrange("p (h k) -> p h k", h=4)).then_inc(S.sa_ptc, 1)
                dve.wait_ge(S.sa_ot, 1)
                for b in range(B):
                    ins = nc.vector.tensor_copy(r0.ot[:, :, b * LQ:(b + 1) * LQ],
                                                halves[2 + b][:, 0:D].rearrange("p (h k) -> p h k", h=4))
                ins.then_inc(S.sa_otc, 1)
                dve.wait_ge(S.out_psum, 2)
                own(nc.vector.tensor_copy(r0.o, ps6[:, 0:D]))
                own.wait()
                norm(4, r0.o, r0.o)
                own(nc.vector.tensor_tensor(r0.o, r0.o, row("l0a_ow"), ALU.mult))
                own.wait()
                own(nc.vector.tensor_tensor(r0.o, r0.o, row("l0a_ob"), ALU.add))
                own.wait()
                own(nc.vector.tensor_tensor(x[:], x[:], r0.o, ALU.add))
                own.wait()
            if stages > 2:
                norm(5, x[:], xh[:])
                tokens_t(2)
                mixture(0)

            def context16(i, bk):
                for j in range(0, 16, 2):
                    dve.wait_ge(S.c_psum, 16 * i + j + 1)
                    src = halves[j % 4]
                    if j < 8:
                        c, kb = j // 4, j % 4
                        nc.vector.tensor_scalar(n16.kt[:, c, kb * 512:(kb + 1) * 512], src, col(bk, c), None, ALU.add)\
                            .then_inc(S.c_dve, 1)
                    else:
                        jj = j - 8
                        nc.vector.tensor_copy(n16.v[:, 2 * jj:2 * jj + 2, :], src.rearrange("p (a d) -> p a d", a=2))\
                            .then_inc(S.c_dve, 1)

            def cross16(i, stage, bq, bk, bv):
                dve.wait_ge(S.q16_psum, i + 1)
                for c in range(C):
                    own(nc.vector.tensor_scalar(n16.qt[:, c, :], ps6[:, c * P:(c + 1) * P], col(bq, c), 0.25,
                                                ALU.add, ALU.mult))
                own.wait()
                for j in range(8):
                    ins = nc.vector.tensor_scalar(n16.qbd[:, :, :, j, :], n16.qt.rearrange("p c (b k) -> p c b k", b=B),
                                                  head8[:, j:j + 1], None, ALU.mult)
                ins.then_inc(S.q16_ready, 1)
                context16(i, bk)
                base = ATT_BASE[stage]

                def o_of(u):
                    cb, g = u // 4, u % 4
                    return n16.o[:, cb // 2, cb % 2, 32 * g:32 * g + 32]

                attention(stage, 16, plain_max(base, lambda t: (ps01, ps23)[t % 2][:]), lambda t: n16.pt[:, t % 2, :],
                          o_of, 32)
                dve.wait_ge(S.o16_psum, i + 1)
                src = ps6[:, 0:512].rearrange("p (c b j k) -> p c b j k", c=C, b=B, j=2)
                ot = n16.ot.rearrange("p c (b k) -> p c b k", b=B)
                tmp = n16.tmp.rearrange("p c (b k) -> p c b k", b=B)
                for c in range(C):
                    own(nc.vector.tensor_scalar(tmp[:, c], src[:, c, :, 0, :], parity[:, 0:1], col(bv, c),
                                                ALU.mult, ALU.add))
                own.wait()
                for c in range(C):
                    ins = nc.vector.scalar_tensor_tensor(ot[:, c], src[:, c, :, 1, :], parity[:, 1:2], tmp[:, c],
                                                         ALU.mult, ALU.add)
                ins.then_inc(S.o16_ready, 1)

            if stages > 3:
                norm(6, x[:], xh[:])
                tokens_t(3)
                cross16(0, "l1x", "l1x_bq", "l1x_bk", "l1x_bv")
                residual(3, ps6[:, 0:D], "l1x_bo")
            if stages > 4:
                norm(7, x[:], xh[:])
                tokens_t(4)
                own(nc.vector.memset(cv.a, 0.0))
                own(nc.vector.memset(cv.full, 0.0))
                own(nc.vector.tensor_scalar(cv.nb, bits, -1.0, 1.0, ALU.mult, ALU.add))
                dve.wait_ge(S.conv_s, 1)
                own(nc.vector.tensor_tensor(cv.w, ps6[:, 0:32], row("l1a_b"), ALU.add))
                own.wait()
                nc.vector.tensor_reduce(cv.mx, cv.w, AX.X, ALU.max, negate=True).then_inc(S.conv_max, 1)
                dve.wait_ge(S.conv_exp, 1)
                own(nc.vector.reciprocal(cv.rs, cv.sum))
                own.wait()
                own(nc.vector.tensor_scalar(cv.a[:, 0, 0:32], cv.w, cv.rs, None, ALU.mult))
                own.wait()
                for i in range(6):
                    src, dst, sh = cv.a[:, i % 2, :], cv.a[:, (i + 1) % 2, :], 1 << i
                    own(nc.vector.tensor_scalar(dst, src, cv.nb[:, i:i + 1], None, ALU.mult))
                    own.wait()
                    own(nc.vector.scalar_tensor_tensor(dst[:, sh:LQ], src[:, 0:LQ - sh], bits[:, i:i + 1], dst[:, sh:LQ],
                                                       ALU.mult, ALU.add))
                    own.wait()
                for b in range(B):
                    h = slice(b * LQ, (b + 1) * LQ)
                    ins = nc.vector.tensor_copy(cv.full[h, h], cv.a[h, 0, :])
                ins.then_inc(S.conv_a, 1)
                dve.wait_ge(S.conv_at, 1)
                nc.vector.tensor_copy(cv.at, ps6[:, 32:32 + P]).then_inc(S.conv_atc, 1)
                dve.wait_ge(S.conv_y, 1)
                own(nc.vector.tensor_tensor(x[:], x[:], ps6[:, 256:512], ALU.add))
                own.wait()
            if stages > 5:
                norm(8, x[:], xh[:])
                tokens_t(5)
                mixture(1)
            if stages > 6:
                norm(9, x[:], xh[:])
                tokens_t(6)
                dve.wait_ge(S.qa_psum, 1)
                nc.vector.tensor_scalar(n64.qt, ps01[:].rearrange("p (h k) -> p h k", h=8), 64 ** -0.5, None, ALU.mult)\
                    .then_inc(S.qa_ready, 1)
                for hh in range(2):
                    dve.wait_ge(S.h1_psum, hh + 1)
                    for b in range(B):
                        src = ps23[:].rearrange("p (a h b q) -> p a h b q", a=2, b=B, q=LQ)[:, :, :, b, :]
                        dst = n64.qa[:, b, 8 * hh:8 * hh + 8, :].rearrange("p (h a) q -> p a h q", a=2)
                        nc.vector.tensor_copy(dst, src).then_inc(S.h1_dve, 1)
                def context_back(u):
                    b, hp = u // 8, u % 8
                    nc.vector.tensor_copy(n64.opa[:, b, 2 * hp:2 * hp + 2, :],
                                          ps7[:, 0:P].rearrange("p (h q) -> p h q", h=2))
                    return nc.vector.tensor_copy(n64.opb[CB:P, b, 2 * hp:2 * hp + 2, :],
                                                 ps7[0:CB, P:2 * P].rearrange("p (h q) -> p h q", h=2))

                attention("l2x", 16, plain_max(20, lambda t: (ps01, ps23)[t % 2][:]), lambda t: n64.pt[:, t % 2, :],
                          lambda u: n64.o[:, u % 2, :], CD, context_back)
                dve.wait_ge(S.ot_psum, 1)
                nc.vector.tensor_copy(n64.ot, ps01[:].rearrange("p (h k) -> p h k", h=8)).then_inc(S.ot_ready, 1)
                residual(4, ps6[:, 0:D], "l2x_bo")
            if stages > 7:
                norm(10, x[:], xh[:])
                tokens_t(7)
                ttt(dve, own, bc)
                residual(5, ps6[:, 0:D], "l2a_pb")
            if stages > 8:
                norm(11, x[:], xh[:])
                tokens_t(8)
                mixture(2)
            if stages > 9:
                norm(12, x[:], xh[:])
                tokens_t(9)
                cross16(1, "l3x", "l3x_bq", "l3x_bk", "l3x_bv")
                residual(6, ps6[:, 0:D], "l3x_b2")
            if stages > 10:
                norm(13, x[:], xh[:])
                tokens_t(10)
                dve.wait_ge(S.g_psum, 1)
                for c in range(C):
                    own(nc.vector.tensor_scalar(gr.t[:, c, :], ps01[:, 512 + c * P:512 + (c + 1) * P], col("l3a_bh", c),
                                                None, ALU.add))
                dve.wait_ge(S.g_z, 1)
                own.wait()
                own(nc.vector.tensor_scalar(gr.a, gr.z, -1.0, 1.0, ALU.mult, ALU.add))
                own(nc.vector.tensor_tensor(gr.b, gr.z, gr.t, ALU.mult))
                own.wait()
                own(nc.vector.tensor_scalar(gr.a, gr.a, 1e-8, None, ALU.add))
                own.wait()
                for c in range(C):
                    for b in range(B):
                        k = slice(b * LQ, (b + 1) * LQ)
                        nc.vector.tensor_tensor_scan(gr.h[:, c, k], gr.a[:, c, k], gr.b[:, c, k], 0.0, ALU.mult, ALU.add)\
                            .then_inc(S.g_scan, 1)
                dve.wait_ge(S.g_back, 1)
                own(nc.vector.tensor_tensor(x[:], x[:], ps6[:, 0:D], ALU.add))
                own.wait()
            if stages > 11:
                norm(14, x[:], xh[:])
                tokens_t(11)
                mixture(3)
            nc.vector.tensor_copy(x[:], x[:]).then_inc(S.x_done, 1)

        def pe_ttt(pe):
            mm = nc.tensor.matmul
            W = lambda name, *shape: weight(wa, L2A, name, *shape)
            gate, val, proj, projt = W("gate", C, 1024), W("val", C, 1024), W("proj", 8, D), W("projt", C, 1024)
            pe.wait_ge(S.in_l2a, 16)
            w = W("qkv", C, 3 * D)
            for n0, n1 in ((0, 512), (512, 768)):
                for c in range(C):
                    ins = mm(ps01[:, n0:n1], xt[:, c, :], w[:, c, n0:n1], start=(c == 0), stop=(c == 1))
            ins.then_inc(S.t_qkv, 1)
            pe.wait_ge(S.t_qk, 2)
            for a in range(2):
                for c in range(C):
                    ins = nc.tensor.transpose(ps6[:, (2 * a + c) * P:(2 * a + c + 1) * P],
                                              tt.qkv[:, 1 - a, c * P:(c + 1) * P], ident)
            ins.then_inc(S.t_kqt, 1)
            pe.wait_ge(S.t_kqtc, 1)
            kt, qt = tt.kqt[:, 0], tt.kqt[:, 1]
            for a, r in ((0, kt), (1, qt)):
                for c in range(C):
                    ins = mm(ps7[:, a * P:(a + 1) * P], kt[:, c, :], r[:, c, :], start=(c == 0), stop=(c == 1))
            ins.then_inc(S.t_gram, 1)

            def through(bank, weights, rhs, updates):
                for f in range(8):
                    terms = [(weights[:, c, f * P:(f + 1) * P], rhs[:, c, :]) for c in range(C)]
                    terms += [(d[:, f, :], r) for d, r in updates]
                    for i, (l, r) in enumerate(terms):
                        ins = mm(bank[:, f * P:(f + 1) * P], l, r, start=(i == 0), stop=(i == len(terms) - 1))
                return ins

            def gram(dst, l, r):
                for f in range(l.shape[1]):
                    ins = mm(dst, l[:, f, :], r[:, f, :], start=(f == 0), stop=(f == l.shape[1] - 1))
                return ins

            def back(bank, src):
                for f in range(8):
                    ins = nc.tensor.transpose(bank[:, f * P:(f + 1) * P], src[:, f, :], ident)
                return ins

            for s in range(2):
                if s == 1:
                    pe.wait_ge(S.t_rc, 1)
                if s == 0:
                    pe.wait_ge(S.t_gramc, 1)
                ug = [(tt.dan[:, 0], tt.tmp[:, 0])] if s else []
                uv = [(tt.dbn[0], tt.tmp[:, 1])] if s else []
                through(ps01, gate, kt, ug).then_inc(S.t_a, 1)
                through(ps23, val, kt, uv).then_inc(S.t_b, 1)
                pe.wait_ge(S.t_h, s + 1)
                h = tt.h[:, s]
                if s == 1:
                    gram(ps7[:, 0:P], tt.h[:, 0], h).then_inc(S.t_x, 1)
                    pe.wait_ge(S.t_xc, 1)
                    mm(ps7[:, P:2 * P], tt.m[0][2][:, 1], tt.tmp[:, 2], start=True, stop=True).then_inc(S.t_z, 1)
                    pe.wait_ge(S.t_zc, 1)
                for f in range(8):
                    ins = mm(ps6[:, 0:D], h[:, f, :], proj[:, f, :], start=(f == 0), stop=(f == 7 and s == 0))
                if s == 1:
                    ins = mm(ps6[:, 0:D], tt.tmp[:, 3], tt.en[:, 0], start=False, stop=True)
                ins.then_inc(S.t_pred, 1)
                back(ps45, h).then_inc(S.t_back, 1)
                gram(ps7[:, 2 * P:3 * P], h, h)
                pe.wait_ge(S.t_e, s + 1)
                for c in range(C):
                    ins = nc.tensor.transpose(ps6[:, D + c * P:D + (c + 1) * P], tt.en[:, s, c * P:(c + 1) * P], ident)
                ins.then_inc(S.t_et, 1)
                pe.wait_ge(S.t_etc, s + 1)
                et = tt.et[:, s]
                if s == 1:
                    gram(ps7[:, 0:P], tt.et[:, 0], et).then_inc(S.t_x, 1)
                    pe.wait_ge(S.t_xc, 2)
                    mm(ps7[:, P:2 * P], tt.m[0][2][:, 0], tt.tmp[:, 4], start=True, stop=True).then_inc(S.t_z, 1)
                    pe.wait_ge(S.t_zc, 2)
                gram(ps7[:, 3 * P:4 * P], et, et).then_inc(S.t_sh, 1)
                through(ps01, projt, et, [(tt.hn[:, 0], tt.tmp[:, 5])] if s else []).then_inc(S.t_dh, 1)
                pe.wait_ge(S.t_da, s + 1)
                gram(ps6[:, 0:P], tt.tb, tt.tb)
                gram(ps6[:, P:2 * P], tt.w, tt.w).then_inc(S.t_s, 1)
                back(ps23, tt.tb).then_inc(S.t_back, 1)
                pe.wait_ge(S.t_backc, 3 * s + 1)
                back(ps45, tt.w).then_inc(S.t_back, 1)
                pe.wait_ge(S.t_tr, s + 1)
                mm(ps7[:, 0:3], ones, tt.tr, start=True, stop=True).then_inc(S.t_trp, 1)
                pe.wait_ge(S.t_backc, 3 * s + 3)
                c_of = (tt.gram[:, 0], tt.gram[:, 0], tt.sh[:, 1])
                s_of = (tt.sgv[:, 0], tt.sgv[:, 1], tt.sh[:, 0])
                with pe.Fori(0, NS_ITERS) as it:
                    n0, m0 = 3 * NS_ITERS * s + 1, 3 * (NS_ITERS + 1) * s + 1
                    for c in range(3):
                        pe.wait_ge(S.n_mc, m0 + c + it * 3)
                        mm(halves[c][:, 0:P], s_of[c], tt.m[s][c][:, 1], start=True, stop=True).then_inc(S.n_u, 1)
                    for c in range(3):
                        pe.wait_ge(S.n_uc, n0 + c + it * 3)
                        mm(halves[c][:, P:2 * P], tt.m[s][c][:, 1], tt.u[c], start=True, stop=True).then_inc(S.n_w, 1)
                    for c in range(3):
                        pe.wait_ge(S.n_wc, n0 + c + it * 3)
                        mm(halves[c][:, 2 * P:3 * P], tt.wm[c], c_of[c], start=True, stop=True)
                        mm(halves[c][:, 3 * P:4 * P], c_of[c], tt.wm[c], start=True, stop=True).then_inc(S.n_e, 1)
                    for c in range(3):
                        pe.wait_ge(S.n_ec, n0 + c + it * 3)
                        mm(halves[3 + c][:, 0:P], tt.e[c][:, 0], tt.e[c][:, 1], start=True, stop=True).then_inc(S.n_p, 1)
                    for c in range(3):
                        pe.wait_ge(S.n_pc, n0 + c + it * 3)
                        mm(halves[3 + c][:, P:2 * P], tt.pt[c], tt.m[s][c][:, 0], start=True, stop=True)
                        mm(halves[3 + c][:, 2 * P:3 * P], tt.m[s][c][:, 0], tt.pt[c], start=True, stop=True)\
                            .then_inc(S.n_m, 1)
                pe.wait_ge(S.n_mc, 3 * (NS_ITERS + 1) * (s + 1))
                if s == 0:
                    for c in range(2):
                        ins = mm(ps6[:, c * P:(c + 1) * P], tt.m[0][c][:, 0], tt.gram[:, 0], start=True, stop=True)
                else:
                    for i, (u, c) in enumerate(((0, 0), (0, 1), (1, 0), (1, 1))):
                        ins = mm(ps6[:, i * P:(i + 1) * P], tt.m[u][c][:, 0], tt.gram[:, 1], start=True, stop=True)
                ins.then_inc(S.t_r, 1)
            pe.wait_ge(S.t_rc, 2)
            through(ps01, gate, qt, [(tt.dan[:, 0], tt.tmp[:, 0]), (tt.dan[:, 1], tt.tmp[:, 2])]).then_inc(S.t_a, 1)
            through(ps23, val, qt, [(tt.dbn[0], tt.tmp[:, 1]), (tt.dbn[1], tt.tmp[:, 3])]).then_inc(S.t_b, 1)
            pe.wait_ge(S.t_h, 3)
            h = tt.tb
            for u in range(2):
                ins = gram(ps7[:, u * P:(u + 1) * P], tt.h[:, u], h)
            ins.then_inc(S.t_x, 1)
            pe.wait_ge(S.t_xc, 3)
            for u in range(2):
                ins = mm(ps7[:, (2 + u) * P:(3 + u) * P], tt.m[u][2][:, 1], tt.tmp[:, 4 + u], start=True, stop=True)
            ins.then_inc(S.t_z, 1)
            pe.wait_ge(S.t_zc, 3)
            for d in range(C):
                k = slice(d * P, (d + 1) * P)
                terms = [(proj[:, f, k], h[:, f, :]) for f in range(8)]
                terms += [(tt.en[:, u, k], tt.tmp[:, u]) for u in range(2)]
                for i, (l, r) in enumerate(terms):
                    ins = mm(ps45[:, k], l, r, start=(i == 0), stop=(i == len(terms) - 1))
            ins.then_inc(S.t_o, 1)
            pe.wait_ge(S.t_oc, 1)
            w = W("pw", C, D)
            for c in range(C):
                ins = mm(ps6[:, 0:D], tt.et[:, 0, c, :], w[:, c, :], start=(c == 0), stop=(c == 1))
            ins.then_inc(S.out_psum, 1)

        @block.tensor
        def _(pe):
            mm = nc.tensor.matmul

            def tokens_t(stage, norms_done):
                pe.wait_ge(S.xh_ready, norms_done)
                for c in range(C):
                    ins = nc.tensor.transpose(ps7[:, c * P:(c + 1) * P], xh[:, c * P:(c + 1) * P], ident)
                ins.then_inc(S.xt_psum, 1)
                pe.wait_ge(S.xt_ready, stage + 1)

            def attention(stage, n, scores, pt_of, v_of, width, tiles, post=None):
                base = ATT_BASE[stage]
                for t in range(n + 2 + (post is not None)):
                    if t < n:
                        if stage == "l0x":
                            if t >= 1:
                                pe.wait_ge(S.att_max, t)
                        elif t >= 2:
                            pe.wait_ge(S.att_exp, base + t - 1)
                        scores(t).then_inc(S.att_s, 1)
                    if 1 <= t <= n:
                        u = t - 1
                        pe.wait_ge(S.att_exp, base + t)
                        if u >= 1:
                            pe.wait_ge(S.att_pta, base + u)
                            pe.wait_ge(S.att_ptd, base + u)
                        src = q.sc[:, u % 2, :] if stage == "l0x" else \
                            (n64.p if stage == "l2x" else n16.p)[:, u % 2, :]
                        for k in range(tiles):
                            dst = ps45[:, k * P:(k + 1) * P] if k < 8 else halves[3][:, 0:P]
                            ins = nc.tensor.transpose(dst, src[:, k * P:(k + 1) * P], ident)
                        ins.then_inc(S.att_pt, 1)
                    if post is not None and t >= 3:
                        u = t - 3
                        pe.wait_ge(S.att_on, base + u + 1)
                        if u >= 1:
                            pe.wait_ge(S.opt_ready, OPT_BASE[stage] + u)
                        post(u).then_inc(S.opt_psum, 1)
                    if 2 <= t < n + 2:
                        u = t - 2
                        pe.wait_ge(S.att_pta, base + u + 1)
                        pe.wait_ge(S.att_ptd, base + u + 1)
                        if u >= 1:
                            pe.wait_ge(S.att_on, base + u)
                        for k in range(tiles):
                            ins = mm(ps6[:, 0:width], pt_of(u)[:, k * P:(k + 1) * P],
                                     v_of(u, k), start=(k == 0), stop=(k == tiles - 1))
                        ins.then_inc(S.att_o, 1)

            def mixture(m):
                base, nu = MOE_BASE[m], MOE_UNITS[m]
                if m == 0:
                    pe.wait_ge(S.in_router, 16)
                for c in range(C):
                    ins = mm(ps7[:, 256:264], xt[:, c, :], router[:, (m * C + c) * E:(m * C + c + 1) * E],
                             start=(c == 0), stop=(c == C - 1))
                ins.then_inc(S.router_psum, 1)
                gated = m >= 2
                down_at = (1 + gated) * C * FU

                def up(s, it, first):
                    par = s % 2
                    pe.wait_ge(slot_full[s], 16 * (base // SLOTS + 1) + it * 16)
                    if not (first and s < 2):
                        pe.wait_ge(S.moe_h, base + s - 1 + it * SLOTS)
                    w = ring[:, s, 0:down_at].rearrange("p (g c f) -> p g c f", g=1 + gated, c=C)
                    for g in range(1 + gated):
                        for fc in range(FC):
                            for c in range(C):
                                ins = mm(halves[2 * g + par][:, fc * P:(fc + 1) * P], w[:, g, c, fc * P:(fc + 1) * P],
                                         xt[:, c, :], start=(c == 0), stop=(c == C - 1))
                    ins.then_inc(S.moe_up, 1)

                def down(s, value):
                    par = s % 2
                    pe.wait_ge(S.moe_h, value)
                    if not (isinstance(value, int) and value - 2 <= 0):
                        pe.wait_ge(S.moe_acc, value - 2)
                    for fc in range(FC):
                        ins = mm(halves[4 + par][:, 0:D], mo.h[:, par, fc * P:(fc + 1) * P],
                                 ring[:, s, down_at + fc * D:down_at + (fc + 1) * D],
                                 start=(fc == 0), stop=(fc == FC - 1))
                    ins.then_inc(S.moe_y, 1)

                def lot(it):
                    for s in range(SLOTS):
                        first = isinstance(it, int) and it == 0
                        up(s, it, first)
                        if not (first and s == 0):
                            down((s - 1) % SLOTS, base + s + it * SLOTS)

                lot(0)
                if m in (1, 3):
                    pe.wait_ge(S.comb_ready, m + 1)
                    if m == 1:
                        pe.wait_ge(S.in_e8, 16)
                    nc.tensor.transpose(ps7[0:E, 264:264 + P], mo.comb, ident).then_inc(S.combt_psum, 1)
                    pe.wait_ge(S.combt_ready, m // 2 + 1)
                    mm(ps7[:, 0:D], mo.combt[0:E, :], e8[:, (m // 2) * D:(m // 2 + 1) * D], start=True, stop=True)\
                        .then_inc(S.b2_psum, 1)
                if nu // SLOTS == 2:
                    lot(1)
                else:
                    with pe.Fori(1, nu // SLOTS) as it:
                        lot(it)
                down(SLOTS - 1, base + nu)

            W = lambda name, *shape: weight(wa, L0X, name, *shape)
            pe.wait_ge(S.in_const, 16)
            tokens_t(0, 2)
            pe.wait_ge(S.in_l0x, 16)
            for c in range(C):
                ins = mm(ps6[:, 0:D], xt[:, c, :], W("wq", C, D)[:, c, :], start=(c == 0), stop=(c == 1))
            ins.then_inc(S.q_psum, 1)
            for g in range(KT // 4):
                pe.wait_ge(S.xn_ready, 4 * g + 4)
                if g >= 1:
                    pe.wait_ge(S.xn_act, g)
                    pe.wait_ge(S.xn_dve, g)
                for i in range(4):
                    xn = q.xn[:, (4 * g + i) % 8, :]
                    nc.tensor.transpose(halves[0][:, i * P:(i + 1) * P], xn[:, 0:P], ident)
                    ins = nc.tensor.transpose(halves[1][0:CB, i * P:(i + 1) * P], xn[:, P:CD], ident)
                ins.then_inc(S.xn_psum, 1)
            for j in range(KT + 1):
                if j < KT:
                    pe.wait_ge(S.xn_act, j // 4 + 1)
                    pe.wait_ge(S.xn_dve, j // 4 + 1)
                if j >= 2:
                    pe.wait_ge(S.kv_v, j - 1)
                dst, k = halves[2 + j % 2], slice(j * P, (j + 1) * P)
                if j < KT:
                    w = W("wkv", C, 2 * D)
                    mm(dst, xnt[:, 0, k], w[:, 0, :], start=True, stop=False)
                    ins = mm(dst, xnt[0:CB, 1, k], w[0:CB, 1, :], start=False, stop=True)
                else:
                    w = W("wlkv", C, 2 * D)
                    mm(dst, xt[:, 0, :], w[:, 0, :], start=True, stop=False)
                    ins = mm(dst, xt[:, 1, :], w[:, 1, :], start=False, stop=True)
                ins.then_inc(S.kv_psum, 1)
            pe.wait_ge(S.q_norm, 1)
            for c in range(C):
                ins = nc.tensor.transpose(ps6[:, 256 + c * P:256 + (c + 1) * P], xh[:, c * P:(c + 1) * P], ident)
            ins.then_inc(S.qt_psum, 1)
            for g in range(9):
                n = 2 if g < 8 else 1
                pe.wait_ge(S.khat_ready, min(2 * g + 2, KT + 1))
                if g >= 2:
                    pe.wait_ge((S.kt_dve, S.kt_act)[g % 2], g // 2)
                for i in range(n):
                    for c in range(C):
                        ins = nc.tensor.transpose(halves[4 + g % 2][:, (c * n + i) * P:(c * n + i + 1) * P],
                                                  q.knat[:, 2 * g + i, c * P:(c + 1) * P], ident)
                ins.then_inc(S.kt_psum, 1)
            pe.wait_ge(S.qbd_ready, 1)
            pe.wait_ge(S.kt_dve, 5)
            pe.wait_ge(S.kt_act, 4)

            def scores_l0x(t):
                b, hp = t // 2, t % 2
                bank = ps01
                mm(bank[:, 0:512], q.qbd[:, b, hp, :], q.kt[:, hp, b * KEYS:b * KEYS + 512], start=True, stop=True)
                mm(bank[:, 512:1024], q.qbd[:, b, hp, :], q.kt[:, hp, b * KEYS + 512:(b + 1) * KEYS], start=True, stop=True)
                return mm(halves[2][:, 0:P], q.qbd[:, b, hp, :], q.kt[:, hp, KT * P:(KT + 1) * P],
                          start=True, stop=True)

            attention("l0x", 4, scores_l0x, lambda u: q.pt[:, u % 2, :],
                      lambda u, k: q.v[:, (u // 2) * KTB + k if k < KTB else KT, (u % 2) * P:(u % 2) * P + P], P, 9,
                      lambda u: nc.tensor.transpose(ps7[:, 0:P], xh[:, (u % 2) * P:(u % 2) * P + P], ident))
            pe.wait_ge(S.opt_ready, 4)
            for c in range(C):
                ins = mm(ps6[:, 0:D], xt[:, c, :], W("wo", C, D)[:, c, :], start=(c == 0), stop=(c == 1))
            ins.then_inc(S.out_psum, 1)

            if stages > 1:
                W = lambda name, *shape: weight(wb, L0A, name, *shape)
                tokens_t(1, 4)
                pe.wait_ge(S.in_l0a, 16)
                for h in range(4):
                    for c in range(C):
                        mm(ps01[:, h * P:(h + 1) * P], W("wq", C, 512)[:, c, h * P:(h + 1) * P], xt[:, c, :],
                           start=(c == 0), stop=(c == 1))
                for c in range(C):
                    mm(ps23[:, 0:P], W("wk", C, P)[:, c, :], xt[:, c, :], start=(c == 0), stop=(c == 1))
                for c in range(C):
                    ins = mm(ps23[:, P:P + 64], xt[:, c, :], W("wv", C, 64)[:, c, :], start=(c == 0), stop=(c == 1))
                ins.then_inc(S.sa_qkv, 1)
                pe.wait_ge(S.sa_q, 1)
                for h in range(4):
                    for b in range(B):
                        ins = mm(ps45[:, (h * 2 + b) * LQ:(h * 2 + b + 1) * LQ], r0.qbd[:, b, h, :],
                                 r0.kt[:, b * LQ:(b + 1) * LQ], start=True, stop=True)
                ins.then_inc(S.sa_s, 1)
                pe.wait_ge(S.sa_norm, 1)
                for h in range(4):
                    ins = nc.tensor.transpose(ps01[:, h * P:(h + 1) * P], r0.p[:, h].rearrange("p b k -> p (b k)"), ident)
                ins.then_inc(S.sa_pt, 1)
                pe.wait_ge(S.sa_ptc, 1)
                for h in range(4):
                    for b in range(B):
                        for j in range(2):
                            k = slice(b * LQ, (b + 1) * LQ)
                            ins = mm(halves[2 + b][64 * j:64 * j + 64, h * LQ:(h + 1) * LQ], r0.v[k, :],
                                     r0.pt[k, h, 64 * j:64 * j + 64], start=True, stop=True)
                ins.then_inc(S.sa_ot, 1)
                pe.wait_ge(S.sa_otc, 1)
                for h in range(4):
                    ins = mm(ps6[:, 0:D], r0.ot[:, h, :], W("wo", 4, D)[:, h, :], start=(h == 0), stop=(h == 3))
                ins.then_inc(S.out_psum, 1)
            if stages > 2:
                tokens_t(2, 6)
                mixture(0)

            def cross16(i, stage, wt, tab, norms_done):
                W = lambda name, *shape: weight(wt, tab, name, *shape)
                tokens_t((3, 9)[i], norms_done)
                pe.wait_ge((S.in_l1x, S.in_l3x)[i], 16)
                for c in range(C):
                    for cc in range(C):
                        ins = mm(ps6[:, c * P:(c + 1) * P], W("wq", C, D)[:, cc, c * P:(c + 1) * P], xt[:, cc, :],
                                 start=(cc == 0), stop=(cc == 1))
                ins.then_inc(S.q16_psum, 1)
                if i == 0:
                    pe.wait_ge(S.in_ctxt, 16)
                ct = carve(ctxt, 0, C, B * KEYS)
                for j in range(16):
                    if j >= 4:
                        pe.wait_ge(S.c_act if j % 2 else S.c_dve, 8 * i + j // 2 - 1)
                    dst = halves[j % 4]
                    if j < 8:
                        c, kb = j // 4, j % 4
                        k = slice(kb * 512, (kb + 1) * 512)
                        w = W("wk", C, D)
                        mm(dst, w[:, 0, c * P:(c + 1) * P], ct[:, 0, k], start=True, stop=False)
                        ins = mm(dst, w[0:CB, 1, c * P:(c + 1) * P], ct[0:CB, 1, k], start=False, stop=True)
                    else:
                        w = W("wv", C, D)
                        for a in range(2):
                            kt = 2 * (j - 8) + a
                            k = slice(kt * P, (kt + 1) * P)
                            mm(dst[:, a * D:(a + 1) * D], ct[:, 0, k], w[:, 0, :], start=True, stop=False)
                            ins = mm(dst[:, a * D:(a + 1) * D], ct[0:CB, 1, k], w[0:CB, 1, :], start=False, stop=True)
                    ins.then_inc(S.c_psum, 1)
                pe.wait_ge(S.c_act, 8 * i + 8)
                pe.wait_ge(S.c_dve, 8 * i + 8)
                pe.wait_ge(S.q16_ready, i + 1)

                def scores(t):
                    cb, g = t // 4, t % 4
                    c, b = cb // 2, cb % 2
                    lhs = n16.qbd[:, c, b, 2 * g:2 * g + 2, :].rearrange("p j k -> p (j k)")
                    for k in range(2):
                        ins = mm((ps01, ps23)[t % 2][:, k * 512:(k + 1) * 512], lhs,
                                 n16.kt[:, c, b * KEYS + k * 512:b * KEYS + (k + 1) * 512], start=True, stop=True)
                    return ins

                def values(u, k):
                    cb, g = u // 4, u % 4
                    at = (cb // 2) * P + 32 * g
                    return n16.v[:, (cb % 2) * KTB + k, at:at + 32]

                attention(stage, 16, scores, lambda u: n16.pt[:, u % 2, :], values, 32, 8)
                pe.wait_ge(S.att_on, ATT_BASE[stage] + 16)
                for c in range(C):
                    for b in range(B):
                        ins = nc.tensor.transpose(ps6[:, (c * 2 + b) * P:(c * 2 + b + 1) * P], n16.o[:, c, b, :], ident)
                ins.then_inc(S.o16_psum, 1)
                pe.wait_ge(S.o16_ready, i + 1)

            if stages > 3:
                cross16(0, "l1x", wa, L1X, 7)
                w = weight(wa, L1X, "wo", C, D)
                for c in range(C):
                    ins = mm(ps6[:, 0:D], n16.ot[:, c, :], w[:, c, :], start=(c == 0), stop=(c == 1))
                ins.then_inc(S.out_psum, 1)
            if stages > 4:
                tokens_t(4, 8)
                w = weight(wa, L1X, "l1a_w", C, 32)
                for c in range(C):
                    ins = mm(ps6[:, 0:32], xt[:, c, :], w[:, c, :], start=(c == 0), stop=(c == 1))
                ins.then_inc(S.conv_s, 1)
                pe.wait_ge(S.conv_a, 1)
                nc.tensor.transpose(ps6[:, 32:32 + P], cv.full, ident).then_inc(S.conv_at, 1)
                pe.wait_ge(S.conv_atc, 1)
                mm(ps6[:, 256:512], cv.at, xh[:], start=True, stop=True).then_inc(S.conv_y, 1)
            if stages > 5:
                tokens_t(5, 9)
                mixture(1)
            if stages > 6:
                W = lambda name, *shape: weight(wb, L2X, name, *shape)
                tokens_t(6, 10)
                pe.wait_ge(S.in_l2x, 16)
                for h in range(8):
                    for c in range(C):
                        ins = mm(ps01[:, h * P:(h + 1) * P], W("wq", C, 1024)[:, c, h * P:(h + 1) * P], xt[:, c, :],
                                 start=(c == 0), stop=(c == 1))
                ins.then_inc(S.qa_psum, 1)
                pe.wait_ge(S.qa_ready, 1)
                for hh in range(2):
                    if hh == 1:
                        pe.wait_ge(S.h1_dve, B)
                        pe.wait_ge(S.h1_act, B)
                    for i in range(8):
                        h = 8 * hh + i
                        r = slice(64 * (h % 2), 64 * (h % 2) + 64)
                        w = W("wk", 8, CD)[r, h // 2, :]
                        dst = slice((i // 2) * P, (i // 2 + 1) * P)
                        mm(halves[2 + i % 2][:, dst], w[:, 0:P], n64.qt[r, h // 2, :], start=True, stop=True)
                        ins = mm(halves[4 + i % 2][0:CB, dst], w[:, P:CD], n64.qt[r, h // 2, :], start=True, stop=True)
                    ins.then_inc(S.h1_psum, 1)
                pe.wait_ge(S.h1_dve, 2 * B)
                pe.wait_ge(S.h1_act, 2 * B)
                ct = carve(ctxt, 0, C, B * KEYS)

                def scores64(t):
                    b, hp = t // 8, t % 8
                    for k in range(2):
                        keys = slice(b * KEYS + k * 512, b * KEYS + (k + 1) * 512)
                        dst = (ps01, ps23)[t % 2][:, k * 512:(k + 1) * 512]
                        heads = slice(2 * hp, 2 * hp + 2)
                        mm(dst, n64.qa[:, b, heads, :].rearrange("p h q -> p (h q)"), ct[:, 0, keys],
                           start=True, stop=False)
                        ins = mm(dst, n64.qb[0:CB, b, heads, :].rearrange("p h q -> p (h q)"), ct[0:CB, 1, keys],
                                 start=False, stop=True)
                    return ins

                def context_out(u):
                    nc.tensor.transpose(ps7[:, 0:P], n64.o[:, u % 2, 0:P], ident)
                    return nc.tensor.transpose(ps7[0:CB, P:2 * P], n64.o[:, u % 2, P:CD], ident)

                attention("l2x", 16, scores64, lambda u: n64.pt[:, u % 2, :],
                          lambda u, k: ctxn[:, ((u // 8) * KTB + k) * CD:((u // 8) * KTB + k + 1) * CD], CD, 8, context_out)
                pe.wait_ge(S.opt_ready, 4 + 16)
                for h in range(16):
                    dst = ps01[64 * (h % 2):64 * (h % 2) + 64, (h // 2) * P:(h // 2 + 1) * P]
                    w = W("wv", 2, 1024)[:, :, h * 64:(h + 1) * 64]
                    mm(dst, w[:, 0, :], n64.opa[:, :, h, :], start=True, stop=False)
                    ins = mm(dst, w[CB:P, 1, :], n64.opb[CB:P, :, h, :], start=False, stop=True)
                ins.then_inc(S.ot_psum, 1)
                pe.wait_ge(S.ot_ready, 1)
                for h in range(8):
                    ins = mm(ps6[:, 0:D], n64.ot[:, h, :], W("wo", 8, D)[:, h, :], start=(h == 0), stop=(h == 7))
                ins.then_inc(S.out_psum, 1)
            if stages > 7:
                tokens_t(7, 11)
                pe_ttt(pe)
            if stages > 8:
                tokens_t(8, 12)
                mixture(2)
            if stages > 9:
                cross16(1, "l3x", wb, L3X, 13)
                w = weight(wb, L3X, "w1", C, 512)
                for f in range(4):
                    for c in range(C):
                        ins = mm(halves[0][:, f * P:(f + 1) * P], w[:, c, f * P:(f + 1) * P], n16.ot[:, c, :],
                                 start=(c == 0), stop=(c == 1))
                ins.then_inc(S.m_h, 1)
                pe.wait_ge(S.m_hc, 1)
                w = weight(wb, L3X, "w2", 4, D)
                for f in range(4):
                    ins = mm(ps6[:, 0:D], n16.h[:, f, :], w[:, f, :], start=(f == 0), stop=(f == 3))
                ins.then_inc(S.out_psum, 1)
            if stages > 10:
                tokens_t(10, 14)
                pe.wait_ge(S.in_l3a, 16)
                for i, name in enumerate(("wz", "wh")):
                    w = weight(wa, L3A, name, C, D)
                    for cc in range(C):
                        for c in range(C):
                            ins = mm(ps01[:, i * 512 + cc * P:i * 512 + (cc + 1) * P], w[:, c, cc * P:(cc + 1) * P], xt[:, c, :],
                                     start=(c == 0), stop=(c == 1))
                ins.then_inc(S.g_psum, 1)
                pe.wait_ge(S.g_scan, 4)
                for c in range(C):
                    ins = nc.tensor.transpose(ps6[:, c * P:(c + 1) * P], gr.h[:, c, :], ident)
                ins.then_inc(S.g_back, 1)
            if stages > 11:
                tokens_t(11, 15)
                mixture(3)


def chunks(a, np):
    n = -(-a.shape[0] // P)
    if a.shape[0] < n * P:
        full = np.zeros((n * P,) + a.shape[1:], a.dtype)
        full[:a.shape[0]] = a
        a = full
    return a.reshape(n, P, -1).transpose(1, 0, 2).reshape(P, -1)


def pack_units(np, ups, down, per):
    cat = []
    for w in ups:
        cat.append(w.reshape(E, C, P, per, FU).transpose(0, 3, 2, 1, 4).reshape(E * per, P, C * FU))
    cat.append(down.reshape(E, per, FC, P, D).transpose(0, 1, 3, 2, 4).reshape(E * per, P, FC * D))
    return np.ascontiguousarray(np.concatenate(cat, axis=2))


def layout(inp, np):
    g = {k: np.asarray(v) for k, v in inp.items()}
    f = np.float32
    a = {}
    a["x"] = np.ascontiguousarray(g["x"].reshape(P, D))
    rows = g["ctx_768"].reshape(KT * P, CD)
    a["ctx"] = np.ascontiguousarray(rows.reshape(KT, P, CD).transpose(1, 0, 2).reshape(P, KT * CD))
    a["ctxt"] = np.ascontiguousarray(chunks(rows.T, np))
    a["mask"] = np.ascontiguousarray(g["mask_BxS2_bk0"].reshape(B * KEYS))

    def column(v):
        return chunks(v.reshape(-1, 1), np)

    twice = lambda v: np.concatenate([v, v])
    c = {"l0x_lg": g["L0_xattn_ln_l_g"], "l0x_lb": g["L0_xattn_ln_l_b"], "l0x_xg": g["L0_xattn_ln_x_g"],
         "l0x_xb": g["L0_xattn_ln_x_b"], "l0x_qg": twice(g["L0_xattn_qn_g"]), "l0x_kg": twice(g["L0_xattn_kn_g"]),
         "l0a_w": g["L0_attn_norm_w"], "l0a_b": g["L0_attn_norm_b"], "l1x_bq": g["L1_xattn_bq"],
         "l1x_bk": g["L1_xattn_bk"], "l1x_bv": g["L1_xattn_bv"], "l3x_bq": g["L3_xattn_bq"],
         "l3x_bk": g["L3_xattn_bk"], "l3x_bv": g["L3_xattn_bv"], "l3x_b1": g["L3_xattn_b1"],
         "l3a_bz": g["L3_attn_bz"], "l3a_bh": g["L3_attn_bh"], "l1f_b1": g["L1_ffn_b1"].reshape(-1),
         "l3f_b0": g["L3_ffn_b0"].reshape(-1), "l3f_b1": g["L3_ffn_b1"].reshape(-1)}
    a["cols"] = np.ascontiguousarray(np.concatenate([column(c[n]) for n in COLS], axis=1))
    r = {"l0x_bo": "L0_xattn_bo", "l0a_ow": "L0_attn_out_norm_w", "l0a_ob": "L0_attn_out_norm_b",
         "l1x_bo": "L1_xattn_bo", "l1a_b": "L1_attn_b", "l2x_bo": "L2_xattn_b_o", "l2a_pb": "L2_attn_proj_b",
         "l3x_b2": "L3_xattn_b2", "l3f_bg": "L3_ffn_bg"}
    a["rows"] = np.concatenate([g[r[n]] for n in ROWS])
    a["late"] = np.concatenate([g["L2_attn_" + n] for n in ("qkv_b", "qn_scale", "qn_bias", "kn_scale", "kn_bias")])
    a["e8"] = np.ascontiguousarray(np.concatenate([g["L1_ffn_b2"], g["L3_ffn_b2"]], axis=1))
    p = np.arange(P)
    a["const"] = np.concatenate([
        np.eye(P, dtype=f), np.ones((P, P), f), np.broadcast_to(np.arange(E, dtype=f), (P, E)),
        np.stack([(p // 16) % 2 == j for j in range(2)], 1).astype(f),
        np.stack([(p % LQ) >> i & 1 for i in range(6)], 1).astype(f),
        np.full((P, 72), -0.5, f), np.full((P, 32), 0.5, f),
        np.stack([(p // 16) % 8 == j for j in range(8)], 1).astype(f)], axis=1)
    a["router"] = np.ascontiguousarray(np.concatenate(
        [chunks(w, np) for w in (g["L0_ffn_router_w"].T, g["L1_ffn_gate_w"], g["L2_ffn_router_w"].T, g["L3_ffn_Wg"])],
        axis=1))

    def pack(*ws):
        return np.ascontiguousarray(np.concatenate([chunks(w, np) for w in ws], axis=1))

    kv = g["L0_attn_Wkv"]
    a["l0x"] = pack(g["L0_xattn_Wq"].T, g["L0_xattn_Wkv"].T, g["L0_xattn_Wlkv"].T, g["L0_xattn_Wo"].T)
    a["l0a"] = pack(g["L0_attn_Wq"], np.concatenate([kv[:, :64], kv[:, :64]], axis=1), kv[:, 64:], g["L0_attn_Wo"])
    a["l1x"] = pack(g["L1_xattn_Wq"], g["L1_xattn_Wk"], g["L1_xattn_Wv"], g["L1_xattn_Wo"], g["L1_attn_W"].T)
    wv = g["L2_xattn_w_v"]
    low = np.zeros((2 * P, 1024), f)
    low[:P], low[P + CB:] = wv[:P], wv[P:]
    a["l2x"] = pack(g["L2_xattn_w_q"], g["L2_xattn_w_k"].T, low, g["L2_xattn_w_o"])
    a["l2a"] = pack(g["L2_attn_qkv_w"], g["L2_attn_ttt_gate"], g["L2_attn_ttt_val"], g["L2_attn_ttt_proj"],
                    g["L2_attn_ttt_proj"].T, g["L2_attn_proj_w"])
    a["l3x"] = pack(g["L3_xattn_Wq"], g["L3_xattn_Wk"], g["L3_xattn_Wv"], g["L3_xattn_W1"], g["L3_xattn_W2"])
    a["l3a"] = pack(g["L3_attn_Wz"].T, g["L3_attn_Wh"].T)
    a["m0"] = pack_units(np, [g["L0_ffn_w1"]], g["L0_ffn_w2"], 1)
    a["m1"] = pack_units(np, [g["L1_ffn_w1"]], g["L1_ffn_w2"], 2)
    a["m2"] = pack_units(np, [g["L2_ffn_w_gate"].transpose(0, 2, 1), g["L2_ffn_w_up"].transpose(0, 2, 1)],
                         g["L2_ffn_w_down"].transpose(0, 2, 1), 1)
    a["m3"] = pack_units(np, [g["L3_ffn_W1"], g["L3_ffn_W0"]], g["L3_ffn_W2"], 2)
    return a


_ORDER = ["x", "ctx", "ctxt", "mask", "cols", "rows", "late", "e8", "const", "router",
          "l0x", "l0a", "l1x", "l2x", "l2a", "l3x", "l3a", "m0", "m1", "m2", "m3"]
STAGES = 12


def kernel(**inputs):
    import numpy as _np
    import concourse.bacc as _bacc
    from concourse import mybir as _mybir
    from concourse.bass_utils import run_bass_kernel_spmd as _run

    nc = _bacc.Bacc("TRN2", target_bir_lowering=False, num_devices=1)
    laid = layout(inputs, _np)
    arrays, args = {}, []
    for name in _ORDER:
        arr = laid[name]
        arrays[f"in_{name}_dram"] = arr
        args.append(nc.dram_tensor(f"in_{name}_dram", arr.shape, _mybir.dt.from_np(arr.dtype), kind="ExternalInput").ap())
    args.append(nc.dram_tensor("out_0_dram", (P, D), F32, kind="ExternalOutput").ap())
    perceiver_kernel(nc, *args, stages=STAGES)
    r = _run(nc, [arrays], core_ids=[0])
    return r.results[0]["out_0_dram"].reshape(B, LQ, D)
```

```python
from contextlib import ExitStack

import concourse.bass as bass
from concourse import mybir

F32 = mybir.dt.float32
I32 = mybir.dt.int32
U32 = mybir.dt.uint32
U8 = mybir.dt.uint8
ALU = mybir.AluOpType
ACT = mybir.ActivationFunctionType
AX = mybir.AxisListType

P = 128
B, LQ = 2, 64
D = 256
C = D // P
KEYS = 1024
CD = 192
CB = CD - P
KT = B * KEYS // P
KTB = KEYS // P
E = 8
SLOTS = 4
FU = 512
FC = FU // P
UNIT = 3 * 1024
LN_EPS = 1e-5
NEG = -3.0e38
MASKED = -1.0e30

COLS = {}
for _name, _n in (("l0x_lg", 2), ("l0x_lb", 2), ("l0x_xg", 2), ("l0x_xb", 2), ("l0x_qg", 1), ("l0x_kg", 1),
                  ("l0a_w", 2), ("l0a_b", 2), ("l1x_bq", 2), ("l1x_bk", 2), ("l1x_bv", 2),
                  ("l3x_bq", 2), ("l3x_bk", 2), ("l3x_bv", 2), ("l3x_b1", 4), ("l3a_bz", 2), ("l3a_bh", 2),
                  ("l1f_b1", 64), ("l3f_b0", 64), ("l3f_b1", 64)):
    COLS[_name] = (sum(n for _, n in COLS.values()), _n)
NCOLS = sum(n for _, n in COLS.values())

ROWS = {}
for _name, _n in (("l0x_bo", D), ("l0a_ow", D), ("l0a_ob", D), ("l1x_bo", D), ("l1a_b", 32), ("l2x_bo", D),
                  ("l2a_pb", D), ("l3x_b2", D), ("l3f_bg", E)):
    ROWS[_name] = (sum(n for _, n in ROWS.values()), _n)
NROWS = sum(n for _, n in ROWS.values())

LATE = {"qkvb": (0, 3 * D), "qs": (768, 16), "qb": (784, 16), "ks": (800, 16), "kb": (816, 16)}
NLATE = 832

CONSTS = {"ident": (0, 128), "ones": (128, 128), "iota": (256, 8), "par": (264, 2), "bits": (266, 6),
          "nhalf": (272, 72), "phalf": (344, 32),
          "head": (376, 8)}
NCONST = 384

ROUTER = 4 * 16

def table(*items):
    out, at = {}, 0
    for name, n in items:
        out[name] = (at, n)
        at += n
    return out, at

L0X, L0X_N = table(("wq", 2 * D), ("wkv", 2 * 2 * D), ("wlkv", 2 * 2 * D), ("wo", 2 * D))
L0A, L0A_N = table(("wq", 2 * 512), ("wk", 2 * P), ("wv", 2 * 64), ("wo", 4 * D))
L1X, L1X_N = table(("wq", 2 * D), ("wk", 2 * D), ("wv", 2 * D), ("wo", 2 * D), ("l1a_w", 2 * 32))
L2X, L2X_N = table(("wq", 2 * 1024), ("wk", 8 * CD), ("wv", 2 * 1024), ("wo", 8 * D))
L2A, L2A_N = table(("qkv", 2 * 768), ("gate", 2 * 1024), ("val", 2 * 1024), ("proj", 8 * D),
                   ("projt", 2 * 1024), ("pw", 2 * D))
L3X, L3X_N = table(("wq", 2 * D), ("wk", 2 * D), ("wv", 2 * D), ("w1", 2 * 512), ("w2", 4 * D))
L3A, L3A_N = table(("wz", 2 * D), ("wh", 2 * D))

L0X_ORDER = [KT] + list(range(KT))
L0X_GROUPS = [(KT, 1)] + [(j, 2) for j in range(0, KT, 2)]
ATT_BASE = {"l0x": 0, "l1x": 4, "l2x": 20, "l3x": 36}
OPT_BASE = {"l0x": 0, "l2x": 4}
MOE_BASE = (0, 8, 24, 32)
MOE_UNITS = (8, 16, 8, 16)



class Views:
    pass


class Own:

    def __init__(self, eng, sem):
        self.eng, self.sem, self.n = eng, sem, 0

    def __call__(self, ins):
        ins.then_inc(self.sem, 1)
        self.n += 1

    def wait(self):
        self.eng.wait_ge(self.sem, self.n)


def perceiver_kernel(nc, x_in, ctx_in, ctxt_in, mask_in, cols_in, rows_in, late_in, e8_in, const_in, router_in,
                     l0x_in, l0a_in, l1x_in, l2x_in, l2a_in, l3x_in, l3a_in, m0_in, m1_in, m2_in, m3_in, out,
                     stages=12):
    with ExitStack() as ctx:
        def sb(name, shape, dt=F32):
            return ctx.enter_context(nc.sbuf_tensor(name, shape, dt))

        def sem(name):
            return ctx.enter_context(nc.semaphore(name))

        class S:
            (in_x, in_const, in_ctx, in_cols, in_l0x, in_mask) = (
                sem(n) for n in "in_x in_const in_ctx in_cols in_l0x in_mask".split())
            (in_rows, in_router, in_e8, in_l0a, moe_y, kv_psum) = (
                sem(n) for n in "in_rows in_router in_e8 in_l0a moe_y kv_psum".split())
            (in_ctxt, in_l1x, out_psum, in_l2x, conv_y, in_l2a) = (
                sem(n) for n in "in_ctxt in_l1x out_psum in_l2x conv_y in_l2a".split())
            (in_late, in_l3x, in_l3a, x_done, stored, ln_var) = (
                sem(n) for n in "in_late in_l3x in_l3a x_done stored ln_var".split())
            (ln_rstd, cln_var, cln_rstd, kv_k, kv_ss, kv_sq) = (
                sem(n) for n in "ln_rstd cln_var cln_rstd kv_k kv_ss kv_sq".split())
            (t_nrm, t_nrmp, att_max, att_pt, att_exp, att_o) = (
                sem(n) for n in "t_nrm t_nrmp att_max att_pt att_exp att_o".split())
            (att_pta, top_gap, top_exp, moe_up, moe_h, moe_g) = (
                sem(n) for n in "att_pta top_gap top_exp moe_up moe_h moe_g".split())
            (c_psum, c_act, kv_v, xn_psum, xn_act, kt_psum) = (
                sem(n) for n in "c_psum c_act kv_v xn_psum xn_act kt_psum".split())
            (kt_act, sa_max, sa_exp, conv_max, conv_exp, h1_psum) = (
                sem(n) for n in "kt_act sa_max sa_exp conv_max conv_exp h1_psum".split())
            (h1_act, t_a, t_sig, t_back, t_backc, n_e) = (
                sem(n) for n in "h1_act t_a t_sig t_back t_backc n_e".split())
            (n_ec, n_m1, n_mc, n_u, n_uc, n_w) = (
                sem(n) for n in "n_ec n_m1 n_mc n_u n_uc n_w".split())
            (n_wc, m_h, m_hc, g_psum, g_z, t_qkv) = (
                sem(n) for n in "n_wc m_h m_hc g_psum g_z t_qkv".split())
            (t_qk, t_kqt, t_kqtc, t_gram, t_gramc, t_b) = (
                sem(n) for n in "t_qk t_kqt t_kqtc t_gram t_gramc t_b".split())
            (t_h, t_x, t_xc, t_z, t_zc, t_pred) = (
                sem(n) for n in "t_h t_x t_xc t_z t_zc t_pred".split())
            (t_e, t_et, t_etc, t_sh, t_dh, t_da) = (
                sem(n) for n in "t_e t_et t_etc t_sh t_dh t_da".split())
            (t_s, t_tr, t_trp, n_ba, n_p, n_pc) = (
                sem(n) for n in "t_s t_tr t_trp n_ba n_p n_pc".split())
            (n_m, t_r, t_rc, t_o, t_oc, dve_own) = (
                sem(n) for n in "n_m t_r t_rc t_o t_oc dve_own".split())
            (xh_ready, xt_psum, xt_ready, att_on, att_ptd, opt_psum) = (
                sem(n) for n in "xh_ready xt_psum xt_ready att_on att_ptd opt_psum".split())
            (opt_ready, att_s, router_psum, comb_ready, moe_acc, combt_psum) = (
                sem(n) for n in "opt_ready att_s router_psum comb_ready moe_acc combt_psum".split())
            (combt_ready, b2_psum, xn_ready, xn_dve, q_norm, khat_ready) = (
                sem(n) for n in "combt_ready b2_psum xn_ready xn_dve q_norm khat_ready".split())
            (q_psum, qt_psum, qbd_ready, kt_dve, sa_qkv, sa_q) = (
                sem(n) for n in "q_psum qt_psum qbd_ready kt_dve sa_qkv sa_q".split())
            (sa_s, sa_norm, sa_pt, sa_ptc, sa_ot, sa_otc) = (
                sem(n) for n in "sa_s sa_norm sa_pt sa_ptc sa_ot sa_otc".split())
            (q16_psum, q16_ready, o16_psum, o16_ready, conv_s, conv_a) = (
                sem(n) for n in "q16_psum q16_ready o16_psum o16_ready conv_s conv_a".split())
            (conv_at, conv_atc, qa_psum, qa_ready, h1_dve, ot_psum) = (
                sem(n) for n in "conv_at conv_atc qa_psum qa_ready h1_dve ot_psum".split())
            (ot_ready, g_scan, g_back) = (
                sem(n) for n in "ot_ready g_scan g_back".split())

        slot_full = [ctx.enter_context(nc.semaphore(f"slot_full{i}")) for i in range(SLOTS)]

        ring = sb("ring", [P, SLOTS, UNIT])
        wa = sb("wa", [P, L2A_N])
        wb = sb("wb", [P, L2X_N])
        ctxn = sb("ctxn", [P, KT * CD])
        ctxt = sb("ctxt", [P, C * B * KEYS])
        scr = sb("scr", [P, 11520])
        cols = sb("cols", [P, NCOLS])
        rows = sb("rows", [P, NROWS])
        cst = sb("cst", [P, NCONST])
        router = sb("router", [P, ROUTER])
        e8 = sb("e8", [E, 2 * D])
        x = sb("x", [P, D])
        xh = sb("xh", [P, D])
        xt = sb("xt", [P, C, P])
        sm = sb("sm", [P, 256])
        ps01 = ctx.enter_context(nc.psum_tensor("ps01", [P, 1024], F32))
        ps23 = ctx.enter_context(nc.psum_tensor("ps23", [P, 1024], F32))
        ps45 = ctx.enter_context(nc.psum_tensor("ps45", [P, 1024], F32))
        ps6 = ctx.enter_context(nc.psum_tensor("ps6", [P, 512], F32))
        ps7 = ctx.enter_context(nc.psum_tensor("ps7", [P, 512], F32))
        halves = [ps01[:, 0:512], ps01[:, 512:1024], ps23[:, 0:512], ps23[:, 512:1024],
                  ps45[:, 0:512], ps45[:, 512:1024]]

        def carve(tensor, at, *shape):
            n = 1
            for s in shape:
                n *= s
            v = tensor[:, at:at + n]
            names = "abcd"[:len(shape)]
            if len(shape) > 1:
                v = v.rearrange(f"p ({' '.join(names)}) -> p {' '.join(names)}",
                                **{k: s for k, s in zip(names, shape)})
            return v

        def weight(tensor, tab, name, *shape):
            at, n = tab[name]
            return carve(tensor, at, *shape)

        def col(name, i=0):
            at, _ = COLS[name]
            return cols[:, at + i:at + i + 1]

        def row(name):
            at, n = ROWS[name]
            return rows[:, at:at + n]

        ident, ones = cst[:, 0:128], cst[:, 128:256]
        iota8, parity, bits = cst[:, 256:264], cst[:, 264:266], cst[:, 266:272]
        nhalf, phalf, head8 = cst[:, 272:344], cst[:, 344:376], cst[:, 376:384]
        stat, mv, ve, rstd = sm[:, 0:6], sm[:, 6:8], sm[:, 8:9], sm[:, 9:10]


        NK = KEYS + P
        a, w, q = L0X_N, L0A_N, Views()
        xnt = carve(ctxt, 0, C, B * KEYS)
        q.kt, q.v = carve(scr, 0, C, (KT + 1) * P), carve(scr, 4352, KT + 1, D)
        q.sc, q.qbd, q.sq = carve(scr, 8704, 2, NK), carve(scr, 11008, B, C, P), carve(wb, w + 2 * NK + 2048, 2, D)
        q.knat, q.pt = carve(wa, a, KT + 1, D), carve(wa, a + 4352, 2, NK)
        q.stats, q.mv = carve(wa, a + 6656, KT, 6), carve(wa, a + 6752, KT, 2)
        q.cve, q.crs = carve(wa, a + 6784, KT), carve(wa, a + 6800, KT)
        q.ss, q.rs, q.rt = carve(wa, a + 6816, 72), carve(wa, a + 6888, 72), carve(sm, 160, 72)
        q.mask, q.mask8 = carve(wb, w, B, NK), wb[:, w + 2 * NK:w + 2 * NK + 512].bitcast(U8)
        q.xn = carve(wb, w + 2 * NK + 512, 8, CD)
        gain = sm[:, 40:41]
        att = Views()
        att.nmax = sm[:, 16:18]
        att.rsum = sm[:, 18:20]
        att.rinv = sm[:, 20:22]
        att.mx = sm[:, 22:24]

        late = ctxn

        r0 = Views()
        r0.qbd = carve(scr, 0, B, 4, P)
        r0.kt = carve(scr, 1024, P)
        r0.v = carve(scr, 1152, 64)
        r0.p = carve(scr, 1216, 4, B, LQ)
        r0.pt = carve(scr, 1728, 4, P)
        r0.ot = carve(scr, 2240, 4, P)
        r0.o = carve(scr, 2752, D)
        r0.mx = sm[:, 48:56]
        r0.sum = sm[:, 56:64]
        r0.rinv = sm[:, 64:72]
        n16 = Views()
        n16.kt = carve(scr, 3072, C, B * KEYS)
        n16.v = carve(scr, 7168, KT, D)
        n16.p = carve(wa, 8064, 2, KEYS)
        n16.pt = carve(wa, 4224, 2, KEYS)
        n16.qt = carve(wa, 6272, C, P)
        n16.qbd = carve(wa, 2176, C, B, 8, LQ)
        n16.o = carve(wa, 6528, C, B, P)
        n16.ot = carve(wa, 7040, C, P)
        n16.tmp = carve(wa, 7296, C, P)
        n16.h = carve(wa, 7552, 4, P)
        n64 = Views()
        n64.qt = carve(scr, 0, 8, P)
        n64.opa = carve(scr, 0, B, 16, LQ)
        n64.qa = carve(scr, 2048, B, 16, LQ)
        n64.qb = carve(scr, 4096, B, 16, LQ)
        n64.opb = carve(scr, 4096, B, 16, LQ)
        n64.p = carve(scr, 6144, 2, KEYS)
        n64.pt = carve(scr, 8192, 2, KEYS)
        n64.o = carve(scr, 10240, 2, CD)
        n64.ot = carve(scr, 6144, 8, P)
        cv = Views()
        cv.w = carve(scr, 0, 32)
        cv.a = carve(scr, 64, 2, LQ)
        cv.b = carve(scr, 192, LQ)
        cv.nb = sm[:, 80:86]
        cv.full = carve(scr, 256, P)
        cv.at = carve(scr, 384, P)
        cv.mx = sm[:, 72:73]
        cv.sum = sm[:, 73:74]
        cv.rs = sm[:, 74:75]
        mo = Views()
        mo.g = carve(scr, 0, 2, FU)
        mo.h = carve(scr, 1024, 2, FU)
        mo.lg = sm[:, 96:104]
        mo.top = sm[:, 104:112]
        mo.idx = sm[:, 112:120].bitcast(U32)
        mo.idxf = sm[:, 120:128]
        mo.gap = sm[:, 128:130]
        mo.ex = sm[:, 130:132]
        mo.z = sm[:, 132:133]
        mo.rz = sm[:, 133:134]
        mo.wt = sm[:, 134:136]
        mo.c0 = sm[:, 136:144]
        mo.c1 = sm[:, 144:152]
        mo.comb = sm[:, 152:160]
        mo.combt = carve(scr, 2048, P)
        gr = Views()
        gr.e = carve(scr, 0, C, P)
        gr.z = carve(scr, 256, C, P)
        gr.a = carve(scr, 512, C, P)
        gr.b = carve(scr, 768, C, P)
        gr.h = carve(scr, 1024, C, P)
        gr.t = carve(scr, 1280, C, P)

        tt = Views()
        tt.qkv = carve(scr, 0, 3, D)
        tt.kqt = carve(scr, 768, 2, C, P)
        tt.gram = carve(scr, 1280, 2, P)
        tt.s = carve(scr, 1536, 8, P)
        tt.g = carve(scr, 2560, 8, P)
        tt.tb = carve(scr, 3584, 8, P)
        tt.w = carve(scr, 4608, 8, P)
        tt.h = carve(scr, 5632, 2, 8, P)
        tt.en = carve(scr, 7680, 2, D)
        tt.et = carve(scr, 8192, 2, C, P)
        tt.m = [[carve(scr, 8704 + (s * 3 + c) * 2 * P, 2, P) for c in range(3)] for s in range(2)]
        tt.sh = carve(scr, 10240, 2, P)
        tt.sgv = carve(scr, 10496, 2, P)
        tt.tmp = carve(scr, 10752, 6, P)
        tt.hn = carve(wb, L3X_N, 2, 8, P)
        tt.dan = carve(wb, L3X_N + 2048, 2, 8, P)
        tt.dbn = [carve(wa, 0, 8, P), carve(ctxn, 0, 8, P)]
        tt.u = [carve(ctxn, 1024 + c * 640, P) for c in range(3)]
        tt.wm = [carve(ctxn, 1152 + c * 640, P) for c in range(3)]
        tt.e = [carve(ctxn, 1280 + c * 640, 2, P) for c in range(3)]
        tt.pt = [carve(ctxn, 1536 + c * 640, P) for c in range(3)]
        tt.ai = xh[:, 0:P]
        tt.ss = sm[:, 160:192]
        tt.nr = sm[:, 192:224]
        tt.sc = xt[:, 0, 0:32]
        tt.nt = xt[:, 0, 32:64]
        tt.tr = sm[:, 224:227]
        tt.n2 = sm[:, 227:230]
        tt.n = sm[:, 230:233]
        tt.rn = sm[:, 233:236]
        tt.rn2 = sm[:, 236:239]
        NS_A, NS_B, NS_C, NS_ITERS, LR = 3.4445, -4.775, 2.0315, 5, 0.1
        block = ctx.enter_context(nc.Block())

        @block.sync
        def _(sp):
            sp.dma_start(x[:], x_in).then_inc(S.in_x, 16)
            sp.dma_start(cst[:], const_in).then_inc(S.in_const, 16)
            sp.dma_start(ctxn[:], ctx_in).then_inc(S.in_ctx, 16)
            sp.dma_start(cols[:], cols_in).then_inc(S.in_cols, 16)
            sp.dma_start(wa[:, 0:L0X_N], l0x_in).then_inc(S.in_l0x, 16)
            sp.dma_start(q.mask8, mask_in.partition_broadcast(P)).then_inc(S.in_mask, 16)
            sp.dma_start(rows[:], rows_in.partition_broadcast(P)).then_inc(S.in_rows, 16)
            sp.dma_start(router[:], router_in).then_inc(S.in_router, 16)
            sp.dma_start(e8[:], e8_in).then_inc(S.in_e8, 16)
            sp.dma_start(wb[:, 0:L0A_N], l0a_in).then_inc(S.in_l0a, 16)

            def units(m, source, first, n):
                width = source.shape[2]

                def lot(it):
                    for s in range(SLOTS):
                        if MOE_BASE[m] + first > 0:
                            sp.wait_ge(S.moe_y, MOE_BASE[m] - SLOTS + s + 1 + it * SLOTS)
                        k = it * SLOTS + s
                        unit = source[k] if isinstance(it, int) else \
                            source[bass.ds(k, 1)].rearrange("o p w -> (o p) w")
                        sp.dma_start(ring[:, s, 0:width], unit).then_inc(slot_full[s], 16)

                lots = range(first // SLOTS, (first + n) // SLOTS)
                if len(lots) == 1:
                    lot(lots[0])
                else:
                    with sp.Fori(lots[0], lots[-1] + 1) as it:
                        lot(it)

            units(0, m0_in, 0, 4)
            if stages > 1:
                sp.wait_ge(S.kv_psum, KT + 1)
                sp.dma_start(ctxt[:], ctxt_in).then_inc(S.in_ctxt, 16)
                sp.dma_start(wa[:, 0:L1X_N], l1x_in).then_inc(S.in_l1x, 16)
                sp.wait_ge(S.out_psum, 2)
                sp.dma_start(wb[:], l2x_in).then_inc(S.in_l2x, 16)
            if stages > 2:
                units(0, m0_in, 4, 4)
            if stages > 5:
                units(1, m1_in, 0, 4)
                sp.wait_ge(S.conv_y, 1)
                sp.dma_start(wa[:, 0:L2A_N], l2a_in).then_inc(S.in_l2a, 16)
                units(1, m1_in, 4, 12)
            if stages > 6:
                sp.wait_ge(S.out_psum, 4)
                sp.dma_start(late[:, 0:NLATE], late_in.partition_broadcast(P)).then_inc(S.in_late, 16)
                sp.dma_start(wb[:, 0:L3X_N], l3x_in).then_inc(S.in_l3x, 16)
            if stages > 8:
                units(2, m2_in, 0, 4)
                sp.wait_ge(S.out_psum, 5)
                sp.dma_start(wa[:, 0:L3A_N], l3a_in).then_inc(S.in_l3a, 16)
                units(2, m2_in, 4, 4)
            if stages > 11:
                units(3, m3_in, 0, 4)
                units(3, m3_in, 4, 12)
            if stages < 12:
                sp.wait_ge(S.in_e8, 16)
            sp.wait_ge(S.x_done, 1)
            sp.dma_start(out, x[:]).then_inc(S.stored, 16)
            sp.wait_ge(S.stored, 16)

        @block.gpsimd
        def _(pool):
            pool.wait_ge(S.in_const, 16)

            def norms(first, n):
                for i in range(first, first + n):
                    pool.wait_ge(S.ln_var, i + 1)
                    nc.gpsimd.tensor_tensor(rstd, ve, nhalf[:, 0:1], ALU.pow).then_inc(S.ln_rstd, 1)

            norms(0, 2)
            for g in range(KT // 4):
                pool.wait_ge(S.cln_var, g + 1)
                nc.gpsimd.tensor_tensor(q.crs[:, 4 * g:4 * g + 4], q.cve[:, 4 * g:4 * g + 4], nhalf[:, 0:4], ALU.pow)\
                    .then_inc(S.cln_rstd, 1)
            for i in range(KT + 1):
                pool.wait_ge(S.kv_k, i + 1)
                if i >= 2:
                    pool.wait_ge(S.kv_ss, i - 1)
                kn = q.knat[:, L0X_ORDER[i], :]
                nc.gpsimd.tensor_tensor(q.sq[:, i % 2, :], kn, kn, ALU.mult).then_inc(S.kv_sq, 1)
            last = 2 if stages == 1 else stages + 3
            norms(2, min(9, last) - 2)
            if stages == 7:
                norms(9, 1)
            if stages > 7:
                norms(9, 2)
                for s in range(2):
                    pool.wait_ge(S.t_nrm, s + 1)
                    nc.gpsimd.tensor_tensor(tt.n, tt.n2, phalf[:, 0:3], ALU.pow).then_inc(S.t_nrmp, 1)
                norms(11, last - 11)

        @block.scalar
        def _(act):
            def attention(stage, n, sc_of, nmax_of, p_of, pt_of):
                base = ATT_BASE[stage]
                for t in range(n + 1):
                    if t < n:
                        act.wait_ge(S.att_max, base + t + 1)
                        if t >= 2:
                            act.wait_ge(S.att_pt, base + t - 1)
                        nc.scalar.activation(p_of(t), sc_of(t), ACT.Exp, bias=att.nmax[:, t % 2:t % 2 + 1],
                                             accum_out=att.rsum[:, t % 2:t % 2 + 1]).then_inc(S.att_exp, 1)
                    if t >= 1:
                        act.wait_ge(S.att_pt, base + t)
                        if t >= 3:
                            act.wait_ge(S.att_o, base + t - 2)
                        nc.scalar.copy(pt_of(t - 1)[:, 0:512], ps45[:, 0:512]).then_inc(S.att_pta, 1)

            def mixture(m):
                base, nu = MOE_BASE[m], MOE_UNITS[m]
                act.wait_ge(S.top_gap, m + 1)
                nc.scalar.activation(mo.ex, mo.gap, ACT.Exp, accum_out=mo.z).then_inc(S.top_exp, 1)
                func = ACT.Gelu if m < 2 else ACT.Silu
                bias = (None, "l1f_b1", None, "l3f_b1")[m]

                def lot(it):
                    for s in range(SLOTS):
                        first = isinstance(it, int) and it == 0
                        k, par = it * SLOTS + s, s % 2
                        act.wait_ge(S.moe_up, base + s + 1 + it * SLOTS)
                        if m < 2:
                            if not (first and s < 2):
                                act.wait_ge(S.moe_y, base + s - 1 + it * SLOTS)
                            dst, done = mo.h, S.moe_h
                        else:
                            if not (first and s < 2):
                                act.wait_ge(S.moe_h, base + s - 1 + it * SLOTS)
                            dst, done = mo.g, S.moe_g
                        up = halves[par]
                        if bias is None:
                            nc.scalar.activation(dst[:, par, :], up, func).then_inc(done, 1)
                        else:
                            for fc in range(FC):
                                c = COLS[bias][0] + fc + s * FC + it * (SLOTS * FC)
                                ins = nc.scalar.activation(dst[:, par, fc * P:(fc + 1) * P], up[:, fc * P:(fc + 1) * P],
                                                           func, bias=cols[:, bass.ds(c, 1)])
                            ins.then_inc(done, 1)

                lot(0)
                if nu // SLOTS == 2:
                    lot(1)
                else:
                    with act.Fori(1, nu // SLOTS) as it:
                        lot(it)

            def context16(i, shares):
                for j in shares:
                    act.wait_ge(S.c_psum, 16 * i + j + 1)
                    src = halves[1 + 4 * (j % 2)]
                    if j < 8:
                        c, kb = j // 4, j % 4
                        nc.scalar.activation(n16.kt[:, c, kb * 512:(kb + 1) * 512], src, ACT.Identity,
                                             bias=col(("l1x_bk", "l3x_bk")[i], c)).then_inc(S.c_act, 1)
                    else:
                        jj = j - 8
                        nc.scalar.copy(n16.v[:, 2 * jj:2 * jj + 2, :], src.rearrange("p (a d) -> p a d", a=2))\
                            .then_inc(S.c_act, 1)

            act.wait_ge(S.in_cols, 16)
            def keys_values(i):
                act.wait_ge(S.kv_psum, i + 1)
                j, src = L0X_ORDER[i], halves[2 + i % 2]
                nc.scalar.copy(q.knat[:, j, :], src[:, 0:D]).then_inc(S.kv_k, 1)
                nc.scalar.copy(q.v[:, j, :], src[:, D:2 * D]).then_inc(S.kv_v, 1)

            def rows_t(g):
                act.wait_ge(S.xn_psum, g + 1)
                nc.scalar.activation(xnt[0:CB, 1, g * 512:(g + 1) * 512], halves[1][0:CB, :], ACT.Identity,
                                     bias=col("l0x_xb", 1)[0:CB], scale=col("l0x_xg", 1)[0:CB]).then_inc(S.xn_act, 1)

            rows_t(0)
            keys_values(0)
            for g in range(1, KT // 4):
                rows_t(g)
                for i in range(4 * g - 3, 4 * g + 1):
                    keys_values(i)
            for i in range(KT - 3, KT + 1):
                keys_values(i)
            for g in range(1, 9, 2):
                act.wait_ge(S.kt_psum, g + 1)
                first, n = L0X_GROUPS[g]
                nc.scalar.copy(q.kt[:, :, first * P:(first + n) * P],
                               halves[4 + g % 2].rearrange("p (c k) -> p c k", c=C)).then_inc(S.kt_act, 1)
            attention("l0x", 4, lambda t: q.sc[:, t % 2, :], None, lambda t: q.sc[:, t % 2, :],
                      lambda t: q.pt[:, t % 2, :])
            if stages > 1:
                context16(0, range(0, 7))
                act.wait_ge(S.sa_max, 1)
                nc.scalar.activation(r0.p, r0.p, ACT.Exp).then_inc(S.sa_exp, 1)
                context16(0, range(7, 16))
            if stages > 2:
                mixture(0)

            def scores(t):
                return ps01[:] if t % 2 == 0 else ps23[:]

            if stages > 3:
                attention("l1x", 16, scores, None, lambda t: n16.p[:, t % 2, :], lambda t: n16.pt[:, t % 2, :])
            if stages > 4:
                act.wait_ge(S.conv_max, 1)
                nc.scalar.activation(cv.w, cv.w, ACT.Exp, bias=cv.mx, accum_out=cv.sum).then_inc(S.conv_exp, 1)
            if stages > 5:
                mixture(1)
            if stages > 6:
                for hh in range(2):
                    act.wait_ge(S.h1_psum, hh + 1)
                    for b in range(B):
                        src = ps45[0:CB, :].rearrange("p (a h b q) -> p a h b q", a=2, b=B, q=LQ)[:, :, :, b, :]
                        dst = n64.qb[0:CB, b, 8 * hh:8 * hh + 8, :].rearrange("p (h a) q -> p a h q", a=2)
                        nc.scalar.copy(dst, src).then_inc(S.h1_act, 1)
                attention("l2x", 16, scores, None, lambda t: n64.p[:, t % 2, :], lambda t: n64.pt[:, t % 2, :])
            if stages > 7:
                for s in range(2):
                    act.wait_ge(S.t_a, s + 1)
                    nc.scalar.activation(tt.s, ps01[:].rearrange("p (f k) -> p f k", f=8), ACT.Sigmoid)\
                        .then_inc(S.t_sig, 1)
                    act.wait_ge(S.t_back, 3 * s + 1)
                    nc.scalar.copy(tt.hn[:, s], ps45[:].rearrange("p (f k) -> p f k", f=8)).then_inc(S.t_backc, 1)
                    act.wait_ge(S.t_back, 3 * s + 2)
                    nc.scalar.copy(tt.dan[:, s], ps23[:].rearrange("p (f k) -> p f k", f=8)).then_inc(S.t_backc, 1)
                    act.wait_ge(S.t_back, 3 * s + 3)
                    nc.scalar.copy(tt.dbn[s], ps45[:].rearrange("p (f k) -> p f k", f=8)).then_inc(S.t_backc, 1)
                    n1 = 3 * NS_ITERS * s + 1
                    for c in range(3):
                        act.wait_ge(S.n_e, n1 + c)
                        nc.scalar.copy(tt.e[c], halves[c][:, 2 * P:4 * P].rearrange("p (a k) -> p a k", a=2))\
                            .then_inc(S.n_ec, 1)
                    for c in range(3):
                        act.wait_ge(S.n_m1, 3 * s + 1 + c)
                        nc.scalar.activation(tt.m[s][c], tt.m[s][c], ACT.Identity, scale=tt.rn[:, c:c + 1])\
                            .then_inc(S.n_mc, 1)
                    with act.Fori(0, NS_ITERS - 1) as it:
                        n0 = 3 * (NS_ITERS - 1) * s + 1
                        for c in range(3):
                            act.wait_ge(S.n_u, n0 + c + it * 3)
                            nc.scalar.copy(tt.u[c], halves[c][:, 0:P]).then_inc(S.n_uc, 1)
                        for c in range(3):
                            act.wait_ge(S.n_w, n0 + c + it * 3)
                            nc.scalar.copy(tt.wm[c], halves[c][:, P:2 * P]).then_inc(S.n_wc, 1)
                        for c in range(3):
                            act.wait_ge(S.n_e, n1 + 3 + c + it * 3)
                            nc.scalar.copy(tt.e[c], halves[c][:, 2 * P:4 * P].rearrange("p (a k) -> p a k", a=2))\
                                .then_inc(S.n_ec, 1)
                act.wait_ge(S.t_a, 3)
                nc.scalar.activation(tt.s, ps01[:].rearrange("p (f k) -> p f k", f=8), ACT.Sigmoid).then_inc(S.t_sig, 1)
            if stages > 8:
                context16(1, range(0, 3))
                mixture(2)
                context16(1, range(3, 16))
            if stages > 9:
                attention("l3x", 16, scores, None, lambda t: n16.p[:, t % 2, :], lambda t: n16.pt[:, t % 2, :])
                for f in range(4):
                    act.wait_ge(S.m_h, 1)
                    ins = nc.scalar.activation(n16.h[:, f, :], halves[0][:, f * P:(f + 1) * P], ACT.Relu,
                                               bias=col("l3x_b1", f))
                ins.then_inc(S.m_hc, 1)
            if stages > 10:
                for c in range(C):
                    act.wait_ge(S.g_psum, 1)
                    ins = nc.scalar.activation(gr.z[:, c, :], ps01[:, c * P:(c + 1) * P], ACT.Sigmoid,
                                               bias=col("l3a_bz", c))
                ins.then_inc(S.g_z, 1)
            if stages > 11:
                mixture(3)

        def ttt(dve, own, bc, inverse_sqrt):
            eight = lambda t: t.rearrange("p (f k) -> p f k", f=8)
            dve.wait_ge(S.t_qkv, 1)
            dve.wait_ge(S.in_late, 16)
            lt = lambda name: late[:, LATE[name][0]:LATE[name][0] + LATE[name][1]]
            flat = tt.qkv.rearrange("p a d -> p (a d)")
            own(nc.vector.tensor_tensor(flat, ps01[:, 0:3 * D], lt("qkvb"), ALU.add))
            own.wait()
            qk, sq = flat[:, 0:2 * D], tt.w.rearrange("p f k -> p (f k)")[:, 0:2 * D]
            own(nc.vector.tensor_tensor(sq, qk, qk, ALU.mult))
            own.wait()
            own(nc.vector.tensor_reduce(tt.ss, sq.rearrange("p (h d) -> p h d", d=16), AX.X, ALU.add))
            own.wait()
            own(nc.vector.tensor_scalar(tt.sc, tt.ss, 1e-30, None, ALU.max))
            own.wait()
            inverse_sqrt(tt.nr, tt.sc, tt.nt)
            own(nc.vector.tensor_tensor(tt.nr, tt.nr, tt.ss, ALU.mult))
            own.wait()
            own(nc.vector.tensor_scalar(tt.nr, tt.nr, 1e-6, None, ALU.add))
            own.wait()
            own(nc.vector.reciprocal(tt.nr, tt.nr))
            own.wait()
            qk3 = qk.rearrange("p (h d) -> p h d", d=16)
            own(nc.vector.tensor_tensor(qk3, qk3, bc(tt.nr, 16), ALU.mult))
            own.wait()
            for i, (g, b) in enumerate((("qs", "qb"), ("ks", "kb"))):
                half = tt.qkv[:, i, :].rearrange("p (h d) -> p h d", d=16)
                own(nc.vector.tensor_tensor(half, half, lt(g).unsqueeze(1).broadcast_to([P, 16, 16]), ALU.mult))
                own.wait()
                nc.vector.tensor_tensor(half, half, lt(b).unsqueeze(1).broadcast_to([P, 16, 16]), ALU.add)\
                    .then_inc(S.t_qk, 1)
            dve.wait_ge(S.t_kqt, 1)
            nc.vector.tensor_copy(tt.kqt, ps6[:, 0:512].rearrange("p (a c k) -> p a c k", a=2, c=C)).then_inc(S.t_kqtc, 1)
            dve.wait_ge(S.t_gram, 1)
            nc.vector.tensor_copy(tt.gram, ps7[:, 0:2 * P].rearrange("p (a k) -> p a k", a=2)).then_inc(S.t_gramc, 1)
            own(nc.vector.tensor_scalar(tt.ai, ident, NS_A, None, ALU.mult))
            a8, b8, w8 = eight(ps01[:]), eight(ps23[:]), tt.w
            for s in range(2):
                dve.wait_ge(S.t_sig, s + 1)
                own(nc.vector.tensor_tensor(tt.g, tt.s, a8, ALU.mult))
                own.wait()
                dve.wait_ge(S.t_b, s + 1)
                nc.vector.tensor_tensor(tt.h[:, s], tt.g, b8, ALU.mult).then_inc(S.t_h, 1)
                own(nc.vector.scalar_tensor_tensor(w8, tt.g, 1.0, tt.s, ALU.subtract, ALU.mult))
                own.wait()
                own(nc.vector.tensor_tensor(tt.tb, tt.g, w8, ALU.subtract))
                own.wait()
                own(nc.vector.tensor_tensor(tt.tb, tt.tb, b8, ALU.mult))
                if s == 1:
                    dve.wait_ge(S.t_x, 1)
                    nc.vector.tensor_copy(tt.tmp[:, 2], ps7[:, 0:P]).then_inc(S.t_xc, 1)
                    dve.wait_ge(S.t_z, 1)
                    nc.vector.tensor_scalar(tt.tmp[:, 3], ps7[:, P:2 * P], -LR, None, ALU.mult).then_inc(S.t_zc, 1)
                dve.wait_ge(S.t_pred, s + 1)
                own(nc.vector.tensor_tensor(tt.en[:, s], ps6[:, 0:D], tt.qkv[:, 2, :], ALU.subtract))
                own.wait()
                nc.vector.tensor_scalar(tt.en[:, s], tt.en[:, s], 2.0 / (P * D), None, ALU.mult).then_inc(S.t_e, 1)
                dve.wait_ge(S.t_et, s + 1)
                nc.vector.tensor_copy(tt.et[:, s], ps6[:, D:2 * D].rearrange("p (c k) -> p c k", c=C)).then_inc(S.t_etc, 1)
                if s == 1:
                    dve.wait_ge(S.t_x, 2)
                    nc.vector.tensor_copy(tt.tmp[:, 4], ps7[:, 0:P]).then_inc(S.t_xc, 1)
                    dve.wait_ge(S.t_z, 2)
                    nc.vector.tensor_scalar(tt.tmp[:, 5], ps7[:, P:2 * P], -LR, None, ALU.mult).then_inc(S.t_zc, 1)
                dve.wait_ge(S.t_sh, s + 1)
                own(nc.vector.tensor_copy(tt.sh, ps7[:, 2 * P:4 * P].rearrange("p (a k) -> p a k", a=2)))
                dve.wait_ge(S.t_dh, s + 1)
                own.wait()
                own(nc.vector.tensor_tensor(tt.tb, tt.tb, a8, ALU.mult))
                nc.vector.tensor_tensor(tt.w, tt.g, a8, ALU.mult).then_inc(S.t_da, 1)
                dve.wait_ge(S.t_s, s + 1)
                own(nc.vector.tensor_copy(tt.sgv, ps6[:, 0:2 * P].rearrange("p (a k) -> p a k", a=2)))
                own.wait()
                for c, (sc, cc) in enumerate(((tt.sgv[:, 0], tt.gram[:, 0]), (tt.sgv[:, 1], tt.gram[:, 0]),
                                              (tt.sh[:, 0], tt.sh[:, 1]))):
                    ins = nc.vector.tensor_tensor_reduce(tt.tmp[:, c], sc, cc, 1.0, 0.0, ALU.mult, ALU.add,
                                                         tt.tr[:, c:c + 1])
                ins.then_inc(S.t_tr, 1)
                dve.wait_ge(S.t_trp, s + 1)
                nc.vector.tensor_copy(tt.n2, ps7[:, 0:3]).then_inc(S.t_nrm, 1)
                dve.wait_ge(S.t_nrmp, s + 1)
                own(nc.vector.tensor_scalar(tt.n, tt.n, 1e-7, None, ALU.add))
                own.wait()
                own(nc.vector.reciprocal(tt.rn, tt.n))
                own.wait()
                own(nc.vector.tensor_tensor(tt.rn2, tt.rn, tt.rn, ALU.mult))
                own.wait()
                for c in range(3):
                    nc.vector.tensor_scalar(tt.wm[c], (tt.sgv[:, 0], tt.sgv[:, 1], tt.sh[:, 0])[c], tt.rn2[:, c:c + 1],
                                            None, ALU.mult).then_inc(S.n_wc, 1)
                n1 = 3 * NS_ITERS * s + 1
                for c in range(3):
                    dve.wait_ge(S.n_ec, n1 + c)
                    nc.vector.scalar_tensor_tensor(tt.tmp[:, 2 * c:2 * c + 2], tt.e[c], NS_B,
                                                   tt.ai.unsqueeze(1).broadcast_to([P, 2, P]), ALU.mult, ALU.add)\
                        .then_inc(S.n_ba, 1)
                for c in range(3):
                    dve.wait_ge(S.n_p, n1 + c)
                    dve.wait_ge(S.n_ba, n1 + c)
                    nc.vector.scalar_tensor_tensor(tt.m[s][c], halves[3 + c][:, 0:2 * P].rearrange("p (a k) -> p a k", a=2),
                                                   NS_C, tt.tmp[:, 2 * c:2 * c + 2], ALU.mult, ALU.add).then_inc(S.n_m1, 1)
                with dve.Fori(0, NS_ITERS - 1) as it:
                    n0 = 3 * (NS_ITERS - 1) * s + 1
                    for c in range(3):
                        dve.wait_ge(S.n_ec, n1 + 3 + c + it * 3)
                        nc.vector.scalar_tensor_tensor(tt.u[c], tt.e[c][:, 1], NS_B, tt.ai, ALU.mult, ALU.add)\
                            .then_inc(S.n_ba, 1)
                    for c in range(3):
                        dve.wait_ge(S.n_p, n1 + 3 + c + it * 3)
                        dve.wait_ge(S.n_ba, n1 + 3 + c + it * 3)
                        nc.vector.scalar_tensor_tensor(tt.pt[c], halves[3 + c][:, 0:P], NS_C, tt.u[c],
                                                       ALU.mult, ALU.add).then_inc(S.n_pc, 1)
                    for c in range(3):
                        dve.wait_ge(S.n_m, n0 + c + it * 3)
                        nc.vector.tensor_copy(tt.m[s][c], halves[3 + c][:, P:3 * P].rearrange("p (a k) -> p a k", a=2))\
                            .then_inc(S.n_mc, 1)
                if s == 0:
                    dve.wait_ge(S.t_r, 1)
                    nc.vector.tensor_scalar(tt.tmp[:, 0:2], ps6[:, 0:2 * P].rearrange("p (a k) -> p a k", a=2), -LR, None,
                                            ALU.mult).then_inc(S.t_rc, 1)
                else:
                    dve.wait_ge(S.t_r, 2)
                    nc.vector.tensor_scalar(tt.tmp[:, 0:4], ps6[:, 0:4 * P].rearrange("p (a k) -> p a k", a=4), -LR, None,
                                            ALU.mult).then_inc(S.t_rc, 1)
            dve.wait_ge(S.t_sig, 3)
            own(nc.vector.tensor_tensor(tt.g, tt.s, a8, ALU.mult))
            own.wait()
            dve.wait_ge(S.t_b, 3)
            nc.vector.tensor_tensor(tt.tb, tt.g, b8, ALU.mult).then_inc(S.t_h, 1)
            dve.wait_ge(S.t_x, 3)
            nc.vector.tensor_copy(tt.tmp[:, 4:6], ps7[:, 0:2 * P].rearrange("p (a k) -> p a k", a=2)).then_inc(S.t_xc, 1)
            dve.wait_ge(S.t_z, 3)
            nc.vector.tensor_scalar(tt.tmp[:, 0:2], ps7[:, 2 * P:4 * P].rearrange("p (a k) -> p a k", a=2), -LR, None,
                                    ALU.mult).then_inc(S.t_zc, 1)
            dve.wait_ge(S.t_o, 1)
            nc.vector.tensor_copy(tt.et[:, 0], ps45[:, 0:D].rearrange("p (c k) -> p c k", c=C)).then_inc(S.t_oc, 1)

        @block.vector
        def _(dve):
            own = Own(dve, S.dve_own)

            def bc(ap, n):
                return ap.unsqueeze(2).broadcast_to([P, ap.shape[1], n])

            def inverse_sqrt(y, v, t):
                own(nc.vector.tensor_scalar(t.bitcast(I32), v.bitcast(I32), 1, None, ALU.logical_shift_right))
                own.wait()
                own(nc.vector.tensor_scalar(y.bitcast(I32), t.bitcast(I32), -1, 0x5f3759df, ALU.mult, ALU.add))
                own.wait()
                for _ in range(3):
                    own(nc.vector.tensor_tensor(t, y, y, ALU.mult))
                    own.wait()
                    own(nc.vector.scalar_tensor_tensor(t, t, -0.5, v, ALU.mult, ALU.mult))
                    own.wait()
                    own(nc.vector.scalar_tensor_tensor(y, t, 1.5, y, ALU.add, ALU.mult))
                    own.wait()

            def norm(n, src, dst):
                own(nc.vector.bn_stats(stat, src))
                own.wait()
                own(nc.vector.bn_aggr(mv, stat))
                own.wait()
                nc.vector.tensor_scalar(ve, mv[:, 1:2], LN_EPS, None, ALU.add).then_inc(S.ln_var, 1)
                dve.wait_ge(S.ln_rstd, n + 1)
                nc.vector.tensor_scalar(dst, src, mv[:, 0:1], rstd, ALU.subtract, ALU.mult).then_inc(S.xh_ready, 1)
                dve.wait_ge(S.xh_ready, n + 1)

            def tokens_t(stage, gain=None, bias=None):
                dve.wait_ge(S.xt_psum, stage + 1)
                if gain is None:
                    nc.vector.tensor_copy(xt[:], ps7[:, 0:D].rearrange("p (c k) -> p c k", c=C)).then_inc(S.xt_ready, 1)
                else:
                    own(nc.vector.tensor_scalar(xt[:, 0, :], ps7[:, 0:P], col(gain, 0), col(bias, 0), ALU.mult, ALU.add))
                    own.wait()
                    nc.vector.tensor_scalar(xt[:, 1, :], ps7[:, P:D], col(gain, 1), col(bias, 1), ALU.mult, ALU.add)\
                        .then_inc(S.xt_ready, 1)

            def residual(k, src, bias):
                if k == 1:
                    dve.wait_ge(S.in_rows, 16)
                own(nc.vector.tensor_tensor(x[:], x[:], row(bias), ALU.add))
                own.wait()
                dve.wait_ge(S.out_psum, k)
                own(nc.vector.tensor_tensor(x[:], x[:], src, ALU.add))
                own.wait()

            def attention(stage, n, take_max, pt_of, o_of, width, post=None):
                base = ATT_BASE[stage]
                for t in range(n + 2 + (post is not None)):
                    if t < n:
                        take_max(t)
                    if 1 <= t <= n:
                        u = t - 1
                        dve.wait_ge(S.att_exp, base + t)
                        if u >= 2:
                            dve.wait_ge(S.att_on, base + u - 1)
                        own(nc.vector.reciprocal(att.rinv[:, u % 2:u % 2 + 1], att.rsum[:, u % 2:u % 2 + 1]))
                        own.wait()
                        dve.wait_ge(S.att_pt, base + t)
                        if t >= 3:
                            dve.wait_ge(S.att_o, base + t - 2)
                        if stage == "l0x":
                            nc.vector.tensor_copy(pt_of(u)[:, 1024:1152], halves[3][:, 0:P])
                        nc.vector.tensor_copy(pt_of(u)[:, 512:1024], ps45[:, 512:1024]).then_inc(S.att_ptd, 1)
                    if post is not None and 3 <= t:
                        u = t - 3
                        dve.wait_ge(S.opt_psum, OPT_BASE[stage] + u + 1)
                        post(u).then_inc(S.opt_ready, 1)
                    if 2 <= t < n + 2:
                        u = t - 2
                        dve.wait_ge(S.att_o, base + t - 1)
                        nc.vector.tensor_scalar(o_of(u), ps6[:, 0:width],
                                                att.rinv[:, u % 2:u % 2 + 1], None, ALU.mult).then_inc(S.att_on, 1)

            def plain_max(base, scores):
                def take(t):
                    dve.wait_ge(S.att_s, base + t + 1)
                    nc.vector.tensor_reduce(att.nmax[:, t % 2:t % 2 + 1], scores(t), AX.X, ALU.max, negate=True)\
                        .then_inc(S.att_max, 1)
                return take

            def mixture(m):
                base, nu = MOE_BASE[m], MOE_UNITS[m]
                dve.wait_ge(S.router_psum, m + 1)
                if m == 3:
                    own(nc.vector.tensor_tensor(mo.lg, ps7[:, 256:264], row("l3f_bg"), ALU.add))
                else:
                    own(nc.vector.tensor_copy(mo.lg, ps7[:, 256:264]))
                own.wait()
                own(nc.vector.max(mo.top, mo.lg))
                own.wait()
                own(nc.vector.max_index(mo.idx, mo.top, mo.lg))
                nc.vector.tensor_scalar(mo.gap, mo.top[:, 0:2], mo.top[:, 0:1], None, ALU.subtract).then_inc(S.top_gap, 1)
                own.wait()
                own(nc.vector.tensor_copy(mo.idxf, mo.idx))
                dve.wait_ge(S.top_exp, m + 1)
                own(nc.vector.reciprocal(mo.rz, mo.z))
                own.wait()
                own(nc.vector.tensor_scalar(mo.wt, mo.ex, mo.rz, None, ALU.mult))
                own.wait()
                own(nc.vector.tensor_scalar(mo.c0, iota8, mo.idxf[:, 0:1], mo.wt[:, 0:1], ALU.is_equal, ALU.mult))
                own(nc.vector.tensor_scalar(mo.c1, iota8, mo.idxf[:, 1:2], mo.wt[:, 1:2], ALU.is_equal, ALU.mult))
                own.wait()
                nc.vector.tensor_tensor(mo.comb, mo.c0, mo.c1, ALU.add).then_inc(S.comb_ready, 1)
                dve.wait_ge(S.comb_ready, m + 1)

                def add_unit(k_mod, prev_s, it, acc_value):
                    e = prev_s // (nu // E) + it * (SLOTS // (nu // E))
                    dve.wait_ge(S.moe_y, acc_value)
                    if not (isinstance(acc_value, int) and acc_value == 1):
                        dve.wait_ge(S.moe_acc, acc_value - 1)
                    nc.vector.scalar_tensor_tensor(x[:], halves[4 + k_mod][:, 0:D], mo.comb[:, bass.ds(e, 1)], x[:],
                                                   ALU.mult, ALU.add).then_inc(S.moe_acc, 1)

                def lot(it):
                    for s in range(SLOTS):
                        first = isinstance(it, int) and it == 0
                        par = s % 2
                        if m >= 2:
                            dve.wait_ge(S.moe_g, (0, 0, 0, 8)[m] + s + 1 + it * SLOTS)
                            if not (first and s < 2):
                                dve.wait_ge(S.moe_y, base + s - 1 + it * SLOTS)
                            up = halves[2 + par]
                            if m == 2:
                                nc.vector.tensor_tensor(mo.h[:, par, :], mo.g[:, par, :], up, ALU.mult)\
                                    .then_inc(S.moe_h, 1)
                            else:
                                for fc in range(FC):
                                    c = COLS["l3f_b0"][0] + fc + s * FC + it * (SLOTS * FC)
                                    f = slice(fc * P, (fc + 1) * P)
                                    ins = nc.vector.scalar_tensor_tensor(
                                        mo.h[:, par, f], up[:, f], cols[:, bass.ds(c, 1)], mo.g[:, par, f],
                                        ALU.add, ALU.mult)
                                ins.then_inc(S.moe_h, 1)
                        if not (first and s == 0):
                            prev = (s - 1) % SLOTS
                            add_unit(1 - par, prev, it if s else it - 1, base + s + it * SLOTS)

                lot(0)
                if m in (1, 3):
                    dve.wait_ge(S.combt_psum, m // 2 + 1)
                    nc.vector.tensor_copy(mo.combt[0:E, :], ps7[0:E, 264:264 + P]).then_inc(S.combt_ready, 1)
                    dve.wait_ge(S.b2_psum, m // 2 + 1)
                    dve.wait_ge(S.moe_acc, base + SLOTS - 1)
                    own(nc.vector.tensor_tensor(x[:], x[:], ps7[:, 0:D], ALU.add))
                    own.wait()
                if nu // SLOTS == 2:
                    lot(1)
                else:
                    with dve.Fori(1, nu // SLOTS) as it:
                        lot(it)
                add_unit(1, SLOTS - 1, nu // SLOTS - 1, base + nu)
                dve.wait_ge(S.moe_acc, base + nu)

            dve.wait_ge(S.in_x, 16)
            norm(0, x[:], xh[:])
            norm(1, xh[:], xh[:])
            dve.wait_ge(S.in_cols, 16)
            tokens_t(0, "l0x_lg", "l0x_lb")
            own(nc.vector.tensor_tensor(gain, col("l0x_qg"), col("l0x_kg"), ALU.mult))
            own(nc.vector.memset(q.qbd, 0.0))
            dve.wait_ge(S.in_ctx, 16)

            def row_stats(g):
                for j in range(4 * g, 4 * g + 4):
                    own(nc.vector.bn_stats(q.stats[:, j, :], ctxn[:, j * CD:(j + 1) * CD]))
                own.wait()
                for j in range(4 * g, 4 * g + 4):
                    own(nc.vector.bn_aggr(q.mv[:, j, :], q.stats[:, j, :]))
                own.wait()
                nc.vector.tensor_scalar(q.cve[:, 4 * g:4 * g + 4], q.mv[:, 4 * g:4 * g + 4, 1], LN_EPS, None, ALU.add)\
                    .then_inc(S.cln_var, 1)

            def norm_rows(g):
                dve.wait_ge(S.cln_rstd, g + 1)
                if g >= 2:
                    dve.wait_ge(S.xn_psum, g - 1)
                for j in range(4 * g, 4 * g + 4):
                    nc.vector.tensor_scalar(q.xn[:, j % 8, :], ctxn[:, j * CD:(j + 1) * CD], q.mv[:, j, 0:1],
                                            q.crs[:, j:j + 1], ALU.subtract, ALU.mult).then_inc(S.xn_ready, 1)

            def rows_t(g):
                dve.wait_ge(S.xn_psum, g + 1)
                nc.vector.tensor_scalar(xnt[:, 0, g * 512:(g + 1) * 512], halves[0], col("l0x_xg"), col("l0x_xb"),
                                        ALU.mult, ALU.add).then_inc(S.xn_dve, 1)

            def key_squares(places):
                for i in places:
                    dve.wait_ge(S.kv_sq, i + 1)
                    nc.vector.tensor_reduce(q.ss[:, 4 * i + 4:4 * i + 8], q.sq[:, i % 2, :].rearrange("p (h d) -> p h d", h=4),
                                            AX.X, ALU.add).then_inc(S.kv_ss, 1)

            def norm_keys(k, places):
                dve.wait_ge(S.kv_ss, places[-1] + 1)
                own(nc.vector.tensor_scalar(q.ss[:, k], q.ss[:, k], 1.0 / 64, 1e-16, ALU.mult, ALU.max))
                own.wait()
                inverse_sqrt(q.rs[:, k], q.ss[:, k], q.rt[:, k])
                if places[0] == 0:
                    nc.vector.tensor_tensor(xh[:].rearrange("p (h d) -> p h d", h=4), xh[:].rearrange("p (h d) -> p h d", h=4),
                                            bc(q.rs[:, 0:4], 64), ALU.mult).then_inc(S.q_norm, 1)
                for i in places:
                    kn = q.knat[:, L0X_ORDER[i], :].rearrange("p (h d) -> p h d", h=4)
                    nc.vector.tensor_tensor(kn, kn, bc(q.rs[:, 4 * i + 4:4 * i + 8], 64), ALU.mult).then_inc(S.khat_ready, 1)

            row_stats(0)
            row_stats(1)
            norm_rows(0)
            row_stats(2)
            norm_rows(1)
            row_stats(3)
            rows_t(0)
            norm_rows(2)
            rows_t(1)
            norm_rows(3)
            dve.wait_ge(S.q_psum, 1)
            own(nc.vector.tensor_copy(xh[:], ps6[:, 0:D]))
            own.wait()
            own(nc.vector.tensor_tensor(q.kt[:, 0, 0:D], xh[:], xh[:], ALU.mult))
            own.wait()
            own(nc.vector.tensor_reduce(q.ss[:, 0:4], q.kt[:, 0, 0:D].rearrange("p (h d) -> p h d", h=4), AX.X, ALU.add))
            own.wait()
            key_squares(range(0, 3))
            rows_t(2)
            dve.wait_ge(S.in_mask, 16)
            own(nc.vector.tensor_scalar(q.mask[:, :, 0:KEYS], q.mask8.rearrange("p (b k) -> p b k", b=B),
                                        -MASKED, MASKED, ALU.mult, ALU.add))
            own(nc.vector.memset(q.mask[:, :, KEYS:NK], MASKED))
            own.wait()
            for b in range(B):
                own(nc.vector.memset(q.mask[:, b, KEYS + b * LQ:KEYS + (b + 1) * LQ], 0.0))
            key_squares(range(3, 7))
            rows_t(3)
            key_squares(range(7, 11))
            norm_keys(slice(0, 48), range(0, 11))
            key_squares(range(11, KT + 1))
            norm_keys(slice(48, 72), range(11, KT + 1))
            dve.wait_ge(S.qt_psum, 1)
            src = ps6[:, 256:512].rearrange("p (c b k) -> p b c k", c=C, b=B)
            for i in range(2):
                for b in range(B):
                    h = slice(64 * i, 64 * i + 64)
                    ins = nc.vector.tensor_scalar(q.qbd[h, b, :, 64 * i:64 * i + 64], src[h, b], gain[h],
                                                  64 ** -0.5, ALU.mult, ALU.mult)
            ins.then_inc(S.qbd_ready, 1)
            for g in range(0, 9, 2):
                dve.wait_ge(S.kt_psum, g + 1)
                first, n = L0X_GROUPS[g]
                nc.vector.tensor_copy(q.kt[:, :, first * P:(first + n) * P],
                                      halves[4 + g % 2][:, 0:2 * n * P].rearrange("p (c k) -> p c k", c=C))\
                    .then_inc(S.kt_dve, 1)

            def masked_max(t):
                dve.wait_ge(S.att_s, t + 1)
                if t >= 2:
                    dve.wait_ge(S.att_pt, t - 1)
                if t >= 1:
                    dve.wait_ge(S.att_max, t)
                b = t // 2
                own(nc.vector.tensor_tensor_reduce(q.sc[:, t % 2, 0:KEYS], ps01[:], q.mask[:, b, 0:KEYS],
                                                   1.0, NEG, ALU.add, ALU.max, att.mx[:, 0:1]))
                own(nc.vector.tensor_tensor_reduce(q.sc[:, t % 2, KEYS:NK], halves[2][:, 0:P],
                                                   q.mask[:, b, KEYS:NK], 1.0, NEG, ALU.add, ALU.max, att.mx[:, 1:2]))
                own.wait()
                nc.vector.tensor_reduce(att.nmax[:, t % 2:t % 2 + 1], att.mx, AX.X, ALU.max, negate=True)\
                    .then_inc(S.att_max, 1)

            def heads_back(u):
                b, hp = u // 2, u % 2
                for j in range(2):
                    h = slice(64 * j, 64 * j + 64)
                    ins = nc.vector.tensor_copy(xt[h, hp, b * LQ:(b + 1) * LQ], ps7[h, 64 * j:64 * j + 64])
                return ins

            attention("l0x", 4, masked_max, lambda t: q.pt[:, t % 2, :],
                      lambda t: xh[:, (t % 2) * P:(t % 2) * P + P], P, heads_back)
            residual(1, ps6[:, 0:D], "l0x_bo")
            if stages > 1:
                norm(2, x[:], xh[:])
                norm(3, xh[:], xh[:])
                tokens_t(1, "l0a_w", "l0a_b")
                own(nc.vector.memset(r0.qbd, 0.0))
                dve.wait_ge(S.sa_qkv, 1)
                own.wait()
                own(nc.vector.tensor_copy(r0.kt, ps23[:, 0:P]))
                own(nc.vector.tensor_copy(r0.v, ps23[:, P:P + 64]))
                src = ps01[:, 0:512].rearrange("p (h b k) -> p h b k", h=4, b=B)
                for i in range(2):
                    for b in range(B):
                        h = slice(64 * i, 64 * i + 64)
                        ins = nc.vector.tensor_scalar(r0.qbd[h, b, :, 64 * i:64 * i + 64], src[h, :, b, :], 64 ** -0.5,
                                                      None, ALU.mult)
                ins.then_inc(S.sa_q, 1)
                dve.wait_ge(S.sa_s, 1)
                s8 = ps45[:, 0:512].rearrange("p (a k) -> p a k", a=8)
                p8 = r0.p.rearrange("p h b k -> p (h b) k")
                own(nc.vector.tensor_reduce(r0.mx, s8, AX.X, ALU.max))
                own.wait()
                nc.vector.tensor_tensor(p8, s8, bc(r0.mx, LQ), ALU.subtract).then_inc(S.sa_max, 1)
                dve.wait_ge(S.sa_exp, 1)
                own(nc.vector.tensor_reduce(r0.sum, p8, AX.X, ALU.add))
                own.wait()
                own(nc.vector.reciprocal(r0.rinv, r0.sum))
                own.wait()
                nc.vector.tensor_tensor(p8, p8, bc(r0.rinv, LQ), ALU.mult).then_inc(S.sa_norm, 1)
                dve.wait_ge(S.sa_pt, 1)
                nc.vector.tensor_copy(r0.pt, ps01[:, 0:512].rearrange("p (h k) -> p h k", h=4)).then_inc(S.sa_ptc, 1)
                dve.wait_ge(S.sa_ot, 1)
                for b in range(B):
                    ins = nc.vector.tensor_copy(r0.ot[:, :, b * LQ:(b + 1) * LQ],
                                                halves[2 + b][:, 0:D].rearrange("p (h k) -> p h k", h=4))
                ins.then_inc(S.sa_otc, 1)
                dve.wait_ge(S.out_psum, 2)
                own(nc.vector.tensor_copy(r0.o, ps6[:, 0:D]))
                own.wait()
                norm(4, r0.o, r0.o)
                own(nc.vector.tensor_tensor(r0.o, r0.o, row("l0a_ow"), ALU.mult))
                own.wait()
                own(nc.vector.tensor_tensor(r0.o, r0.o, row("l0a_ob"), ALU.add))
                own.wait()
                own(nc.vector.tensor_tensor(x[:], x[:], r0.o, ALU.add))
                own.wait()
            if stages > 2:
                norm(5, x[:], xh[:])
                tokens_t(2)
                mixture(0)

            def cross16(i, stage, bq, bv):
                dve.wait_ge(S.q16_psum, i + 1)
                for c in range(C):
                    own(nc.vector.tensor_scalar(n16.qt[:, c, :], ps6[:, c * P:(c + 1) * P], col(bq, c), 0.25,
                                                ALU.add, ALU.mult))
                own.wait()
                for j in range(8):
                    ins = nc.vector.tensor_scalar(n16.qbd[:, :, :, j, :], n16.qt.rearrange("p c (b k) -> p c b k", b=B),
                                                  head8[:, j:j + 1], None, ALU.mult)
                ins.then_inc(S.q16_ready, 1)
                base = ATT_BASE[stage]

                def o_of(u):
                    cb, g = u // 4, u % 4
                    return n16.o[:, cb // 2, cb % 2, 32 * g:32 * g + 32]

                attention(stage, 16, plain_max(base, lambda t: (ps01, ps23)[t % 2][:]), lambda t: n16.pt[:, t % 2, :],
                          o_of, 32)
                dve.wait_ge(S.o16_psum, i + 1)
                src = ps6[:, 0:512].rearrange("p (c b j k) -> p c b j k", c=C, b=B, j=2)
                ot = n16.ot.rearrange("p c (b k) -> p c b k", b=B)
                tmp = n16.tmp.rearrange("p c (b k) -> p c b k", b=B)
                for c in range(C):
                    own(nc.vector.tensor_scalar(tmp[:, c], src[:, c, :, 0, :], parity[:, 0:1], col(bv, c),
                                                ALU.mult, ALU.add))
                own.wait()
                for c in range(C):
                    ins = nc.vector.scalar_tensor_tensor(ot[:, c], src[:, c, :, 1, :], parity[:, 1:2], tmp[:, c],
                                                         ALU.mult, ALU.add)
                ins.then_inc(S.o16_ready, 1)

            if stages > 3:
                norm(6, x[:], xh[:])
                tokens_t(3)
                cross16(0, "l1x", "l1x_bq", "l1x_bv")
                residual(3, ps6[:, 0:D], "l1x_bo")
            if stages > 4:
                norm(7, x[:], xh[:])
                tokens_t(4)
                own(nc.vector.memset(cv.a, 0.0))
                own(nc.vector.memset(cv.full, 0.0))
                own(nc.vector.tensor_scalar(cv.nb, bits, -1.0, 1.0, ALU.mult, ALU.add))
                dve.wait_ge(S.conv_s, 1)
                own(nc.vector.tensor_tensor(cv.w, ps6[:, 0:32], row("l1a_b"), ALU.add))
                own.wait()
                nc.vector.tensor_reduce(cv.mx, cv.w, AX.X, ALU.max, negate=True).then_inc(S.conv_max, 1)
                dve.wait_ge(S.conv_exp, 1)
                own(nc.vector.reciprocal(cv.rs, cv.sum))
                own.wait()
                own(nc.vector.tensor_scalar(cv.a[:, 0, 0:32], cv.w, cv.rs, None, ALU.mult))
                own.wait()
                for i in range(6):
                    src, dst, sh = cv.a[:, i % 2, :], cv.a[:, (i + 1) % 2, :], 1 << i
                    own(nc.vector.tensor_scalar(dst, src, cv.nb[:, i:i + 1], None, ALU.mult))
                    own.wait()
                    own(nc.vector.scalar_tensor_tensor(dst[:, sh:LQ], src[:, 0:LQ - sh], bits[:, i:i + 1], dst[:, sh:LQ],
                                                       ALU.mult, ALU.add))
                    own.wait()
                for b in range(B):
                    h = slice(b * LQ, (b + 1) * LQ)
                    ins = nc.vector.tensor_copy(cv.full[h, h], cv.a[h, 0, :])
                ins.then_inc(S.conv_a, 1)
                dve.wait_ge(S.conv_at, 1)
                nc.vector.tensor_copy(cv.at, ps6[:, 32:32 + P]).then_inc(S.conv_atc, 1)
                dve.wait_ge(S.conv_y, 1)
                own(nc.vector.tensor_tensor(x[:], x[:], ps6[:, 256:512], ALU.add))
                own.wait()
            if stages > 5:
                norm(8, x[:], xh[:])
                tokens_t(5)
                mixture(1)
            if stages > 6:
                norm(9, x[:], xh[:])
                tokens_t(6)
                dve.wait_ge(S.qa_psum, 1)
                nc.vector.tensor_scalar(n64.qt, ps01[:].rearrange("p (h k) -> p h k", h=8), 64 ** -0.5, None, ALU.mult)\
                    .then_inc(S.qa_ready, 1)
                for hh in range(2):
                    dve.wait_ge(S.h1_psum, hh + 1)
                    for b in range(B):
                        src = ps23[:].rearrange("p (a h b q) -> p a h b q", a=2, b=B, q=LQ)[:, :, :, b, :]
                        dst = n64.qa[:, b, 8 * hh:8 * hh + 8, :].rearrange("p (h a) q -> p a h q", a=2)
                        nc.vector.tensor_copy(dst, src).then_inc(S.h1_dve, 1)
                def context_back(u):
                    b, hp = u // 8, u % 8
                    nc.vector.tensor_copy(n64.opa[:, b, 2 * hp:2 * hp + 2, :],
                                          ps7[:, 0:P].rearrange("p (h q) -> p h q", h=2))
                    return nc.vector.tensor_copy(n64.opb[CB:P, b, 2 * hp:2 * hp + 2, :],
                                                 ps7[0:CB, P:2 * P].rearrange("p (h q) -> p h q", h=2))

                attention("l2x", 16, plain_max(20, lambda t: (ps01, ps23)[t % 2][:]), lambda t: n64.pt[:, t % 2, :],
                          lambda u: n64.o[:, u % 2, :], CD, context_back)
                dve.wait_ge(S.ot_psum, 1)
                nc.vector.tensor_copy(n64.ot, ps01[:].rearrange("p (h k) -> p h k", h=8)).then_inc(S.ot_ready, 1)
                residual(4, ps6[:, 0:D], "l2x_bo")
            if stages > 7:
                norm(10, x[:], xh[:])
                tokens_t(7)
                ttt(dve, own, bc, inverse_sqrt)
                residual(5, ps6[:, 0:D], "l2a_pb")
            if stages > 8:
                norm(11, x[:], xh[:])
                tokens_t(8)
                mixture(2)
            if stages > 9:
                norm(12, x[:], xh[:])
                tokens_t(9)
                cross16(1, "l3x", "l3x_bq", "l3x_bv")
                residual(6, ps6[:, 0:D], "l3x_b2")
            if stages > 10:
                norm(13, x[:], xh[:])
                tokens_t(10)
                dve.wait_ge(S.g_psum, 1)
                for c in range(C):
                    own(nc.vector.tensor_scalar(gr.t[:, c, :], ps01[:, 512 + c * P:512 + (c + 1) * P], col("l3a_bh", c),
                                                None, ALU.add))
                dve.wait_ge(S.g_z, 1)
                own.wait()
                own(nc.vector.tensor_scalar(gr.a, gr.z, -1.0, 1.0, ALU.mult, ALU.add))
                own(nc.vector.tensor_tensor(gr.b, gr.z, gr.t, ALU.mult))
                own.wait()
                own(nc.vector.tensor_scalar(gr.a, gr.a, 1e-8, None, ALU.add))
                own.wait()
                for c in range(C):
                    for b in range(B):
                        k = slice(b * LQ, (b + 1) * LQ)
                        nc.vector.tensor_tensor_scan(gr.h[:, c, k], gr.a[:, c, k], gr.b[:, c, k], 0.0, ALU.mult, ALU.add)\
                            .then_inc(S.g_scan, 1)
                dve.wait_ge(S.g_back, 1)
                own(nc.vector.tensor_tensor(x[:], x[:], ps6[:, 0:D], ALU.add))
                own.wait()
            if stages > 11:
                norm(14, x[:], xh[:])
                tokens_t(11)
                mixture(3)
            nc.vector.tensor_copy(x[:], x[:]).then_inc(S.x_done, 1)

        def pe_ttt(pe):
            mm = nc.tensor.matmul
            W = lambda name, *shape: weight(wa, L2A, name, *shape)
            gate, val, proj, projt = W("gate", C, 1024), W("val", C, 1024), W("proj", 8, D), W("projt", C, 1024)
            pe.wait_ge(S.in_l2a, 16)
            w = W("qkv", C, 3 * D)
            for n0, n1 in ((0, 512), (512, 768)):
                for c in range(C):
                    ins = mm(ps01[:, n0:n1], xt[:, c, :], w[:, c, n0:n1], start=(c == 0), stop=(c == 1))
            ins.then_inc(S.t_qkv, 1)
            pe.wait_ge(S.t_qk, 2)
            for a in range(2):
                for c in range(C):
                    ins = nc.tensor.transpose(ps6[:, (2 * a + c) * P:(2 * a + c + 1) * P],
                                              tt.qkv[:, 1 - a, c * P:(c + 1) * P], ident)
            ins.then_inc(S.t_kqt, 1)
            pe.wait_ge(S.t_kqtc, 1)
            kt, qt = tt.kqt[:, 0], tt.kqt[:, 1]
            for a, r in ((0, kt), (1, qt)):
                for c in range(C):
                    ins = mm(ps7[:, a * P:(a + 1) * P], kt[:, c, :], r[:, c, :], start=(c == 0), stop=(c == 1))
            ins.then_inc(S.t_gram, 1)

            def through(bank, weights, rhs, updates):
                for f in range(8):
                    terms = [(weights[:, c, f * P:(f + 1) * P], rhs[:, c, :]) for c in range(C)]
                    terms += [(d[:, f, :], r) for d, r in updates]
                    for i, (l, r) in enumerate(terms):
                        ins = mm(bank[:, f * P:(f + 1) * P], l, r, start=(i == 0), stop=(i == len(terms) - 1))
                return ins

            def gram(dst, l, r):
                for f in range(l.shape[1]):
                    ins = mm(dst, l[:, f, :], r[:, f, :], start=(f == 0), stop=(f == l.shape[1] - 1))
                return ins

            def back(bank, src):
                for f in range(8):
                    ins = nc.tensor.transpose(bank[:, f * P:(f + 1) * P], src[:, f, :], ident)
                return ins

            for s in range(2):
                if s == 1:
                    pe.wait_ge(S.t_rc, 1)
                if s == 0:
                    pe.wait_ge(S.t_gramc, 1)
                ug = [(tt.dan[:, 0], tt.tmp[:, 0])] if s else []
                uv = [(tt.dbn[0], tt.tmp[:, 1])] if s else []
                through(ps01, gate, kt, ug).then_inc(S.t_a, 1)
                through(ps23, val, kt, uv).then_inc(S.t_b, 1)
                pe.wait_ge(S.t_h, s + 1)
                h = tt.h[:, s]
                if s == 1:
                    gram(ps7[:, 0:P], tt.h[:, 0], h).then_inc(S.t_x, 1)
                    pe.wait_ge(S.t_xc, 1)
                    mm(ps7[:, P:2 * P], tt.m[0][2][:, 1], tt.tmp[:, 2], start=True, stop=True).then_inc(S.t_z, 1)
                    pe.wait_ge(S.t_zc, 1)
                for f in range(8):
                    ins = mm(ps6[:, 0:D], h[:, f, :], proj[:, f, :], start=(f == 0), stop=(f == 7 and s == 0))
                if s == 1:
                    ins = mm(ps6[:, 0:D], tt.tmp[:, 3], tt.en[:, 0], start=False, stop=True)
                ins.then_inc(S.t_pred, 1)
                back(ps45, h).then_inc(S.t_back, 1)
                gram(ps7[:, 2 * P:3 * P], h, h)
                pe.wait_ge(S.t_e, s + 1)
                for c in range(C):
                    ins = nc.tensor.transpose(ps6[:, D + c * P:D + (c + 1) * P], tt.en[:, s, c * P:(c + 1) * P], ident)
                ins.then_inc(S.t_et, 1)
                pe.wait_ge(S.t_etc, s + 1)
                et = tt.et[:, s]
                if s == 1:
                    gram(ps7[:, 0:P], tt.et[:, 0], et).then_inc(S.t_x, 1)
                    pe.wait_ge(S.t_xc, 2)
                    mm(ps7[:, P:2 * P], tt.m[0][2][:, 0], tt.tmp[:, 4], start=True, stop=True).then_inc(S.t_z, 1)
                    pe.wait_ge(S.t_zc, 2)
                gram(ps7[:, 3 * P:4 * P], et, et).then_inc(S.t_sh, 1)
                through(ps01, projt, et, [(tt.hn[:, 0], tt.tmp[:, 5])] if s else []).then_inc(S.t_dh, 1)
                pe.wait_ge(S.t_da, s + 1)
                gram(ps6[:, 0:P], tt.tb, tt.tb)
                gram(ps6[:, P:2 * P], tt.w, tt.w).then_inc(S.t_s, 1)
                back(ps23, tt.tb).then_inc(S.t_back, 1)
                pe.wait_ge(S.t_backc, 3 * s + 1)
                back(ps45, tt.w).then_inc(S.t_back, 1)
                pe.wait_ge(S.t_tr, s + 1)
                mm(ps7[:, 0:3], ones, tt.tr, start=True, stop=True).then_inc(S.t_trp, 1)
                pe.wait_ge(S.t_backc, 3 * s + 3)
                c_of = (tt.gram[:, 0], tt.gram[:, 0], tt.sh[:, 1])
                s_of = (tt.sgv[:, 0], tt.sgv[:, 1], tt.sh[:, 0])
                n1 = 3 * NS_ITERS * s + 1
                for c in range(3):
                    pe.wait_ge(S.n_wc, n1 + c)
                    mm(halves[c][:, 2 * P:3 * P], tt.wm[c], c_of[c], start=True, stop=True)
                    mm(halves[c][:, 3 * P:4 * P], c_of[c], tt.wm[c], start=True, stop=True).then_inc(S.n_e, 1)
                for c in range(3):
                    pe.wait_ge(S.n_ec, n1 + c)
                    mm(halves[3 + c][:, 0:P], tt.e[c][:, 1], tt.e[c][:, 0], start=True, stop=True)
                    mm(halves[3 + c][:, P:2 * P], tt.e[c][:, 0], tt.e[c][:, 1], start=True, stop=True).then_inc(S.n_p, 1)
                with pe.Fori(0, NS_ITERS - 1) as it:
                    n0 = 3 * (NS_ITERS - 1) * s + 1
                    for c in range(3):
                        pe.wait_ge(S.n_mc, n1 + c + it * 3)
                        mm(halves[c][:, 0:P], s_of[c], tt.m[s][c][:, 1], start=True, stop=True).then_inc(S.n_u, 1)
                    for c in range(3):
                        pe.wait_ge(S.n_uc, n0 + c + it * 3)
                        mm(halves[c][:, P:2 * P], tt.m[s][c][:, 1], tt.u[c], start=True, stop=True).then_inc(S.n_w, 1)
                    for c in range(3):
                        pe.wait_ge(S.n_wc, n1 + 3 + c + it * 3)
                        mm(halves[c][:, 2 * P:3 * P], tt.wm[c], c_of[c], start=True, stop=True)
                        mm(halves[c][:, 3 * P:4 * P], c_of[c], tt.wm[c], start=True, stop=True).then_inc(S.n_e, 1)
                    for c in range(3):
                        pe.wait_ge(S.n_ec, n1 + 3 + c + it * 3)
                        mm(halves[3 + c][:, 0:P], tt.e[c][:, 0], tt.e[c][:, 1], start=True, stop=True).then_inc(S.n_p, 1)
                    for c in range(3):
                        pe.wait_ge(S.n_pc, n0 + c + it * 3)
                        mm(halves[3 + c][:, P:2 * P], tt.pt[c], tt.m[s][c][:, 0], start=True, stop=True)
                        mm(halves[3 + c][:, 2 * P:3 * P], tt.m[s][c][:, 0], tt.pt[c], start=True, stop=True)\
                            .then_inc(S.n_m, 1)
                pe.wait_ge(S.n_mc, 3 * NS_ITERS * (s + 1))
                if s == 0:
                    for c in range(2):
                        ins = mm(ps6[:, c * P:(c + 1) * P], tt.m[0][c][:, 0], tt.gram[:, 0], start=True, stop=True)
                else:
                    for i, (u, c) in enumerate(((0, 0), (0, 1), (1, 0), (1, 1))):
                        ins = mm(ps6[:, i * P:(i + 1) * P], tt.m[u][c][:, 0], tt.gram[:, 1], start=True, stop=True)
                ins.then_inc(S.t_r, 1)
            pe.wait_ge(S.t_rc, 2)
            through(ps01, gate, qt, [(tt.dan[:, 0], tt.tmp[:, 0]), (tt.dan[:, 1], tt.tmp[:, 2])]).then_inc(S.t_a, 1)
            through(ps23, val, qt, [(tt.dbn[0], tt.tmp[:, 1]), (tt.dbn[1], tt.tmp[:, 3])]).then_inc(S.t_b, 1)
            pe.wait_ge(S.t_h, 3)
            h = tt.tb
            for u in range(2):
                ins = gram(ps7[:, u * P:(u + 1) * P], tt.h[:, u], h)
            ins.then_inc(S.t_x, 1)
            pe.wait_ge(S.t_xc, 3)
            for u in range(2):
                ins = mm(ps7[:, (2 + u) * P:(3 + u) * P], tt.m[u][2][:, 1], tt.tmp[:, 4 + u], start=True, stop=True)
            ins.then_inc(S.t_z, 1)
            pe.wait_ge(S.t_zc, 3)
            for d in range(C):
                k = slice(d * P, (d + 1) * P)
                terms = [(proj[:, f, k], h[:, f, :]) for f in range(8)]
                terms += [(tt.en[:, u, k], tt.tmp[:, u]) for u in range(2)]
                for i, (l, r) in enumerate(terms):
                    ins = mm(ps45[:, k], l, r, start=(i == 0), stop=(i == len(terms) - 1))
            ins.then_inc(S.t_o, 1)
            pe.wait_ge(S.t_oc, 1)
            w = W("pw", C, D)
            for c in range(C):
                ins = mm(ps6[:, 0:D], tt.et[:, 0, c, :], w[:, c, :], start=(c == 0), stop=(c == 1))
            ins.then_inc(S.out_psum, 1)

        @block.tensor
        def _(pe):
            mm = nc.tensor.matmul

            def tokens_t(stage, norms_done):
                pe.wait_ge(S.xh_ready, norms_done)
                for c in range(C):
                    ins = nc.tensor.transpose(ps7[:, c * P:(c + 1) * P], xh[:, c * P:(c + 1) * P], ident)
                ins.then_inc(S.xt_psum, 1)
                pe.wait_ge(S.xt_ready, stage + 1)

            def attention(stage, n, scores, pt_of, v_of, width, tiles, post=None):
                base = ATT_BASE[stage]
                for t in range(n + 2 + (post is not None)):
                    if t < n:
                        if stage == "l0x":
                            if t >= 1:
                                pe.wait_ge(S.att_max, t)
                        elif t >= 2:
                            pe.wait_ge(S.att_exp, base + t - 1)
                        scores(t).then_inc(S.att_s, 1)
                    if 1 <= t <= n:
                        u = t - 1
                        pe.wait_ge(S.att_exp, base + t)
                        if u >= 1:
                            pe.wait_ge(S.att_pta, base + u)
                            pe.wait_ge(S.att_ptd, base + u)
                        src = q.sc[:, u % 2, :] if stage == "l0x" else \
                            (n64.p if stage == "l2x" else n16.p)[:, u % 2, :]
                        for k in range(tiles):
                            dst = ps45[:, k * P:(k + 1) * P] if k < 8 else halves[3][:, 0:P]
                            ins = nc.tensor.transpose(dst, src[:, k * P:(k + 1) * P], ident)
                        ins.then_inc(S.att_pt, 1)
                    if post is not None and t >= 3:
                        u = t - 3
                        pe.wait_ge(S.att_on, base + u + 1)
                        if u >= 1:
                            pe.wait_ge(S.opt_ready, OPT_BASE[stage] + u)
                        post(u).then_inc(S.opt_psum, 1)
                    if 2 <= t < n + 2:
                        u = t - 2
                        pe.wait_ge(S.att_pta, base + u + 1)
                        pe.wait_ge(S.att_ptd, base + u + 1)
                        if u >= 1:
                            pe.wait_ge(S.att_on, base + u)
                        for k in range(tiles):
                            ins = mm(ps6[:, 0:width], pt_of(u)[:, k * P:(k + 1) * P],
                                     v_of(u, k), start=(k == 0), stop=(k == tiles - 1))
                        ins.then_inc(S.att_o, 1)

            def mixture(m):
                base, nu = MOE_BASE[m], MOE_UNITS[m]
                if m == 0:
                    pe.wait_ge(S.in_router, 16)
                for c in range(C):
                    ins = mm(ps7[:, 256:264], xt[:, c, :], router[:, (m * C + c) * E:(m * C + c + 1) * E],
                             start=(c == 0), stop=(c == C - 1))
                ins.then_inc(S.router_psum, 1)
                gated = m >= 2
                down_at = (1 + gated) * C * FU

                def up(s, it, first):
                    par = s % 2
                    pe.wait_ge(slot_full[s], 16 * (base // SLOTS + 1) + it * 16)
                    if not (first and s < 2):
                        pe.wait_ge(S.moe_h, base + s - 1 + it * SLOTS)
                    w = ring[:, s, 0:down_at].rearrange("p (g c f) -> p g c f", g=1 + gated, c=C)
                    for g in range(1 + gated):
                        for fc in range(FC):
                            for c in range(C):
                                ins = mm(halves[2 * g + par][:, fc * P:(fc + 1) * P], w[:, g, c, fc * P:(fc + 1) * P],
                                         xt[:, c, :], start=(c == 0), stop=(c == C - 1))
                    ins.then_inc(S.moe_up, 1)

                def down(s, value):
                    par = s % 2
                    pe.wait_ge(S.moe_h, value)
                    if not (isinstance(value, int) and value - 2 <= 0):
                        pe.wait_ge(S.moe_acc, value - 2)
                    for fc in range(FC):
                        ins = mm(halves[4 + par][:, 0:D], mo.h[:, par, fc * P:(fc + 1) * P],
                                 ring[:, s, down_at + fc * D:down_at + (fc + 1) * D],
                                 start=(fc == 0), stop=(fc == FC - 1))
                    ins.then_inc(S.moe_y, 1)

                def lot(it):
                    for s in range(SLOTS):
                        first = isinstance(it, int) and it == 0
                        up(s, it, first)
                        if not (first and s == 0):
                            down((s - 1) % SLOTS, base + s + it * SLOTS)

                lot(0)
                if m in (1, 3):
                    pe.wait_ge(S.comb_ready, m + 1)
                    if m == 1:
                        pe.wait_ge(S.in_e8, 16)
                    nc.tensor.transpose(ps7[0:E, 264:264 + P], mo.comb, ident).then_inc(S.combt_psum, 1)
                    pe.wait_ge(S.combt_ready, m // 2 + 1)
                    mm(ps7[:, 0:D], mo.combt[0:E, :], e8[:, (m // 2) * D:(m // 2 + 1) * D], start=True, stop=True)\
                        .then_inc(S.b2_psum, 1)
                if nu // SLOTS == 2:
                    lot(1)
                else:
                    with pe.Fori(1, nu // SLOTS) as it:
                        lot(it)
                down(SLOTS - 1, base + nu)

            W = lambda name, *shape: weight(wa, L0X, name, *shape)
            pe.wait_ge(S.in_const, 16)
            tokens_t(0, 2)
            pe.wait_ge(S.in_l0x, 16)
            for c in range(C):
                ins = mm(ps6[:, 0:D], xt[:, c, :], W("wq", C, D)[:, c, :], start=(c == 0), stop=(c == 1))
            ins.then_inc(S.q_psum, 1)
            def keys_values(i):
                j = L0X_ORDER[i]
                if j < KT:
                    pe.wait_ge(S.xn_act, j // 4 + 1)
                    pe.wait_ge(S.xn_dve, j // 4 + 1)
                if i >= 2:
                    pe.wait_ge(S.kv_v, i - 1)
                dst, k = halves[2 + i % 2], slice(j * P, (j + 1) * P)
                if j < KT:
                    w = W("wkv", C, 2 * D)
                    mm(dst, xnt[:, 0, k], w[:, 0, :], start=True, stop=False)
                    ins = mm(dst, xnt[0:CB, 1, k], w[0:CB, 1, :], start=False, stop=True)
                else:
                    w = W("wlkv", C, 2 * D)
                    mm(dst, xt[:, 0, :], w[:, 0, :], start=True, stop=False)
                    ins = mm(dst, xt[:, 1, :], w[:, 1, :], start=False, stop=True)
                ins.then_inc(S.kv_psum, 1)

            def rows_t(g):
                pe.wait_ge(S.xn_ready, 4 * g + 4)
                if g >= 1:
                    pe.wait_ge(S.xn_act, g)
                    pe.wait_ge(S.xn_dve, g)
                for i in range(4):
                    xn = q.xn[:, (4 * g + i) % 8, :]
                    nc.tensor.transpose(halves[0][:, i * P:(i + 1) * P], xn[:, 0:P], ident)
                    ins = nc.tensor.transpose(halves[1][0:CB, i * P:(i + 1) * P], xn[:, P:CD], ident)
                ins.then_inc(S.xn_psum, 1)

            rows_t(0)
            keys_values(0)
            for g in range(1, KT // 4):
                rows_t(g)
                for i in range(4 * g - 3, 4 * g + 1):
                    keys_values(i)
            for i in range(KT - 3, KT + 1):
                keys_values(i)
            pe.wait_ge(S.q_norm, 1)
            for c in range(C):
                ins = nc.tensor.transpose(ps6[:, 256 + c * P:256 + (c + 1) * P], xh[:, c * P:(c + 1) * P], ident)
            ins.then_inc(S.qt_psum, 1)
            for g, (first, n) in enumerate(L0X_GROUPS):
                pe.wait_ge(S.khat_ready, 2 * g + 1)
                if g >= 2:
                    pe.wait_ge((S.kt_dve, S.kt_act)[g % 2], g // 2)
                for i in range(n):
                    for c in range(C):
                        ins = nc.tensor.transpose(halves[4 + g % 2][:, (c * n + i) * P:(c * n + i + 1) * P],
                                                  q.knat[:, first + i, c * P:(c + 1) * P], ident)
                ins.then_inc(S.kt_psum, 1)
            pe.wait_ge(S.qbd_ready, 1)
            pe.wait_ge(S.kt_dve, 5)
            pe.wait_ge(S.kt_act, 4)

            def scores_l0x(t):
                b, hp = t // 2, t % 2
                bank = ps01
                mm(bank[:, 0:512], q.qbd[:, b, hp, :], q.kt[:, hp, b * KEYS:b * KEYS + 512], start=True, stop=True)
                mm(bank[:, 512:1024], q.qbd[:, b, hp, :], q.kt[:, hp, b * KEYS + 512:(b + 1) * KEYS], start=True, stop=True)
                return mm(halves[2][:, 0:P], q.qbd[:, b, hp, :], q.kt[:, hp, KT * P:(KT + 1) * P],
                          start=True, stop=True)

            attention("l0x", 4, scores_l0x, lambda u: q.pt[:, u % 2, :],
                      lambda u, k: q.v[:, (u // 2) * KTB + k if k < KTB else KT, (u % 2) * P:(u % 2) * P + P], P, 9,
                      lambda u: nc.tensor.transpose(ps7[:, 0:P], xh[:, (u % 2) * P:(u % 2) * P + P], ident))
            pe.wait_ge(S.opt_ready, 4)
            for c in range(C):
                ins = mm(ps6[:, 0:D], xt[:, c, :], W("wo", C, D)[:, c, :], start=(c == 0), stop=(c == 1))
            ins.then_inc(S.out_psum, 1)

            def context16(i, shares):
                W = lambda name, *shape: weight((wa, wb)[i], (L1X, L3X)[i], name, *shape)
                ct = carve(ctxt, 0, C, B * KEYS)
                for j in shares:
                    if j >= 2:
                        pe.wait_ge(S.c_act, 16 * i + j - 1)
                    dst = halves[1 + 4 * (j % 2)]
                    if j < 8:
                        c, kb = j // 4, j % 4
                        k = slice(kb * 512, (kb + 1) * 512)
                        w = W("wk", C, D)
                        mm(dst, w[:, 0, c * P:(c + 1) * P], ct[:, 0, k], start=True, stop=False)
                        ins = mm(dst, w[0:CB, 1, c * P:(c + 1) * P], ct[0:CB, 1, k], start=False, stop=True)
                    else:
                        w = W("wv", C, D)
                        for a in range(2):
                            kt = 2 * (j - 8) + a
                            k = slice(kt * P, (kt + 1) * P)
                            mm(dst[:, a * D:(a + 1) * D], ct[:, 0, k], w[:, 0, :], start=True, stop=False)
                            ins = mm(dst[:, a * D:(a + 1) * D], ct[0:CB, 1, k], w[0:CB, 1, :], start=False, stop=True)
                    ins.then_inc(S.c_psum, 1)

            if stages > 1:
                W = lambda name, *shape: weight(wb, L0A, name, *shape)
                pe.wait_ge(S.in_l1x, 16)
                pe.wait_ge(S.in_ctxt, 16)
                context16(0, range(0, 5))
                tokens_t(1, 4)
                pe.wait_ge(S.in_l0a, 16)
                for h in range(4):
                    for c in range(C):
                        mm(ps01[:, h * P:(h + 1) * P], W("wq", C, 512)[:, c, h * P:(h + 1) * P], xt[:, c, :],
                           start=(c == 0), stop=(c == 1))
                for c in range(C):
                    mm(ps23[:, 0:P], W("wk", C, P)[:, c, :], xt[:, c, :], start=(c == 0), stop=(c == 1))
                for c in range(C):
                    ins = mm(ps23[:, P:P + 64], xt[:, c, :], W("wv", C, 64)[:, c, :], start=(c == 0), stop=(c == 1))
                ins.then_inc(S.sa_qkv, 1)
                context16(0, range(5, 7))
                pe.wait_ge(S.sa_q, 1)
                for h in range(4):
                    for b in range(B):
                        ins = mm(ps45[:, (h * 2 + b) * LQ:(h * 2 + b + 1) * LQ], r0.qbd[:, b, h, :],
                                 r0.kt[:, b * LQ:(b + 1) * LQ], start=True, stop=True)
                ins.then_inc(S.sa_s, 1)
                context16(0, range(7, 10))
                pe.wait_ge(S.sa_norm, 1)
                for h in range(4):
                    ins = nc.tensor.transpose(ps01[:, h * P:(h + 1) * P], r0.p[:, h].rearrange("p b k -> p (b k)"), ident)
                ins.then_inc(S.sa_pt, 1)
                context16(0, range(10, 11))
                pe.wait_ge(S.sa_ptc, 1)
                for h in range(4):
                    for b in range(B):
                        for j in range(2):
                            k = slice(b * LQ, (b + 1) * LQ)
                            ins = mm(halves[2 + b][64 * j:64 * j + 64, h * LQ:(h + 1) * LQ], r0.v[k, :],
                                     r0.pt[k, h, 64 * j:64 * j + 64], start=True, stop=True)
                ins.then_inc(S.sa_ot, 1)
                context16(0, range(11, 12))
                pe.wait_ge(S.sa_otc, 1)
                for h in range(4):
                    ins = mm(ps6[:, 0:D], r0.ot[:, h, :], W("wo", 4, D)[:, h, :], start=(h == 0), stop=(h == 3))
                ins.then_inc(S.out_psum, 1)
                context16(0, range(12, 16))
            if stages > 2:
                tokens_t(2, 6)
                pe.wait_ge(S.c_act, 16)
                mixture(0)

            def cross16(i, stage, wt, tab, norms_done):
                W = lambda name, *shape: weight(wt, tab, name, *shape)
                tokens_t((3, 9)[i], norms_done)
                for c in range(C):
                    for cc in range(C):
                        ins = mm(ps6[:, c * P:(c + 1) * P], W("wq", C, D)[:, cc, c * P:(c + 1) * P], xt[:, cc, :],
                                 start=(cc == 0), stop=(cc == 1))
                ins.then_inc(S.q16_psum, 1)
                pe.wait_ge(S.c_act, 16 * i + 16)
                pe.wait_ge(S.q16_ready, i + 1)

                def scores(t):
                    cb, g = t // 4, t % 4
                    c, b = cb // 2, cb % 2
                    lhs = n16.qbd[:, c, b, 2 * g:2 * g + 2, :].rearrange("p j k -> p (j k)")
                    for k in range(2):
                        ins = mm((ps01, ps23)[t % 2][:, k * 512:(k + 1) * 512], lhs,
                                 n16.kt[:, c, b * KEYS + k * 512:b * KEYS + (k + 1) * 512], start=True, stop=True)
                    return ins

                def values(u, k):
                    cb, g = u // 4, u % 4
                    at = (cb // 2) * P + 32 * g
                    return n16.v[:, (cb % 2) * KTB + k, at:at + 32]

                attention(stage, 16, scores, lambda u: n16.pt[:, u % 2, :], values, 32, 8)
                pe.wait_ge(S.att_on, ATT_BASE[stage] + 16)
                for c in range(C):
                    for b in range(B):
                        ins = nc.tensor.transpose(ps6[:, (c * 2 + b) * P:(c * 2 + b + 1) * P], n16.o[:, c, b, :], ident)
                ins.then_inc(S.o16_psum, 1)
                pe.wait_ge(S.o16_ready, i + 1)

            if stages > 3:
                cross16(0, "l1x", wa, L1X, 7)
                w = weight(wa, L1X, "wo", C, D)
                for c in range(C):
                    ins = mm(ps6[:, 0:D], n16.ot[:, c, :], w[:, c, :], start=(c == 0), stop=(c == 1))
                ins.then_inc(S.out_psum, 1)
            if stages > 4:
                tokens_t(4, 8)
                w = weight(wa, L1X, "l1a_w", C, 32)
                for c in range(C):
                    ins = mm(ps6[:, 0:32], xt[:, c, :], w[:, c, :], start=(c == 0), stop=(c == 1))
                ins.then_inc(S.conv_s, 1)
                pe.wait_ge(S.conv_a, 1)
                nc.tensor.transpose(ps6[:, 32:32 + P], cv.full, ident).then_inc(S.conv_at, 1)
                pe.wait_ge(S.conv_atc, 1)
                mm(ps6[:, 256:512], cv.at, xh[:], start=True, stop=True).then_inc(S.conv_y, 1)
            if stages > 5:
                tokens_t(5, 9)
                mixture(1)
            if stages > 6:
                W = lambda name, *shape: weight(wb, L2X, name, *shape)
                tokens_t(6, 10)
                pe.wait_ge(S.in_l2x, 16)
                for h in range(8):
                    for c in range(C):
                        ins = mm(ps01[:, h * P:(h + 1) * P], W("wq", C, 1024)[:, c, h * P:(h + 1) * P], xt[:, c, :],
                                 start=(c == 0), stop=(c == 1))
                ins.then_inc(S.qa_psum, 1)
                pe.wait_ge(S.qa_ready, 1)
                for hh in range(2):
                    if hh == 1:
                        pe.wait_ge(S.h1_dve, B)
                        pe.wait_ge(S.h1_act, B)
                    for i in range(8):
                        h = 8 * hh + i
                        r = slice(64 * (h % 2), 64 * (h % 2) + 64)
                        w = W("wk", 8, CD)[r, h // 2, :]
                        dst = slice((i // 2) * P, (i // 2 + 1) * P)
                        mm(halves[2 + i % 2][:, dst], w[:, 0:P], n64.qt[r, h // 2, :], start=True, stop=True)
                        ins = mm(halves[4 + i % 2][0:CB, dst], w[:, P:CD], n64.qt[r, h // 2, :], start=True, stop=True)
                    ins.then_inc(S.h1_psum, 1)
                pe.wait_ge(S.h1_dve, 2 * B)
                pe.wait_ge(S.h1_act, 2 * B)
                ct = carve(ctxt, 0, C, B * KEYS)

                def scores64(t):
                    b, hp = t // 8, t % 8
                    for k in range(2):
                        keys = slice(b * KEYS + k * 512, b * KEYS + (k + 1) * 512)
                        dst = (ps01, ps23)[t % 2][:, k * 512:(k + 1) * 512]
                        heads = slice(2 * hp, 2 * hp + 2)
                        mm(dst, n64.qa[:, b, heads, :].rearrange("p h q -> p (h q)"), ct[:, 0, keys],
                           start=True, stop=False)
                        ins = mm(dst, n64.qb[0:CB, b, heads, :].rearrange("p h q -> p (h q)"), ct[0:CB, 1, keys],
                                 start=False, stop=True)
                    return ins

                def context_out(u):
                    nc.tensor.transpose(ps7[:, 0:P], n64.o[:, u % 2, 0:P], ident)
                    return nc.tensor.transpose(ps7[0:CB, P:2 * P], n64.o[:, u % 2, P:CD], ident)

                attention("l2x", 16, scores64, lambda u: n64.pt[:, u % 2, :],
                          lambda u, k: ctxn[:, ((u // 8) * KTB + k) * CD:((u // 8) * KTB + k + 1) * CD], CD, 8, context_out)
                pe.wait_ge(S.opt_ready, 4 + 16)
                for h in range(16):
                    dst = ps01[64 * (h % 2):64 * (h % 2) + 64, (h // 2) * P:(h // 2 + 1) * P]
                    w = W("wv", 2, 1024)[:, :, h * 64:(h + 1) * 64]
                    mm(dst, w[:, 0, :], n64.opa[:, :, h, :], start=True, stop=False)
                    ins = mm(dst, w[CB:P, 1, :], n64.opb[CB:P, :, h, :], start=False, stop=True)
                ins.then_inc(S.ot_psum, 1)
                pe.wait_ge(S.ot_ready, 1)
                for h in range(8):
                    ins = mm(ps6[:, 0:D], n64.ot[:, h, :], W("wo", 8, D)[:, h, :], start=(h == 0), stop=(h == 7))
                ins.then_inc(S.out_psum, 1)
            if stages > 7:
                tokens_t(7, 11)
                pe_ttt(pe)
            if stages > 8:
                pe.wait_ge(S.in_l3x, 16)
                context16(1, range(0, 3))
                tokens_t(8, 12)
                pe.wait_ge(S.c_act, 16 + 3)
                mixture(2)
                pe.wait_ge(S.moe_acc, MOE_BASE[3])
                context16(1, range(3, 16))
            if stages > 9:
                cross16(1, "l3x", wb, L3X, 13)
                w = weight(wb, L3X, "w1", C, 512)
                for f in range(4):
                    for c in range(C):
                        ins = mm(halves[0][:, f * P:(f + 1) * P], w[:, c, f * P:(f + 1) * P], n16.ot[:, c, :],
                                 start=(c == 0), stop=(c == 1))
                ins.then_inc(S.m_h, 1)
                pe.wait_ge(S.m_hc, 1)
                w = weight(wb, L3X, "w2", 4, D)
                for f in range(4):
                    ins = mm(ps6[:, 0:D], n16.h[:, f, :], w[:, f, :], start=(f == 0), stop=(f == 3))
                ins.then_inc(S.out_psum, 1)
            if stages > 10:
                tokens_t(10, 14)
                pe.wait_ge(S.in_l3a, 16)
                for i, name in enumerate(("wz", "wh")):
                    w = weight(wa, L3A, name, C, D)
                    for cc in range(C):
                        for c in range(C):
                            ins = mm(ps01[:, i * 512 + cc * P:i * 512 + (cc + 1) * P], w[:, c, cc * P:(cc + 1) * P], xt[:, c, :],
                                     start=(c == 0), stop=(c == 1))
                ins.then_inc(S.g_psum, 1)
                pe.wait_ge(S.g_scan, 4)
                for c in range(C):
                    ins = nc.tensor.transpose(ps6[:, c * P:(c + 1) * P], gr.h[:, c, :], ident)
                ins.then_inc(S.g_back, 1)
            if stages > 11:
                tokens_t(11, 15)
                mixture(3)


def chunks(a, np):
    n = -(-a.shape[0] // P)
    if a.shape[0] < n * P:
        full = np.zeros((n * P,) + a.shape[1:], a.dtype)
        full[:a.shape[0]] = a
        a = full
    return a.reshape(n, P, -1).transpose(1, 0, 2).reshape(P, -1)


def pack_units(np, ups, down, per):
    cat = []
    for w in ups:
        cat.append(w.reshape(E, C, P, per, FU).transpose(0, 3, 2, 1, 4).reshape(E * per, P, C * FU))
    cat.append(down.reshape(E, per, FC, P, D).transpose(0, 1, 3, 2, 4).reshape(E * per, P, FC * D))
    return np.ascontiguousarray(np.concatenate(cat, axis=2))


def layout(inp, np):
    g = {k: np.asarray(v) for k, v in inp.items()}
    f = np.float32
    a = {}
    a["x"] = np.ascontiguousarray(g["x"].reshape(P, D))
    rows = g["ctx_768"].reshape(KT * P, CD)
    a["ctx"] = np.ascontiguousarray(rows.reshape(KT, P, CD).transpose(1, 0, 2).reshape(P, KT * CD))
    a["ctxt"] = np.ascontiguousarray(chunks(rows.T, np))
    a["mask"] = np.ascontiguousarray(g["mask_BxS2_bk0"].reshape(B * KEYS))

    def column(v):
        return chunks(v.reshape(-1, 1), np)

    twice = lambda v: np.concatenate([v, v])
    c = {"l0x_lg": g["L0_xattn_ln_l_g"], "l0x_lb": g["L0_xattn_ln_l_b"], "l0x_xg": g["L0_xattn_ln_x_g"],
         "l0x_xb": g["L0_xattn_ln_x_b"], "l0x_qg": twice(g["L0_xattn_qn_g"]), "l0x_kg": twice(g["L0_xattn_kn_g"]),
         "l0a_w": g["L0_attn_norm_w"], "l0a_b": g["L0_attn_norm_b"], "l1x_bq": g["L1_xattn_bq"],
         "l1x_bk": g["L1_xattn_bk"], "l1x_bv": g["L1_xattn_bv"], "l3x_bq": g["L3_xattn_bq"],
         "l3x_bk": g["L3_xattn_bk"], "l3x_bv": g["L3_xattn_bv"], "l3x_b1": g["L3_xattn_b1"],
         "l3a_bz": g["L3_attn_bz"], "l3a_bh": g["L3_attn_bh"], "l1f_b1": g["L1_ffn_b1"].reshape(-1),
         "l3f_b0": g["L3_ffn_b0"].reshape(-1), "l3f_b1": g["L3_ffn_b1"].reshape(-1)}
    a["cols"] = np.ascontiguousarray(np.concatenate([column(c[n]) for n in COLS], axis=1))
    r = {"l0x_bo": "L0_xattn_bo", "l0a_ow": "L0_attn_out_norm_w", "l0a_ob": "L0_attn_out_norm_b",
         "l1x_bo": "L1_xattn_bo", "l1a_b": "L1_attn_b", "l2x_bo": "L2_xattn_b_o", "l2a_pb": "L2_attn_proj_b",
         "l3x_b2": "L3_xattn_b2", "l3f_bg": "L3_ffn_bg"}
    a["rows"] = np.concatenate([g[r[n]] for n in ROWS])
    a["late"] = np.concatenate([g["L2_attn_" + n] for n in ("qkv_b", "qn_scale", "qn_bias", "kn_scale", "kn_bias")])
    a["e8"] = np.ascontiguousarray(np.concatenate([g["L1_ffn_b2"], g["L3_ffn_b2"]], axis=1))
    p = np.arange(P)
    a["const"] = np.concatenate([
        np.eye(P, dtype=f), np.ones((P, P), f), np.broadcast_to(np.arange(E, dtype=f), (P, E)),
        np.stack([(p // 16) % 2 == j for j in range(2)], 1).astype(f),
        np.stack([(p % LQ) >> i & 1 for i in range(6)], 1).astype(f),
        np.full((P, 72), -0.5, f), np.full((P, 32), 0.5, f),
        np.stack([(p // 16) % 8 == j for j in range(8)], 1).astype(f)], axis=1)
    a["router"] = np.ascontiguousarray(np.concatenate(
        [chunks(w, np) for w in (g["L0_ffn_router_w"].T, g["L1_ffn_gate_w"], g["L2_ffn_router_w"].T, g["L3_ffn_Wg"])],
        axis=1))

    def pack(*ws):
        return np.ascontiguousarray(np.concatenate([chunks(w, np) for w in ws], axis=1))

    kv = g["L0_attn_Wkv"]
    a["l0x"] = pack(g["L0_xattn_Wq"].T, g["L0_xattn_Wkv"].T, g["L0_xattn_Wlkv"].T, g["L0_xattn_Wo"].T)
    a["l0a"] = pack(g["L0_attn_Wq"], np.concatenate([kv[:, :64], kv[:, :64]], axis=1), kv[:, 64:], g["L0_attn_Wo"])
    a["l1x"] = pack(g["L1_xattn_Wq"], g["L1_xattn_Wk"], g["L1_xattn_Wv"], g["L1_xattn_Wo"], g["L1_attn_W"].T)
    wv = g["L2_xattn_w_v"]
    low = np.zeros((2 * P, 1024), f)
    low[:P], low[P + CB:] = wv[:P], wv[P:]
    a["l2x"] = pack(g["L2_xattn_w_q"], g["L2_xattn_w_k"].T, low, g["L2_xattn_w_o"])
    a["l2a"] = pack(g["L2_attn_qkv_w"], g["L2_attn_ttt_gate"], g["L2_attn_ttt_val"], g["L2_attn_ttt_proj"],
                    g["L2_attn_ttt_proj"].T, g["L2_attn_proj_w"])
    a["l3x"] = pack(g["L3_xattn_Wq"], g["L3_xattn_Wk"], g["L3_xattn_Wv"], g["L3_xattn_W1"], g["L3_xattn_W2"])
    a["l3a"] = pack(g["L3_attn_Wz"].T, g["L3_attn_Wh"].T)
    a["m0"] = pack_units(np, [g["L0_ffn_w1"]], g["L0_ffn_w2"], 1)
    a["m1"] = pack_units(np, [g["L1_ffn_w1"]], g["L1_ffn_w2"], 2)
    a["m2"] = pack_units(np, [g["L2_ffn_w_gate"].transpose(0, 2, 1), g["L2_ffn_w_up"].transpose(0, 2, 1)],
                         g["L2_ffn_w_down"].transpose(0, 2, 1), 1)
    a["m3"] = pack_units(np, [g["L3_ffn_W1"], g["L3_ffn_W0"]], g["L3_ffn_W2"], 2)
    return a


_ORDER = ["x", "ctx", "ctxt", "mask", "cols", "rows", "late", "e8", "const", "router",
          "l0x", "l0a", "l1x", "l2x", "l2a", "l3x", "l3a", "m0", "m1", "m2", "m3"]
STAGES = 12


def kernel(**inputs):
    import numpy as _np
    import concourse.bacc as _bacc
    from concourse import mybir as _mybir
    from concourse.bass_utils import run_bass_kernel_spmd as _run

    nc = _bacc.Bacc("TRN2", target_bir_lowering=False, num_devices=1)
    laid = layout(inputs, _np)
    arrays, args = {}, []
    for name in _ORDER:
        arr = laid[name]
        arrays[f"in_{name}_dram"] = arr
        args.append(nc.dram_tensor(f"in_{name}_dram", arr.shape, _mybir.dt.from_np(arr.dtype), kind="ExternalInput").ap())
    args.append(nc.dram_tensor("out_0_dram", (P, D), F32, kind="ExternalOutput").ap())
    perceiver_kernel(nc, *args, stages=STAGES)
    r = _run(nc, [arrays], core_ids=[0])
    return r.results[0]["out_0_dram"].reshape(B, LQ, D)
```

```python
from contextlib import ExitStack

import concourse.bass as bass
from concourse import mybir

F32 = mybir.dt.float32
I32 = mybir.dt.int32
F32R = mybir.dt.float32r
U32 = mybir.dt.uint32
U8 = mybir.dt.uint8
ALU = mybir.AluOpType
ACT = mybir.ActivationFunctionType
AX = mybir.AxisListType

P = 128
B, LQ = 2, 64
D = 256
C = D // P
KEYS = 1024
CD = 192
CB = CD - P
KT = B * KEYS // P
KTB = KEYS // P
E = 8
SLOTS = 4
FU = 512
FC = FU // P
UNIT = 3 * 1024
LN_EPS = 1e-5
NEG = -3.0e38
MASKED = -1.0e30

COLS = {}
for _name, _n in (("l0x_lg", 2), ("l0x_lb", 2), ("l0x_xg", 2), ("l0x_xb", 2), ("l0x_qg", 1), ("l0x_kg", 1),
                  ("l0a_w", 2), ("l0a_b", 2), ("l1x_bq", 2), ("l1x_bk", 2), ("l1x_bv", 2),
                  ("l3x_bq", 2), ("l3x_bk", 2), ("l3x_bv", 2), ("l3x_b1", 4), ("l3a_bz", 2), ("l3a_bh", 2),
                  ("l1f_b1", 64), ("l3f_b0", 64), ("l3f_b1", 64)):
    COLS[_name] = (sum(n for _, n in COLS.values()), _n)
NCOLS = sum(n for _, n in COLS.values())

ROWS = {}
for _name, _n in (("l0x_bo", D), ("l0a_ow", D), ("l0a_ob", D), ("l1x_bo", D), ("l1a_b", 32), ("l2x_bo", D),
                  ("l2a_pb", D), ("l3x_b2", D), ("l3f_bg", E)):
    ROWS[_name] = (sum(n for _, n in ROWS.values()), _n)
NROWS = sum(n for _, n in ROWS.values())

LATE = {"qkvb": (0, 3 * D), "qs": (768, 16), "qb": (784, 16), "ks": (800, 16), "kb": (816, 16)}
NLATE = 832

CONSTS = {"ident": (0, 128), "ones": (128, 128), "iota": (256, 8), "par": (264, 2), "bits": (266, 6),
          "nhalf": (272, 72), "phalf": (344, 32),
          "head": (376, 8)}
NCONST = 384

ROUTER = 4 * 16

def table(*items):
    out, at = {}, 0
    for name, n in items:
        out[name] = (at, n)
        at += n
    return out, at

L0X, L0X_N = table(("wq", 2 * D), ("wkv", 2 * 2 * D), ("wlkv", 2 * 2 * D), ("wo", 2 * D))
L0A, L0A_N = table(("wq", 2 * 512), ("wk", 2 * P), ("wv", 2 * 64), ("wo", 4 * D))
L1X, L1X_N = table(("wq", 2 * D), ("wk", 2 * D), ("wv", 2 * D), ("wo", 2 * D), ("l1a_w", 2 * 32))
L2X, L2X_N = table(("wq", 2 * 1024), ("wk", 8 * CD), ("wv", 2 * 1024), ("wo", 8 * D))
L2A, L2A_N = table(("qkv", 2 * 768), ("gate", 2 * 1024), ("val", 2 * 1024), ("proj", 8 * D),
                   ("projt", 2 * 1024), ("pw", 2 * D))
L3X, L3X_N = table(("wq", 2 * D), ("wk", 2 * D), ("wv", 2 * D), ("w1", 2 * 512), ("w2", 4 * D))
L3A, L3A_N = table(("wz", 2 * D), ("wh", 2 * D))

L0X_ORDER = [KT] + list(range(KT))
L0X_GROUPS = [(KT, 1)] + [(j, 2) for j in range(0, KT, 2)]
ATT_BASE = {"l0x": 0, "l1x": 4, "l2x": 20, "l3x": 36}
KEEP = (0, 0, 6, 9, 9, 9, 10, 9, 3, 6, 9, 9)
SHARE_BANKS = ((1, 5) * 8, (3, 5) * 3 + (5, 3, 5, 3, 5) + (3, 5, 3) + (5, 3))
HI_BASE = (0, 4, 14)
OPT_BASE = {"l0x": 0, "l2x": 4}
MOE_BASE = (0, 8, 24, 32)
MOE_UNITS = (8, 16, 8, 16)


class Views:
    pass


class Own:

    def __init__(self, eng, sem):
        self.eng, self.sem, self.n = eng, sem, 0

    def __call__(self, ins):
        ins.then_inc(self.sem, 1)
        self.n += 1

    def wait(self):
        self.eng.wait_ge(self.sem, self.n)


def perceiver_kernel(nc, x_in, ctx_in, ctxt_in, mask_in, cols_in, rows_in, late_in, e8_in, const_in, router_in,
                     l0x_in, l0a_in, l1x_in, l2x_in, l2a_in, l3x_in, l3a_in, m0_in, m1_in, m2_in, m3_in, out):
    with ExitStack() as ctx:
        def sb(name, shape, dt=F32):
            return ctx.enter_context(nc.sbuf_tensor(name, shape, dt))

        def sb_split(name, shape):
            whole = sb(name, shape)
            words = shape[-1] * (shape[1] if len(shape) == 3 else 1)
            return whole, nc.alloc_sbuf_tensor_at(name + "_r", [P, words], F32R, offset=nc.sbuf_base - 4 * words)

        def sem(name):
            return ctx.enter_context(nc.semaphore(name))

        class S:
            (in_x, in_const, in_cols, in_ctx0, in_ctx1, in_l0x) = (
                sem(n) for n in "in_x in_const in_cols in_ctx0 in_ctx1 in_l0x".split())
            (in_mask, in_rows, in_router, in_e8, in_l0a, moe_y) = (
                sem(n) for n in "in_mask in_rows in_router in_e8 in_l0a moe_y".split())
            (kv_psum, in_ctxt, in_l1x, in_l2x, out_psum, in_l2a) = (
                sem(n) for n in "kv_psum in_ctxt in_l1x in_l2x out_psum in_l2a".split())
            (att_s, in_late, in_l3x, t_h, in_l3a, stored) = (
                sem(n) for n in "att_s in_late in_l3x t_h in_l3a stored".split())
            (ln_var, ln_rstd, cln_var, cln_rstd, kv_k, kv_ss) = (
                sem(n) for n in "ln_var ln_rstd cln_var cln_rstd kv_k kv_ss".split())
            (kv_sq, hi_ready, lo_ready, t_nrm, t_nrmp, att_max) = (
                sem(n) for n in "kv_sq hi_ready lo_ready t_nrm t_nrmp att_max".split())
            (att_pt, att_exp, att_o, att_pta, top_gap, top_exp) = (
                sem(n) for n in "att_pt att_exp att_o att_pta top_gap top_exp".split())
            (moe_up, moe_h, moe_g, c_psum, c_act, kv_v) = (
                sem(n) for n in "moe_up moe_h moe_g c_psum c_act kv_v".split())
            (xn_psum, xn_act, qt_psum, qbd_ready, kt_psum, kt_act) = (
                sem(n) for n in "xn_psum xn_act qt_psum qbd_ready kt_psum kt_act".split())
            (sa_max, sa_exp, q16_split, q16_low, conv_max, conv_exp) = (
                sem(n) for n in "sa_max sa_exp q16_split q16_low conv_max conv_exp".split())
            (h1_psum, h1_act, h1_dve, t_a, t_sig, t_back) = (
                sem(n) for n in "h1_psum h1_act h1_dve t_a t_sig t_back".split())
            (t_backc, n_e, n_ec, n_m1, n_mc, n_u) = (
                sem(n) for n in "t_backc n_e n_ec n_m1 n_mc n_u".split())
            (n_uc, n_w, n_wc, m_h, m_hc, g_psum) = (
                sem(n) for n in "n_uc n_w n_wc m_h m_hc g_psum".split())
            (g_z, t_qkv, t_qk, t_kqt, t_kqtc, t_gram) = (
                sem(n) for n in "g_z t_qkv t_qk t_kqt t_kqtc t_gram".split())
            (t_gramc, t_b, t_x, t_xc, t_z, t_zc) = (
                sem(n) for n in "t_gramc t_b t_x t_xc t_z t_zc".split())
            (t_pred, t_e, t_et, t_etc, t_sh, t_dh) = (
                sem(n) for n in "t_pred t_e t_et t_etc t_sh t_dh".split())
            (t_da, t_s, t_tr, t_trp, n_ba, n_p) = (
                sem(n) for n in "t_da t_s t_tr t_trp n_ba n_p".split())
            (n_pc, n_m, t_r, t_rc, t_o, t_oc) = (
                sem(n) for n in "n_pc n_m t_r t_rc t_o t_oc".split())
            (dve_own, xh_ready, xt_psum, xt_ready, att_on, att_ptd) = (
                sem(n) for n in "dve_own xh_ready xt_psum xt_ready att_on att_ptd".split())
            (opt_psum, opt_ready, router_psum, comb_ready, moe_acc, combt_psum) = (
                sem(n) for n in "opt_psum opt_ready router_psum comb_ready moe_acc combt_psum".split())
            (combt_ready, b2_psum, xn_ready, xn_dve, q_norm, khat_ready) = (
                sem(n) for n in "combt_ready b2_psum xn_ready xn_dve q_norm khat_ready".split())
            (q_psum, kt_dve, sa_qkv, sa_q, sa_s, sa_norm) = (
                sem(n) for n in "q_psum kt_dve sa_qkv sa_q sa_s sa_norm".split())
            (sa_pt, sa_ptc, sa_ot, sa_otc, q16_psum, q16_ready) = (
                sem(n) for n in "sa_pt sa_ptc sa_ot sa_otc q16_psum q16_ready".split())
            (o16_psum, o16_ready, conv_s, conv_a, conv_at, conv_atc) = (
                sem(n) for n in "o16_psum o16_ready conv_s conv_a conv_at conv_atc".split())
            (conv_y, qa_psum, qa_ready, qlo_ready, ot_psum, ot_ready) = (
                sem(n) for n in "conv_y qa_psum qa_ready qlo_ready ot_psum ot_ready".split())
            (g_scan, g_back) = (
                sem(n) for n in "g_scan g_back".split())

        slot_full = [ctx.enter_context(nc.semaphore(f"slot_full{i}")) for i in range(SLOTS)]

        ring, ring_r = sb_split("ring", [P, SLOTS, UNIT])
        wa, wa_r = sb_split("wa", [P, L2A_N])
        wb = sb("wb", [P, L2X_N])
        ctxn = sb("ctxn", [P, KT * CD])
        ctxt, ctxt_r = sb_split("ctxt", [P, C * B * KEYS])
        scr, scr_r = sb_split("scr", [P, 11520])
        cols = sb("cols", [P, NCOLS])
        rows = sb("rows", [P, NROWS])
        cst = sb("cst", [P, NCONST])
        router = sb("router", [P, ROUTER])
        e8 = sb("e8", [E, 2 * D])
        x = sb("x", [P, D])
        xh = sb("xh", [P, D])
        xt = sb("xt", [P, C, P])
        sm = sb("sm", [P, 256])
        ps01 = ctx.enter_context(nc.psum_tensor("ps01", [P, 1024], F32))
        ps23 = ctx.enter_context(nc.psum_tensor("ps23", [P, 1024], F32))
        ps45 = ctx.enter_context(nc.psum_tensor("ps45", [P, 1024], F32))
        ps6 = ctx.enter_context(nc.psum_tensor("ps6", [P, 512], F32))
        ps7 = ctx.enter_context(nc.psum_tensor("ps7", [P, 512], F32))
        halves = [ps01[:, 0:512], ps01[:, 512:1024], ps23[:, 0:512], ps23[:, 512:1024],
                  ps45[:, 0:512], ps45[:, 512:1024]]

        def carve(tensor, at, *shape):
            n = 1
            for s in shape:
                n *= s
            v = tensor[:, at:at + n]
            names = "abcd"[:len(shape)]
            if len(shape) > 1:
                v = v.rearrange(f"p ({' '.join(names)}) -> p {' '.join(names)}",
                                **{k: s for k, s in zip(names, shape)})
            return v

        def weight(tensor, tab, name, *shape):
            at, n = tab[name]
            return carve(tensor, at, *shape)

        def col(name, i=0):
            at, _ = COLS[name]
            return cols[:, at + i:at + i + 1]

        def row(name):
            at, n = ROWS[name]
            return rows[:, at:at + n]

        ident, ones = cst[:, 0:128], cst[:, 128:256]
        iota8, parity, bits = cst[:, 256:264], cst[:, 264:266], cst[:, 266:272]
        nhalf, phalf, head8 = cst[:, 272:344], cst[:, 344:376], cst[:, 376:384]
        stat, mv, ve, rstd = sm[:, 0:6], sm[:, 6:8], sm[:, 8:9], sm[:, 9:10]

        NK = KEYS + P
        a, w, q = L0X_N, L0A_N, Views()
        xnt = carve(ctxt, 0, C, B * KEYS)
        q.kt, q.v = carve(scr, 0, C, (KT + 1) * P), carve(scr, 4352, KT + 1, D)
        q.sc, q.qbd, q.sq = carve(scr, 8704, 2, NK), carve(scr, 11008, B, C, P), carve(wb, w + 2 * NK + 2048, 2, D)
        q.knat, q.pt = carve(wa, a, KT + 1, D), carve(wa, a + 4352, 2, NK)
        q.stats, q.mv = carve(wa, a + 6656, KT, 6), carve(wa, a + 6752, KT, 2)
        q.cve, q.crs = carve(wa, a + 6784, KT), carve(wa, a + 6800, KT)
        q.ss, q.rs, q.rt = carve(wa, a + 6816, 72), carve(wa, a + 6888, 72), carve(sm, 160, 72)
        q.mask, q.mask8 = carve(wb, w, B, NK), wb[:, w + 2 * NK:w + 2 * NK + 512].bitcast(U8)
        q.xn = carve(wb, w + 2 * NK + 512, 8, CD)
        gain = sm[:, 40:41]
        att = Views()
        att.nmax = sm[:, 16:18]
        att.rsum = sm[:, 18:20]
        att.rinv = sm[:, 20:22]
        att.mx = sm[:, 22:24]

        late = ctxn

        r0 = Views()
        r0.qbd = carve(scr, 0, B, 4, P)
        r0.kt = carve(scr, 1024, P)
        r0.v = carve(scr, 1152, 64)
        r0.p = carve(scr, 1216, 4, B, LQ)
        r0.pt = carve(scr, 1728, 4, P)
        r0.ot = carve(scr, 2240, 4, P)
        r0.o = carve(scr, 2752, D)
        r0.mx = sm[:, 48:56]
        r0.sum = sm[:, 56:64]
        r0.rinv = sm[:, 64:72]
        flat = ring[:].rearrange("p s w -> p (s w)")
        n16 = Views()
        n16.kt = carve(scr, 3072, C, B * KEYS)
        n16.v = carve(scr, 7168, KT, D)
        n16.p = carve(wa, 8064, 2, KEYS)
        n16.pt = carve(wa, 4224, 2, KEYS)
        n16.qt = carve(wa, 6272, C, P)
        n16.o = carve(wa, 6528, C, B, P)
        n16.ot = carve(wa, 7040, C, P)
        n16.tmp = carve(wa, 7296, C, P)
        n16.h = carve(wa, 7552, 4, P)
        n16.qthi = carve(flat, 6144, C, P)
        n16.qtlo = carve(flat, 6400, C, P)
        n16.khi = carve(ring_r, 0, C, B * KEYS)
        n16.klo = carve(scr_r, 3072, C, B * KEYS)
        n16.qhi = carve(wa_r, 2176, C, B, 8, LQ)
        n16.qlo = carve(ring_r, 4096, C, B, 8, LQ)
        n64 = Views()
        n64.chi = carve(ring_r, 0, C, B * KEYS)
        n64.clo = carve(ctxt_r, 0, C, B * KEYS)
        n64.ahi = carve(ring_r, 4096, B, 16, LQ)
        n64.bhi = carve(ring_r, 6144, B, 16, LQ)
        n64.alo = carve(scr_r, 2048, B, 16, LQ)
        n64.blo = carve(scr_r, 4096, B, 16, LQ)
        n64.qz = carve(scr, 0, 8, 2, P)
        n64.opa = carve(scr, 0, B, 16, LQ)
        n64.qa = carve(scr, 2048, B, 16, LQ)
        n64.qb = carve(scr, 4096, B, 16, LQ)
        n64.opb = carve(scr, 4096, B, 16, LQ)
        n64.p = carve(scr, 6144, 2, KEYS)
        n64.pt = carve(scr, 8192, 2, KEYS)
        n64.o = carve(scr, 10240, 2, CD)
        n64.ot = carve(scr, 6144, 8, P)
        cv = Views()
        cv.w = carve(scr, 0, 32)
        cv.a = carve(scr, 64, 2, LQ)
        cv.b = carve(scr, 192, LQ)
        cv.nb = sm[:, 80:86]
        cv.full = carve(scr, 256, P)
        cv.at = carve(scr, 384, P)
        cv.mx = sm[:, 72:73]
        cv.sum = sm[:, 73:74]
        cv.rs = sm[:, 74:75]
        mo = Views()
        mo.g = carve(scr, 0, 2, FU)
        mo.h = carve(scr, 1024, 2, FU)
        mo.lg = sm[:, 96:104]
        mo.top = sm[:, 104:112]
        mo.idx = sm[:, 112:120].bitcast(U32)
        mo.idxf = sm[:, 120:128]
        mo.gap = sm[:, 128:130]
        mo.ex = sm[:, 130:132]
        mo.z = sm[:, 132:133]
        mo.rz = sm[:, 133:134]
        mo.wt = sm[:, 134:136]
        mo.c0 = sm[:, 136:144]
        mo.c1 = sm[:, 144:152]
        mo.comb = sm[:, 152:160]
        mo.combt = carve(scr, 2048, P)
        gr = Views()
        gr.e = carve(scr, 0, C, P)
        gr.z = carve(scr, 256, C, P)
        gr.a = carve(scr, 512, C, P)
        gr.b = carve(scr, 768, C, P)
        gr.h = carve(scr, 1024, C, P)
        gr.t = carve(scr, 1280, C, P)

        tt = Views()
        tt.qkv = carve(flat, 0, 3, D)
        tt.kqt = carve(flat, 768, 2, C, P)
        tt.gram = carve(flat, 1280, 2, P)
        tt.s = carve(flat, 1536, 8, P)
        tt.g = carve(flat, 2560, 8, P)
        tt.tb = carve(flat, 3584, 8, P)
        tt.w = carve(flat, 4608, 8, P)
        tt.h = carve(flat, 5632, 2, 8, P)
        tt.en = carve(flat, 7680, 2, D)
        tt.et = carve(flat, 8192, 2, C, P)
        tt.m = [[carve(flat, 8704 + (s * 3 + c) * 2 * P, 2, P) for c in range(3)] for s in range(2)]
        tt.sh = carve(flat, 10240, 2, P)
        tt.sgv = carve(flat, 10496, 2, P)
        tt.tmp = carve(flat, 10752, 6, P)
        tt.hn = carve(wb, L3X_N, 2, 8, P)
        tt.dan = carve(wb, L3X_N + 2048, 2, 8, P)
        tt.dbn = [carve(wa, 0, 8, P), carve(ctxn, 0, 8, P)]
        tt.u = [carve(ctxn, 1024 + c * 640, P) for c in range(3)]
        tt.wm = [carve(ctxn, 1152 + c * 640, P) for c in range(3)]
        tt.e = [carve(ctxn, 1280 + c * 640, 2, P) for c in range(3)]
        tt.pt = [carve(ctxn, 1536 + c * 640, P) for c in range(3)]
        tt.ai = xh[:, 0:P]
        tt.ss = sm[:, 160:192]
        tt.nr = sm[:, 192:224]
        tt.sc = xt[:, 0, 0:32]
        tt.nt = xt[:, 0, 32:64]
        tt.tr = sm[:, 224:227]
        tt.n2 = sm[:, 227:230]
        tt.n = sm[:, 230:233]
        tt.rn = sm[:, 233:236]
        tt.rn2 = sm[:, 236:239]
        ctxt3 = carve(ctxt, 0, C, B * KEYS)
        NS_A, NS_B, NS_C, NS_ITERS, LR = 3.4445, -4.775, 2.0315, 5, 0.1
        block = ctx.enter_context(nc.Block())

        @block.sync
        def _(sp):
            sp.dma_start(x[:], x_in).then_inc(S.in_x, 16)
            sp.dma_start(cst[:], const_in).then_inc(S.in_const, 16)
            sp.dma_start(cols[:], cols_in).then_inc(S.in_cols, 16)
            half = KTB * CD
            sp.dma_start(ctxn[:, 0:half], ctx_in[:, 0:half]).then_inc(S.in_ctx0, 16)
            sp.dma_start(ctxn[:, half:2 * half], ctx_in[:, half:2 * half]).then_inc(S.in_ctx1, 16)
            sp.dma_start(wa[:, 0:L0X_N], l0x_in).then_inc(S.in_l0x, 16)
            sp.dma_start(q.mask8, mask_in.partition_broadcast(P)).then_inc(S.in_mask, 16)
            sp.dma_start(rows[:], rows_in.partition_broadcast(P)).then_inc(S.in_rows, 16)
            sp.dma_start(router[:], router_in).then_inc(S.in_router, 16)
            sp.dma_start(e8[:], e8_in).then_inc(S.in_e8, 16)
            sp.dma_start(wb[:, 0:L0A_N], l0a_in).then_inc(S.in_l0a, 16)

            def units(m, source, first, n):
                width = source.shape[2]

                def lot(it):
                    for s in range(SLOTS):
                        if MOE_BASE[m] + first > 0:
                            sp.wait_ge(S.moe_y, MOE_BASE[m] - SLOTS + s + 1 + it * SLOTS)
                        k = it * SLOTS + s
                        unit = source[k] if isinstance(it, int) else \
                            source[bass.ds(k, 1)].rearrange("o p w -> (o p) w")
                        sp.dma_start(ring[:, s, 0:width], unit).then_inc(slot_full[s], 16)

                lots = range(first // SLOTS, (first + n) // SLOTS)
                if len(lots) == 1:
                    lot(lots[0])
                else:
                    with sp.Fori(lots[0], lots[-1] + 1) as it:
                        lot(it)

            units(0, m0_in, 0, 4)
            sp.wait_ge(S.kv_psum, KT + 1)
            sp.dma_start(ctxt[:], ctxt_in).then_inc(S.in_ctxt, 16)
            sp.dma_start(wa[:, 0:L1X_N], l1x_in).then_inc(S.in_l1x, 16)
            units(0, m0_in, 4, 4)
            sp.dma_start(wb[:], l2x_in).then_inc(S.in_l2x, 16)
            sp.wait_ge(S.out_psum, 3)
            units(1, m1_in, 0, 4)
            units(1, m1_in, 4, 12)
            sp.dma_start(wa[:, 0:L2A_N], l2a_in).then_inc(S.in_l2a, 16)
            sp.wait_ge(S.att_s, ATT_BASE["l2x"] + 16)
            sp.dma_start(ctxt[:], ctxt_in).then_inc(S.in_ctxt, 16)
            sp.wait_ge(S.out_psum, 4)
            sp.dma_start(late[:, 0:NLATE], late_in.partition_broadcast(P)).then_inc(S.in_late, 16)
            sp.dma_start(wb[:, 0:L3X_N], l3x_in).then_inc(S.in_l3x, 16)
            sp.wait_ge(S.t_h, 3)
            sp.dma_start(ring[:, 0, :], m2_in[0]).then_inc(slot_full[0], 16)
            sp.wait_ge(S.out_psum, 5)
            for s in range(1, SLOTS):
                sp.dma_start(ring[:, s, :], m2_in[s]).then_inc(slot_full[s], 16)
            units(2, m2_in, 4, 4)
            sp.wait_ge(S.out_psum, 6)
            sp.dma_start(wa[:, 0:L3A_N], l3a_in).then_inc(S.in_l3a, 16)
            units(3, m3_in, 0, 4)
            units(3, m3_in, 4, 12)
            sp.wait_ge(S.moe_acc, MOE_BASE[3] + MOE_UNITS[3])
            sp.dma_start(out, x[:]).then_inc(S.stored, 16)
            sp.wait_ge(S.stored, 16)

        @block.gpsimd
        def _(pool):
            pool.wait_ge(S.in_const, 16)

            def norms(first, n):
                for i in range(first, first + n):
                    pool.wait_ge(S.ln_var, i + 1)
                    nc.gpsimd.tensor_tensor(rstd, ve, nhalf[:, 0:1], ALU.pow).then_inc(S.ln_rstd, 1)

            norms(0, 2)
            for g in range(KT // 4):
                pool.wait_ge(S.cln_var, g + 1)
                nc.gpsimd.tensor_tensor(q.crs[:, 4 * g:4 * g + 4], q.cve[:, 4 * g:4 * g + 4], nhalf[:, 0:4], ALU.pow)\
                    .then_inc(S.cln_rstd, 1)
            for i in range(KT + 1):
                pool.wait_ge(S.kv_k, i + 1)
                if i >= 2:
                    pool.wait_ge(S.kv_ss, i - 1)
                kn = q.knat[:, L0X_ORDER[i], :]
                nc.gpsimd.tensor_tensor(q.sq[:, i % 2, :], kn, kn, ALU.mult).then_inc(S.kv_sq, 1)

            def low(n, lo, whole, hi):
                pool.wait_ge(S.hi_ready, n)
                nc.gpsimd.tensor_tensor(lo, whole, hi.bitcast(F32), ALU.subtract).then_inc(S.lo_ready, 1)

            def keys_low(i):
                for n in range(4):
                    k = slice((n % 2) * KEYS, (n % 2 + 1) * KEYS)
                    low(HI_BASE[i] + n + 1, n16.klo[:, n // 2, k], n16.kt[:, n // 2, k], n16.khi[:, n // 2, k])

            norms(2, 4)
            norms(6, 1)
            keys_low(0)
            norms(7, 2)
            norms(9, 1)
            for n in range(4):
                k = slice((n // 2) * KEYS, (n // 2 + 1) * KEYS)
                low(HI_BASE[1] + n + 1, n64.clo[:, n % 2, k], ctxt3[:, n % 2, k], n64.chi[:, n % 2, k])
            low(HI_BASE[1] + 9, n64.alo[:, 1], n64.qa[:, 1], n64.ahi[:, 1])
            low(HI_BASE[1] + 10, n64.blo[0:CB, 1], n64.qb[0:CB, 1], n64.bhi[0:CB, 1])
            norms(10, 1)
            for s in range(2):
                pool.wait_ge(S.t_nrm, s + 1)
                nc.gpsimd.tensor_tensor(tt.n, tt.n2, phalf[:, 0:3], ALU.pow).then_inc(S.t_nrmp, 1)
            norms(11, 2)
            keys_low(2)
            norms(13, 2)

        @block.scalar
        def _(act):
            def attention(stage, n, sc_of, p_of, pt_of):
                base = ATT_BASE[stage]
                for t in range(n + 1):
                    if t < n:
                        act.wait_ge(S.att_max, base + t + 1)
                        if t >= 2:
                            act.wait_ge(S.att_pt, base + t - 1)
                        nc.scalar.activation(p_of(t), sc_of(t), ACT.Exp, bias=att.nmax[:, t % 2:t % 2 + 1],
                                             accum_out=att.rsum[:, t % 2:t % 2 + 1]).then_inc(S.att_exp, 1)
                    if t >= 1:
                        act.wait_ge(S.att_pt, base + t)
                        if t >= 3:
                            act.wait_ge(S.att_o, base + t - 2)
                        nc.scalar.copy(pt_of(t - 1)[:, 0:512], ps45[:, 0:512]).then_inc(S.att_pta, 1)

            def mixture(m):
                base, nu = MOE_BASE[m], MOE_UNITS[m]
                act.wait_ge(S.top_gap, m + 1)
                nc.scalar.activation(mo.ex, mo.gap, ACT.Exp, accum_out=mo.z).then_inc(S.top_exp, 1)
                func = ACT.Gelu if m < 2 else ACT.Silu
                bias = (None, "l1f_b1", None, "l3f_b1")[m]

                def lot(it):
                    for s in range(SLOTS):
                        first = isinstance(it, int) and it == 0
                        k, par = it * SLOTS + s, s % 2
                        act.wait_ge(S.moe_up, base + s + 1 + it * SLOTS)
                        if m < 2:
                            if not (first and s < 2):
                                act.wait_ge(S.moe_y, base + s - 1 + it * SLOTS)
                            dst, done = mo.h, S.moe_h
                        else:
                            if not (first and s < 2):
                                act.wait_ge(S.moe_h, base + s - 1 + it * SLOTS)
                            dst, done = mo.g, S.moe_g
                        up = halves[par]
                        if bias is None:
                            nc.scalar.activation(dst[:, par, :], up, func).then_inc(done, 1)
                        else:
                            for fc in range(FC):
                                c = COLS[bias][0] + fc + s * FC + it * (SLOTS * FC)
                                ins = nc.scalar.activation(dst[:, par, fc * P:(fc + 1) * P], up[:, fc * P:(fc + 1) * P],
                                                           func, bias=cols[:, bass.ds(c, 1)])
                            ins.then_inc(done, 1)

                lot(0)
                if nu // SLOTS == 2:
                    lot(1)
                else:
                    with act.Fori(1, nu // SLOTS) as it:
                        lot(it)

            def context16(i, shares):
                for j in shares:
                    act.wait_ge(S.c_psum, 16 * i + j + 1)
                    src = halves[SHARE_BANKS[i][j]]
                    if j < 8:
                        c, kb = j // 4, j % 4
                        nc.scalar.activation(n16.kt[:, c, kb * 512:(kb + 1) * 512], src, ACT.Identity,
                                             bias=col(("l1x_bk", "l3x_bk")[i], c)).then_inc(S.c_act, 1)
                    else:
                        jj = j - 8
                        nc.scalar.copy(n16.v[:, 2 * jj:2 * jj + 2, :], src.rearrange("p (a d) -> p a d", a=2))\
                            .then_inc(S.c_act, 1)

            act.wait_ge(S.in_cols, 16)
            def keys_values(i):
                act.wait_ge(S.kv_psum, i + 1)
                j, src = L0X_ORDER[i], halves[2 + i % 2]
                nc.scalar.copy(q.knat[:, j, :], src[:, 0:D]).then_inc(S.kv_k, 1)
                nc.scalar.copy(q.v[:, j, :], src[:, D:2 * D]).then_inc(S.kv_v, 1)

            def rows_t(g):
                act.wait_ge(S.xn_psum, g + 1)
                nc.scalar.activation(xnt[0:CB, 1, g * 512:(g + 1) * 512], halves[1][0:CB, :], ACT.Identity,
                                     bias=col("l0x_xb", 1)[0:CB], scale=col("l0x_xg", 1)[0:CB]).then_inc(S.xn_act, 1)

            rows_t(0)
            keys_values(0)
            for g in range(1, KT // 4):
                rows_t(g)
                for i in range(4 * g - 3, 4 * g + 1):
                    keys_values(i)
            for i in range(KT - 3, KT + 1):
                keys_values(i)
            act.wait_ge(S.qt_psum, 1)
            src = ps6[:, 256:512].rearrange("p (c b k) -> p b c k", c=C, b=B)
            for i in range(2):
                for b in range(B):
                    h = slice(64 * i, 64 * i + 64)
                    ins = nc.scalar.activation(q.qbd[h, b, :, 64 * i:64 * i + 64], src[h, b], ACT.Identity, scale=gain[h])
            ins.then_inc(S.qbd_ready, 1)
            for g in (0, 1, 2, 3, 4, 5, 7):
                act.wait_ge(S.kt_psum, g + 1)
                first, n = L0X_GROUPS[g]
                nc.scalar.copy(q.kt[:, :, first * P:(first + n) * P],
                               halves[4 + g % 2][:, 0:2 * n * P].rearrange("p (c k) -> p c k", c=C)).then_inc(S.kt_act, 1)
            attention("l0x", 4, lambda t: q.sc[:, t % 2, :], lambda t: q.sc[:, t % 2, :],
                      lambda t: q.pt[:, t % 2, :])
            context16(0, range(0, 7))
            act.wait_ge(S.sa_max, 1)
            nc.scalar.activation(r0.p, r0.p, ACT.Exp).then_inc(S.sa_exp, 1)
            context16(0, range(7, 16))
            mixture(0)

            def keys_high(i, base):
                act.wait_ge(S.moe_y, base)
                for n in range(4):
                    k = slice((n % 2) * KEYS, (n % 2 + 1) * KEYS)
                    nc.scalar.copy(n16.khi[:, n // 2, k], n16.kt[:, n // 2, k]).then_inc(S.hi_ready, 1)

            def queries_low(i):
                act.wait_ge(S.q16_split, i + 1)
                for j in range(8):
                    nc.scalar.activation(n16.qlo[:, :, :, j, :], n16.qtlo.rearrange("p c (b k) -> p c b k", b=B),
                                         ACT.Identity, scale=head8[:, j:j + 1]).then_inc(S.q16_low, 1)

            def scores(t):
                return ps01[:] if t % 2 == 0 else ps23[:]

            keys_high(0, MOE_BASE[1])
            queries_low(0)
            attention("l1x", 16, scores, lambda t: n16.p[:, t % 2, :], lambda t: n16.pt[:, t % 2, :])
            act.wait_ge(S.conv_max, 1)
            nc.scalar.activation(cv.w, cv.w, ACT.Exp, bias=cv.mx, accum_out=cv.sum).then_inc(S.conv_exp, 1)
            mixture(1)
            act.wait_ge(S.moe_y, MOE_BASE[2])
            for n in range(4):
                k = slice((n // 2) * KEYS, (n // 2 + 1) * KEYS)
                nc.scalar.copy(n64.chi[:, n % 2, k], ctxt3[:, n % 2, k]).then_inc(S.hi_ready, 1)
            for hh in range(2):
                act.wait_ge(S.h1_psum, hh + 1)
                for b in range(B):
                    src = ps45[0:CB, :].rearrange("p (h b q) -> p h b q", b=B, q=LQ)[:, :, b, :]
                    dst = n64.qb[0:CB, b, 8 * hh:8 * hh + 8, :]
                    nc.scalar.copy(dst, src).then_inc(S.h1_act, 1)
                act.wait_ge(S.h1_act, (hh + 1) * B)
                act.wait_ge(S.h1_dve, (hh + 1) * B)
                for b, heads in ((0, slice(8 * hh, 8 * hh + 8)), (1, slice(0, 16)))[0:hh + 1]:
                    nc.scalar.copy(n64.ahi[:, b, heads], n64.qa[:, b, heads]).then_inc(S.hi_ready, 1)
                    nc.scalar.copy(n64.bhi[0:CB, b, heads], n64.qb[0:CB, b, heads]).then_inc(S.hi_ready, 1)
            attention("l2x", 16, scores, lambda t: n64.p[:, t % 2, :], lambda t: n64.pt[:, t % 2, :])
            context16(1, range(0, 6))
            for s in range(2):
                act.wait_ge(S.t_a, s + 1)
                nc.scalar.activation(tt.s, ps01[:].rearrange("p (f k) -> p f k", f=8), ACT.Sigmoid)\
                    .then_inc(S.t_sig, 1)
                context16(1, range(6 + 2 * s, 7 + 2 * s))
                act.wait_ge(S.t_back, 3 * s + 1)
                nc.scalar.copy(tt.hn[:, s], ps45[:].rearrange("p (f k) -> p f k", f=8)).then_inc(S.t_backc, 1)
                context16(1, range(7 + 2 * s, 8 + 2 * s))
                act.wait_ge(S.t_back, 3 * s + 2)
                nc.scalar.copy(tt.dan[:, s], ps23[:].rearrange("p (f k) -> p f k", f=8)).then_inc(S.t_backc, 1)
                act.wait_ge(S.t_back, 3 * s + 3)
                nc.scalar.copy(tt.dbn[s], ps45[:].rearrange("p (f k) -> p f k", f=8)).then_inc(S.t_backc, 1)
                n1 = 3 * NS_ITERS * s + 1
                for c in range(3):
                    act.wait_ge(S.n_e, n1 + c)
                    nc.scalar.copy(tt.e[c], halves[c][:, 2 * P:4 * P].rearrange("p (a k) -> p a k", a=2))\
                        .then_inc(S.n_ec, 1)
                for c in range(3):
                    act.wait_ge(S.n_m1, 3 * s + 1 + c)
                    nc.scalar.activation(tt.m[s][c], tt.m[s][c], ACT.Identity, scale=tt.rn[:, c:c + 1])\
                        .then_inc(S.n_mc, 1)
                with act.Fori(0, NS_ITERS - 1) as it:
                    n0 = 3 * (NS_ITERS - 1) * s + 1
                    for c in range(3):
                        act.wait_ge(S.n_u, n0 + c + it * 3)
                        nc.scalar.copy(tt.u[c], halves[c][:, 0:P]).then_inc(S.n_uc, 1)
                    for c in range(3):
                        act.wait_ge(S.n_w, n0 + c + it * 3)
                        nc.scalar.copy(tt.wm[c], halves[c][:, P:2 * P]).then_inc(S.n_wc, 1)
                    for c in range(3):
                        act.wait_ge(S.n_e, n1 + 3 + c + it * 3)
                        nc.scalar.copy(tt.e[c], halves[c][:, 2 * P:4 * P].rearrange("p (a k) -> p a k", a=2))\
                            .then_inc(S.n_ec, 1)
            act.wait_ge(S.t_a, 3)
            nc.scalar.activation(tt.s, ps01[:].rearrange("p (f k) -> p f k", f=8), ACT.Sigmoid).then_inc(S.t_sig, 1)
            context16(1, range(10, 11))
            context16(1, range(11, 14))
            mixture(2)
            context16(1, range(14, 16))
            keys_high(2, MOE_BASE[3])
            queries_low(1)
            attention("l3x", 16, scores, lambda t: n16.p[:, t % 2, :], lambda t: n16.pt[:, t % 2, :])
            for f in range(4):
                act.wait_ge(S.m_h, 1)
                ins = nc.scalar.activation(n16.h[:, f, :], halves[0][:, f * P:(f + 1) * P], ACT.Relu,
                                           bias=col("l3x_b1", f))
            ins.then_inc(S.m_hc, 1)
            for c in range(C):
                act.wait_ge(S.g_psum, 1)
                ins = nc.scalar.activation(gr.z[:, c, :], ps01[:, c * P:(c + 1) * P], ACT.Sigmoid,
                                           bias=col("l3a_bz", c))
            ins.then_inc(S.g_z, 1)
            mixture(3)

        def ttt(dve, own, bc, inverse_sqrt):
            eight = lambda t: t.rearrange("p (f k) -> p f k", f=8)
            dve.wait_ge(S.t_qkv, 1)
            dve.wait_ge(S.in_late, 16)
            lt = lambda name: late[:, LATE[name][0]:LATE[name][0] + LATE[name][1]]
            flat = tt.qkv.rearrange("p a d -> p (a d)")
            own(nc.vector.tensor_tensor(flat, ps01[:, 0:3 * D], lt("qkvb"), ALU.add))
            own.wait()
            qk, sq = flat[:, 0:2 * D], tt.w.rearrange("p f k -> p (f k)")[:, 0:2 * D]
            own(nc.vector.tensor_tensor(sq, qk, qk, ALU.mult))
            own.wait()
            own(nc.vector.tensor_reduce(tt.ss, sq.rearrange("p (h d) -> p h d", d=16), AX.X, ALU.add))
            own.wait()
            own(nc.vector.tensor_scalar(tt.sc, tt.ss, 1e-30, None, ALU.max))
            own.wait()
            inverse_sqrt(tt.nr, tt.sc, tt.nt)
            own(nc.vector.tensor_tensor(tt.nr, tt.nr, tt.ss, ALU.mult))
            own.wait()
            own(nc.vector.tensor_scalar(tt.nr, tt.nr, 1e-6, None, ALU.add))
            own.wait()
            own(nc.vector.reciprocal(tt.nr, tt.nr))
            own.wait()
            qk3 = qk.rearrange("p (h d) -> p h d", d=16)
            own(nc.vector.tensor_tensor(qk3, qk3, bc(tt.nr, 16), ALU.mult))
            own.wait()
            for i, (g, b) in enumerate((("qs", "qb"), ("ks", "kb"))):
                half = tt.qkv[:, i, :].rearrange("p (h d) -> p h d", d=16)
                own(nc.vector.tensor_tensor(half, half, lt(g).unsqueeze(1).broadcast_to([P, 16, 16]), ALU.mult))
                own.wait()
                nc.vector.tensor_tensor(half, half, lt(b).unsqueeze(1).broadcast_to([P, 16, 16]), ALU.add)\
                    .then_inc(S.t_qk, 1)
            dve.wait_ge(S.t_kqt, 1)
            nc.vector.tensor_copy(tt.kqt, ps6[:, 0:512].rearrange("p (a c k) -> p a c k", a=2, c=C)).then_inc(S.t_kqtc, 1)
            dve.wait_ge(S.t_gram, 1)
            nc.vector.tensor_copy(tt.gram, ps7[:, 0:2 * P].rearrange("p (a k) -> p a k", a=2)).then_inc(S.t_gramc, 1)
            own(nc.vector.tensor_scalar(tt.ai, ident, NS_A, None, ALU.mult))
            a8, b8, w8 = eight(ps01[:]), eight(ps23[:]), tt.w
            for s in range(2):
                dve.wait_ge(S.t_sig, s + 1)
                own(nc.vector.tensor_tensor(tt.g, tt.s, a8, ALU.mult))
                own.wait()
                dve.wait_ge(S.t_b, s + 1)
                nc.vector.tensor_tensor(tt.h[:, s], tt.g, b8, ALU.mult).then_inc(S.t_h, 1)
                own(nc.vector.scalar_tensor_tensor(w8, tt.g, 1.0, tt.s, ALU.subtract, ALU.mult))
                own.wait()
                own(nc.vector.tensor_tensor(tt.tb, tt.g, w8, ALU.subtract))
                own.wait()
                own(nc.vector.tensor_tensor(tt.tb, tt.tb, b8, ALU.mult))
                if s == 1:
                    dve.wait_ge(S.t_x, 1)
                    nc.vector.tensor_copy(tt.tmp[:, 2], ps7[:, 0:P]).then_inc(S.t_xc, 1)
                    dve.wait_ge(S.t_z, 1)
                    nc.vector.tensor_scalar(tt.tmp[:, 3], ps7[:, P:2 * P], -LR, None, ALU.mult).then_inc(S.t_zc, 1)
                dve.wait_ge(S.t_pred, s + 1)
                own(nc.vector.tensor_tensor(tt.en[:, s], ps6[:, 0:D], tt.qkv[:, 2, :], ALU.subtract))
                own.wait()
                nc.vector.tensor_scalar(tt.en[:, s], tt.en[:, s], 2.0 / (P * D), None, ALU.mult).then_inc(S.t_e, 1)
                dve.wait_ge(S.t_et, s + 1)
                nc.vector.tensor_copy(tt.et[:, s], ps6[:, D:2 * D].rearrange("p (c k) -> p c k", c=C)).then_inc(S.t_etc, 1)
                if s == 1:
                    dve.wait_ge(S.t_x, 2)
                    nc.vector.tensor_copy(tt.tmp[:, 4], ps7[:, 0:P]).then_inc(S.t_xc, 1)
                    dve.wait_ge(S.t_z, 2)
                    nc.vector.tensor_scalar(tt.tmp[:, 5], ps7[:, P:2 * P], -LR, None, ALU.mult).then_inc(S.t_zc, 1)
                dve.wait_ge(S.t_sh, s + 1)
                own(nc.vector.tensor_copy(tt.sh, ps7[:, 2 * P:4 * P].rearrange("p (a k) -> p a k", a=2)))
                dve.wait_ge(S.t_dh, s + 1)
                own.wait()
                own(nc.vector.tensor_tensor(tt.tb, tt.tb, a8, ALU.mult))
                nc.vector.tensor_tensor(tt.w, tt.g, a8, ALU.mult).then_inc(S.t_da, 1)
                dve.wait_ge(S.t_s, s + 1)
                own(nc.vector.tensor_copy(tt.sgv, ps6[:, 0:2 * P].rearrange("p (a k) -> p a k", a=2)))
                own.wait()
                for c, (sc, cc) in enumerate(((tt.sgv[:, 0], tt.gram[:, 0]), (tt.sgv[:, 1], tt.gram[:, 0]),
                                              (tt.sh[:, 0], tt.sh[:, 1]))):
                    ins = nc.vector.tensor_tensor_reduce(tt.tmp[:, c], sc, cc, 1.0, 0.0, ALU.mult, ALU.add,
                                                         tt.tr[:, c:c + 1])
                ins.then_inc(S.t_tr, 1)
                dve.wait_ge(S.t_trp, s + 1)
                nc.vector.tensor_copy(tt.n2, ps7[:, 0:3]).then_inc(S.t_nrm, 1)
                dve.wait_ge(S.t_nrmp, s + 1)
                own(nc.vector.tensor_scalar(tt.n, tt.n, 1e-7, None, ALU.add))
                own.wait()
                own(nc.vector.reciprocal(tt.rn, tt.n))
                own.wait()
                own(nc.vector.tensor_tensor(tt.rn2, tt.rn, tt.rn, ALU.mult))
                own.wait()
                for c in range(3):
                    nc.vector.tensor_scalar(tt.wm[c], (tt.sgv[:, 0], tt.sgv[:, 1], tt.sh[:, 0])[c], tt.rn2[:, c:c + 1],
                                            None, ALU.mult).then_inc(S.n_wc, 1)
                n1 = 3 * NS_ITERS * s + 1
                for c in range(3):
                    dve.wait_ge(S.n_ec, n1 + c)
                    nc.vector.scalar_tensor_tensor(tt.tmp[:, 2 * c:2 * c + 2], tt.e[c], NS_B,
                                                   tt.ai.unsqueeze(1).broadcast_to([P, 2, P]), ALU.mult, ALU.add)\
                        .then_inc(S.n_ba, 1)
                for c in range(3):
                    dve.wait_ge(S.n_p, n1 + c)
                    dve.wait_ge(S.n_ba, n1 + c)
                    nc.vector.scalar_tensor_tensor(tt.m[s][c], halves[3 + c][:, 0:2 * P].rearrange("p (a k) -> p a k", a=2),
                                                   NS_C, tt.tmp[:, 2 * c:2 * c + 2], ALU.mult, ALU.add).then_inc(S.n_m1, 1)
                with dve.Fori(0, NS_ITERS - 1) as it:
                    n0 = 3 * (NS_ITERS - 1) * s + 1
                    for c in range(3):
                        dve.wait_ge(S.n_ec, n1 + 3 + c + it * 3)
                        nc.vector.scalar_tensor_tensor(tt.u[c], tt.e[c][:, 1], NS_B, tt.ai, ALU.mult, ALU.add)\
                            .then_inc(S.n_ba, 1)
                    for c in range(3):
                        dve.wait_ge(S.n_p, n1 + 3 + c + it * 3)
                        dve.wait_ge(S.n_ba, n1 + 3 + c + it * 3)
                        nc.vector.scalar_tensor_tensor(tt.pt[c], halves[3 + c][:, 0:P], NS_C, tt.u[c],
                                                       ALU.mult, ALU.add).then_inc(S.n_pc, 1)
                    for c in range(3):
                        dve.wait_ge(S.n_m, n0 + c + it * 3)
                        nc.vector.tensor_copy(tt.m[s][c], halves[3 + c][:, P:3 * P].rearrange("p (a k) -> p a k", a=2))\
                            .then_inc(S.n_mc, 1)
                if s == 0:
                    dve.wait_ge(S.t_r, 1)
                    nc.vector.tensor_scalar(tt.tmp[:, 0:2], ps6[:, 0:2 * P].rearrange("p (a k) -> p a k", a=2), -LR, None,
                                            ALU.mult).then_inc(S.t_rc, 1)
                else:
                    dve.wait_ge(S.t_r, 2)
                    nc.vector.tensor_scalar(tt.tmp[:, 0:4], ps6[:, 0:4 * P].rearrange("p (a k) -> p a k", a=4), -LR, None,
                                            ALU.mult).then_inc(S.t_rc, 1)
            dve.wait_ge(S.t_sig, 3)
            own(nc.vector.tensor_tensor(tt.g, tt.s, a8, ALU.mult))
            own.wait()
            dve.wait_ge(S.t_b, 3)
            nc.vector.tensor_tensor(tt.tb, tt.g, b8, ALU.mult).then_inc(S.t_h, 1)
            dve.wait_ge(S.t_x, 3)
            nc.vector.tensor_copy(tt.tmp[:, 4:6], ps7[:, 0:2 * P].rearrange("p (a k) -> p a k", a=2)).then_inc(S.t_xc, 1)
            dve.wait_ge(S.t_z, 3)
            nc.vector.tensor_scalar(tt.tmp[:, 0:2], ps7[:, 2 * P:4 * P].rearrange("p (a k) -> p a k", a=2), -LR, None,
                                    ALU.mult).then_inc(S.t_zc, 1)
            dve.wait_ge(S.t_o, 1)
            nc.vector.tensor_copy(tt.et[:, 0], ps45[:, 0:D].rearrange("p (c k) -> p c k", c=C)).then_inc(S.t_oc, 1)

        @block.vector
        def _(dve):
            own = Own(dve, S.dve_own)

            def bc(ap, n):
                return ap.unsqueeze(2).broadcast_to([P, ap.shape[1], n])

            def inverse_sqrt(y, v, t):
                own(nc.vector.tensor_scalar(t.bitcast(I32), v.bitcast(I32), 1, None, ALU.logical_shift_right))
                own.wait()
                own(nc.vector.tensor_scalar(y.bitcast(I32), t.bitcast(I32), -1, 0x5f3759df, ALU.mult, ALU.add))
                own.wait()
                for _ in range(3):
                    own(nc.vector.tensor_tensor(t, y, y, ALU.mult))
                    own.wait()
                    own(nc.vector.scalar_tensor_tensor(t, t, -0.5, v, ALU.mult, ALU.mult))
                    own.wait()
                    own(nc.vector.scalar_tensor_tensor(y, t, 1.5, y, ALU.add, ALU.mult))
                    own.wait()

            def norm(n, src, dst):
                own(nc.vector.bn_stats(stat, src))
                own.wait()
                own(nc.vector.bn_aggr(mv, stat))
                own.wait()
                nc.vector.tensor_scalar(ve, mv[:, 1:2], LN_EPS, None, ALU.add).then_inc(S.ln_var, 1)
                dve.wait_ge(S.ln_rstd, n + 1)
                nc.vector.tensor_scalar(dst, src, mv[:, 0:1], rstd, ALU.subtract, ALU.mult).then_inc(S.xh_ready, 1)
                dve.wait_ge(S.xh_ready, n + 1)

            def tokens_t(stage, gain=None, bias=None):
                dve.wait_ge(S.xt_psum, stage + 1)
                if gain is None:
                    nc.vector.tensor_copy(xt[:], ps7[:, 0:D].rearrange("p (c k) -> p c k", c=C)).then_inc(S.xt_ready, 1)
                else:
                    own(nc.vector.tensor_scalar(xt[:, 0, :], ps7[:, 0:P], col(gain, 0), col(bias, 0), ALU.mult, ALU.add))
                    own.wait()
                    nc.vector.tensor_scalar(xt[:, 1, :], ps7[:, P:D], col(gain, 1), col(bias, 1), ALU.mult, ALU.add)\
                        .then_inc(S.xt_ready, 1)

            def residual(k, src, bias):
                if k == 1:
                    dve.wait_ge(S.in_rows, 16)
                own(nc.vector.tensor_tensor(x[:], x[:], row(bias), ALU.add))
                own.wait()
                dve.wait_ge(S.out_psum, k)
                own(nc.vector.tensor_tensor(x[:], x[:], src, ALU.add))
                own.wait()

            def attention(stage, n, take_max, pt_of, o_of, width, post=None):
                base = ATT_BASE[stage]
                for t in range(n + 2 + (post is not None)):
                    if t < n:
                        take_max(t)
                    if 1 <= t <= n:
                        u = t - 1
                        dve.wait_ge(S.att_exp, base + t)
                        if u >= 2:
                            dve.wait_ge(S.att_on, base + u - 1)
                        own(nc.vector.reciprocal(att.rinv[:, u % 2:u % 2 + 1], att.rsum[:, u % 2:u % 2 + 1]))
                        own.wait()
                        dve.wait_ge(S.att_pt, base + t)
                        if t >= 3:
                            dve.wait_ge(S.att_o, base + t - 2)
                        if stage == "l0x":
                            nc.vector.tensor_copy(pt_of(u)[:, 1024:1152], halves[3][:, 0:P])
                        nc.vector.tensor_copy(pt_of(u)[:, 512:1024], ps45[:, 512:1024]).then_inc(S.att_ptd, 1)
                    if post is not None and 3 <= t:
                        u = t - 3
                        dve.wait_ge(S.opt_psum, OPT_BASE[stage] + u + 1)
                        post(u).then_inc(S.opt_ready, 1)
                    if 2 <= t < n + 2:
                        u = t - 2
                        dve.wait_ge(S.att_o, base + t - 1)
                        nc.vector.tensor_scalar(o_of(u), ps6[:, 0:width],
                                                att.rinv[:, u % 2:u % 2 + 1], None, ALU.mult).then_inc(S.att_on, 1)

            def plain_max(base, scores):
                def take(t):
                    dve.wait_ge(S.att_s, base + t + 1)
                    nc.vector.tensor_reduce(att.nmax[:, t % 2:t % 2 + 1], scores(t), AX.X, ALU.max, negate=True)\
                        .then_inc(S.att_max, 1)
                return take

            def mixture(m):
                base, nu = MOE_BASE[m], MOE_UNITS[m]
                dve.wait_ge(S.router_psum, m + 1)
                if m == 3:
                    own(nc.vector.tensor_tensor(mo.lg, ps7[:, 256:264], row("l3f_bg"), ALU.add))
                else:
                    own(nc.vector.tensor_copy(mo.lg, ps7[:, 256:264]))
                own.wait()
                own(nc.vector.max(mo.top, mo.lg))
                own.wait()
                own(nc.vector.max_index(mo.idx, mo.top, mo.lg))
                nc.vector.tensor_scalar(mo.gap, mo.top[:, 0:2], mo.top[:, 0:1], None, ALU.subtract).then_inc(S.top_gap, 1)
                own.wait()
                own(nc.vector.tensor_copy(mo.idxf, mo.idx))
                dve.wait_ge(S.top_exp, m + 1)
                own(nc.vector.reciprocal(mo.rz, mo.z))
                own.wait()
                own(nc.vector.tensor_scalar(mo.wt, mo.ex, mo.rz, None, ALU.mult))
                own.wait()
                own(nc.vector.tensor_scalar(mo.c0, iota8, mo.idxf[:, 0:1], mo.wt[:, 0:1], ALU.is_equal, ALU.mult))
                own(nc.vector.tensor_scalar(mo.c1, iota8, mo.idxf[:, 1:2], mo.wt[:, 1:2], ALU.is_equal, ALU.mult))
                own.wait()
                nc.vector.tensor_tensor(mo.comb, mo.c0, mo.c1, ALU.add).then_inc(S.comb_ready, 1)
                dve.wait_ge(S.comb_ready, m + 1)

                def add_unit(k_mod, prev_s, it, acc_value):
                    e = prev_s // (nu // E) + it * (SLOTS // (nu // E))
                    dve.wait_ge(S.moe_y, acc_value)
                    if not (isinstance(acc_value, int) and acc_value == 1):
                        dve.wait_ge(S.moe_acc, acc_value - 1)
                    nc.vector.scalar_tensor_tensor(x[:], halves[4 + k_mod][:, 0:D], mo.comb[:, bass.ds(e, 1)], x[:],
                                                   ALU.mult, ALU.add).then_inc(S.moe_acc, 1)

                def lot(it):
                    for s in range(SLOTS):
                        first = isinstance(it, int) and it == 0
                        par = s % 2
                        if m >= 2:
                            dve.wait_ge(S.moe_g, (0, 0, 0, 8)[m] + s + 1 + it * SLOTS)
                            if not (first and s < 2):
                                dve.wait_ge(S.moe_y, base + s - 1 + it * SLOTS)
                            up = halves[2 + par]
                            if m == 2:
                                nc.vector.tensor_tensor(mo.h[:, par, :], mo.g[:, par, :], up, ALU.mult)\
                                    .then_inc(S.moe_h, 1)
                            else:
                                for fc in range(FC):
                                    c = COLS["l3f_b0"][0] + fc + s * FC + it * (SLOTS * FC)
                                    f = slice(fc * P, (fc + 1) * P)
                                    ins = nc.vector.scalar_tensor_tensor(
                                        mo.h[:, par, f], up[:, f], cols[:, bass.ds(c, 1)], mo.g[:, par, f],
                                        ALU.add, ALU.mult)
                                ins.then_inc(S.moe_h, 1)
                        if not (first and s == 0):
                            prev = (s - 1) % SLOTS
                            add_unit(1 - par, prev, it if s else it - 1, base + s + it * SLOTS)

                lot(0)
                if m in (1, 3):
                    dve.wait_ge(S.combt_psum, m // 2 + 1)
                    nc.vector.tensor_copy(mo.combt[0:E, :], ps7[0:E, 264:264 + P]).then_inc(S.combt_ready, 1)
                    dve.wait_ge(S.b2_psum, m // 2 + 1)
                    dve.wait_ge(S.moe_acc, base + SLOTS - 1)
                    own(nc.vector.tensor_tensor(x[:], x[:], ps7[:, 0:D], ALU.add))
                    own.wait()
                if nu // SLOTS == 2:
                    lot(1)
                else:
                    with dve.Fori(1, nu // SLOTS) as it:
                        lot(it)
                add_unit(1, SLOTS - 1, nu // SLOTS - 1, base + nu)
                dve.wait_ge(S.moe_acc, base + nu)

            dve.wait_ge(S.in_x, 16)
            norm(0, x[:], xh[:])
            norm(1, xh[:], xh[:])
            dve.wait_ge(S.in_cols, 16)
            tokens_t(0, "l0x_lg", "l0x_lb")
            own(nc.vector.tensor_scalar(gain, col("l0x_qg"), col("l0x_kg"), 64 ** -0.5, ALU.mult, ALU.mult))
            own(nc.vector.memset(q.qbd, 0.0))

            def row_stats(g):
                dve.wait_ge((S.in_ctx0, S.in_ctx1)[g // 2], 16)
                for j in range(4 * g, 4 * g + 4):
                    own(nc.vector.bn_stats(q.stats[:, j, :], ctxn[:, j * CD:(j + 1) * CD]))
                own.wait()
                for j in range(4 * g, 4 * g + 4):
                    own(nc.vector.bn_aggr(q.mv[:, j, :], q.stats[:, j, :]))
                own.wait()
                nc.vector.tensor_scalar(q.cve[:, 4 * g:4 * g + 4], q.mv[:, 4 * g:4 * g + 4, 1], LN_EPS, None, ALU.add)\
                    .then_inc(S.cln_var, 1)

            def norm_rows(g):
                dve.wait_ge(S.cln_rstd, g + 1)
                if g >= 2:
                    dve.wait_ge(S.xn_psum, g - 1)
                for j in range(4 * g, 4 * g + 4):
                    nc.vector.tensor_scalar(q.xn[:, j % 8, :], ctxn[:, j * CD:(j + 1) * CD], q.mv[:, j, 0:1],
                                            q.crs[:, j:j + 1], ALU.subtract, ALU.mult).then_inc(S.xn_ready, 1)

            def rows_t(g):
                dve.wait_ge(S.xn_psum, g + 1)
                nc.vector.tensor_scalar(xnt[:, 0, g * 512:(g + 1) * 512], halves[0], col("l0x_xg"), col("l0x_xb"),
                                        ALU.mult, ALU.add).then_inc(S.xn_dve, 1)

            def key_squares(places):
                for i in places:
                    dve.wait_ge(S.kv_sq, i + 1)
                    nc.vector.tensor_reduce(q.ss[:, 4 * i + 4:4 * i + 8], q.sq[:, i % 2, :].rearrange("p (h d) -> p h d", h=4),
                                            AX.X, ALU.add).then_inc(S.kv_ss, 1)

            def norm_keys(k, places):
                dve.wait_ge(S.kv_ss, places[-1] + 1)
                own(nc.vector.tensor_scalar(q.ss[:, k], q.ss[:, k], 1.0 / 64, 1e-16, ALU.mult, ALU.max))
                own.wait()
                inverse_sqrt(q.rs[:, k], q.ss[:, k], q.rt[:, k])
                if places[0] == 0:
                    nc.vector.tensor_tensor(xh[:].rearrange("p (h d) -> p h d", h=4), xh[:].rearrange("p (h d) -> p h d", h=4),
                                            bc(q.rs[:, 0:4], 64), ALU.mult).then_inc(S.q_norm, 1)
                for i in places:
                    kn = q.knat[:, L0X_ORDER[i], :].rearrange("p (h d) -> p h d", h=4)
                    nc.vector.tensor_tensor(kn, kn, bc(q.rs[:, 4 * i + 4:4 * i + 8], 64), ALU.mult).then_inc(S.khat_ready, 1)

            row_stats(0)
            row_stats(1)
            norm_rows(0)
            row_stats(2)
            norm_rows(1)
            row_stats(3)
            rows_t(0)
            norm_rows(2)
            rows_t(1)
            norm_rows(3)
            dve.wait_ge(S.q_psum, 1)
            own(nc.vector.tensor_copy(xh[:], ps6[:, 0:D]))
            own.wait()
            own(nc.vector.tensor_tensor(q.kt[:, 0, 0:D], xh[:], xh[:], ALU.mult))
            own.wait()
            own(nc.vector.tensor_reduce(q.ss[:, 0:4], q.kt[:, 0, 0:D].rearrange("p (h d) -> p h d", h=4), AX.X, ALU.add))
            own.wait()
            key_squares(range(0, 3))
            rows_t(2)
            dve.wait_ge(S.in_mask, 16)
            own(nc.vector.tensor_scalar(q.mask[:, :, 0:KEYS], q.mask8.rearrange("p (b k) -> p b k", b=B),
                                        -MASKED, MASKED, ALU.mult, ALU.add))
            own(nc.vector.memset(q.mask[:, :, KEYS:NK], MASKED))
            own.wait()
            for b in range(B):
                own(nc.vector.memset(q.mask[:, b, KEYS + b * LQ:KEYS + (b + 1) * LQ], 0.0))
            key_squares(range(3, 7))
            rows_t(3)
            key_squares(range(7, 11))
            norm_keys(slice(0, 48), range(0, 11))
            key_squares(range(11, KT + 1))
            norm_keys(slice(48, 72), range(11, KT + 1))
            for g in (6, 8):
                dve.wait_ge(S.kt_psum, g + 1)
                first, n = L0X_GROUPS[g]
                nc.vector.tensor_copy(q.kt[:, :, first * P:(first + n) * P],
                                      halves[4 + g % 2][:, 0:2 * n * P].rearrange("p (c k) -> p c k", c=C))\
                    .then_inc(S.kt_dve, 1)

            def masked_max(t):
                dve.wait_ge(S.att_s, t + 1)
                if t >= 2:
                    dve.wait_ge(S.att_pt, t - 1)
                if t >= 1:
                    dve.wait_ge(S.att_max, t)
                b = t // 2
                own(nc.vector.tensor_tensor_reduce(q.sc[:, t % 2, 0:KEYS], ps01[:], q.mask[:, b, 0:KEYS],
                                                   1.0, NEG, ALU.add, ALU.max, att.mx[:, 0:1]))
                own(nc.vector.tensor_tensor_reduce(q.sc[:, t % 2, KEYS:NK], halves[2][:, 0:P],
                                                   q.mask[:, b, KEYS:NK], 1.0, NEG, ALU.add, ALU.max, att.mx[:, 1:2]))
                own.wait()
                nc.vector.tensor_reduce(att.nmax[:, t % 2:t % 2 + 1], att.mx, AX.X, ALU.max, negate=True)\
                    .then_inc(S.att_max, 1)

            def heads_back(u):
                b, hp = u // 2, u % 2
                for j in range(2):
                    h = slice(64 * j, 64 * j + 64)
                    ins = nc.vector.tensor_copy(xt[h, hp, b * LQ:(b + 1) * LQ], ps7[h, 64 * j:64 * j + 64])
                return ins

            attention("l0x", 4, masked_max, lambda t: q.pt[:, t % 2, :],
                      lambda t: xh[:, (t % 2) * P:(t % 2) * P + P], P, heads_back)
            residual(1, ps6[:, 0:D], "l0x_bo")
            norm(2, x[:], xh[:])
            norm(3, xh[:], xh[:])
            tokens_t(1, "l0a_w", "l0a_b")
            own(nc.vector.memset(r0.qbd, 0.0))
            dve.wait_ge(S.sa_qkv, 1)
            own.wait()
            own(nc.vector.tensor_copy(r0.kt, ps23[:, 0:P]))
            own(nc.vector.tensor_copy(r0.v, ps23[:, P:P + 64]))
            src = ps01[:, 0:512].rearrange("p (h b k) -> p h b k", h=4, b=B)
            for i in range(2):
                for b in range(B):
                    h = slice(64 * i, 64 * i + 64)
                    ins = nc.vector.tensor_scalar(r0.qbd[h, b, :, 64 * i:64 * i + 64], src[h, :, b, :], 64 ** -0.5,
                                                  None, ALU.mult)
            ins.then_inc(S.sa_q, 1)
            dve.wait_ge(S.sa_s, 1)
            s8 = ps45[:, 0:512].rearrange("p (a k) -> p a k", a=8)
            p8 = r0.p.rearrange("p h b k -> p (h b) k")
            own(nc.vector.tensor_reduce(r0.mx, s8, AX.X, ALU.max))
            own.wait()
            nc.vector.tensor_tensor(p8, s8, bc(r0.mx, LQ), ALU.subtract).then_inc(S.sa_max, 1)
            dve.wait_ge(S.sa_exp, 1)
            own(nc.vector.tensor_reduce(r0.sum, p8, AX.X, ALU.add))
            own.wait()
            own(nc.vector.reciprocal(r0.rinv, r0.sum))
            own.wait()
            nc.vector.tensor_tensor(p8, p8, bc(r0.rinv, LQ), ALU.mult).then_inc(S.sa_norm, 1)
            dve.wait_ge(S.sa_pt, 1)
            nc.vector.tensor_copy(r0.pt, ps01[:, 0:512].rearrange("p (h k) -> p h k", h=4)).then_inc(S.sa_ptc, 1)
            dve.wait_ge(S.sa_ot, 1)
            for b in range(B):
                ins = nc.vector.tensor_copy(r0.ot[:, :, b * LQ:(b + 1) * LQ],
                                            halves[2 + b][:, 0:D].rearrange("p (h k) -> p h k", h=4))
            ins.then_inc(S.sa_otc, 1)
            dve.wait_ge(S.out_psum, 2)
            own(nc.vector.tensor_copy(r0.o, ps6[:, 0:D]))
            own.wait()
            norm(4, r0.o, r0.o)
            own(nc.vector.tensor_tensor(r0.o, r0.o, row("l0a_ow"), ALU.mult))
            own.wait()
            own(nc.vector.tensor_tensor(r0.o, r0.o, row("l0a_ob"), ALU.add))
            own.wait()
            own(nc.vector.tensor_tensor(x[:], x[:], r0.o, ALU.add))
            own.wait()
            norm(5, x[:], xh[:])
            tokens_t(2)
            mixture(0)

            def cross16(i, stage, bq, bv):
                dve.wait_ge(S.q16_psum, i + 1)
                for c in range(C):
                    own(nc.vector.tensor_scalar(n16.qt[:, c, :], ps6[:, c * P:(c + 1) * P], col(bq, c), 0.25,
                                                ALU.add, ALU.mult))
                own.wait()
                dve.wait_ge(S.hi_ready, (HI_BASE[0], HI_BASE[2])[i] + 1)
                own(nc.vector.tensor_copy(n16.qthi.bitcast(F32R), n16.qt))
                own.wait()
                nc.vector.tensor_tensor(n16.qtlo, n16.qt, n16.qthi, ALU.subtract).then_inc(S.q16_split, 1)
                for j in range(8):
                    nc.vector.tensor_scalar(n16.qhi[:, :, :, j, :], n16.qthi.rearrange("p c (b k) -> p c b k", b=B),
                                            head8[:, j:j + 1], None, ALU.mult).then_inc(S.q16_ready, 1)
                base = ATT_BASE[stage]

                def o_of(u):
                    cb, g = u // 4, u % 4
                    return n16.o[:, cb // 2, cb % 2, 32 * g:32 * g + 32]

                attention(stage, 16, plain_max(base, lambda t: (ps01, ps23)[t % 2][:]), lambda t: n16.pt[:, t % 2, :],
                          o_of, 32)
                dve.wait_ge(S.o16_psum, i + 1)
                src = ps6[:, 0:512].rearrange("p (c b j k) -> p c b j k", c=C, b=B, j=2)
                ot = n16.ot.rearrange("p c (b k) -> p c b k", b=B)
                tmp = n16.tmp.rearrange("p c (b k) -> p c b k", b=B)
                for c in range(C):
                    own(nc.vector.tensor_scalar(tmp[:, c], src[:, c, :, 0, :], parity[:, 0:1], col(bv, c),
                                                ALU.mult, ALU.add))
                own.wait()
                for c in range(C):
                    ins = nc.vector.scalar_tensor_tensor(ot[:, c], src[:, c, :, 1, :], parity[:, 1:2], tmp[:, c],
                                                         ALU.mult, ALU.add)
                ins.then_inc(S.o16_ready, 1)

            norm(6, x[:], xh[:])
            tokens_t(3)
            cross16(0, "l1x", "l1x_bq", "l1x_bv")
            residual(3, ps6[:, 0:D], "l1x_bo")
            norm(7, x[:], xh[:])
            tokens_t(4)
            own(nc.vector.memset(cv.a, 0.0))
            own(nc.vector.memset(cv.full, 0.0))
            own(nc.vector.tensor_scalar(cv.nb, bits, -1.0, 1.0, ALU.mult, ALU.add))
            dve.wait_ge(S.conv_s, 1)
            own(nc.vector.tensor_tensor(cv.w, ps6[:, 0:32], row("l1a_b"), ALU.add))
            own.wait()
            nc.vector.tensor_reduce(cv.mx, cv.w, AX.X, ALU.max, negate=True).then_inc(S.conv_max, 1)
            dve.wait_ge(S.conv_exp, 1)
            own(nc.vector.reciprocal(cv.rs, cv.sum))
            own.wait()
            own(nc.vector.tensor_scalar(cv.a[:, 0, 0:32], cv.w, cv.rs, None, ALU.mult))
            own.wait()
            for i in range(6):
                src, dst, sh = cv.a[:, i % 2, :], cv.a[:, (i + 1) % 2, :], 1 << i
                own(nc.vector.tensor_scalar(dst, src, cv.nb[:, i:i + 1], None, ALU.mult))
                own.wait()
                own(nc.vector.scalar_tensor_tensor(dst[:, sh:LQ], src[:, 0:LQ - sh], bits[:, i:i + 1], dst[:, sh:LQ],
                                                   ALU.mult, ALU.add))
                own.wait()
            for b in range(B):
                h = slice(b * LQ, (b + 1) * LQ)
                ins = nc.vector.tensor_copy(cv.full[h, h], cv.a[h, 0, :])
            ins.then_inc(S.conv_a, 1)
            dve.wait_ge(S.conv_at, 1)
            nc.vector.tensor_copy(cv.at, ps6[:, 32:32 + P]).then_inc(S.conv_atc, 1)
            dve.wait_ge(S.conv_y, 1)
            own(nc.vector.tensor_tensor(x[:], x[:], ps6[:, 256:512], ALU.add))
            own.wait()
            norm(8, x[:], xh[:])
            tokens_t(5)
            mixture(1)
            norm(9, x[:], xh[:])
            tokens_t(6)
            own(nc.vector.memset(n64.qz, 0.0))
            own.wait()
            dve.wait_ge(S.qa_psum, 1)
            for hh in range(2):
                pairs = slice(4 * hh, 4 * hh + 4)
                for j in range(2):
                    h = slice(64 * j, 64 * j + 64)
                    ins = nc.vector.tensor_scalar(n64.qz[h, pairs, j, :],
                                                  ps01[h].rearrange("p (h k) -> p h k", h=8)[:, pairs, :], 64 ** -0.5,
                                                  None, ALU.mult)
                ins.then_inc(S.qa_ready, 1)
            for hh in range(2):
                dve.wait_ge(S.h1_psum, hh + 1)
                for b in range(B):
                    src = ps23[:].rearrange("p (h b q) -> p h b q", b=B, q=LQ)[:, :, b, :]
                    dst = n64.qa[:, b, 8 * hh:8 * hh + 8, :]
                    nc.vector.tensor_copy(dst, src).then_inc(S.h1_dve, 1)
                dve.wait_ge(S.h1_dve, (hh + 1) * B)
                heads = slice(8 * hh, 8 * hh + 8)
                dve.wait_ge(S.hi_ready, HI_BASE[1] + 5 + 2 * hh)
                nc.vector.tensor_tensor(n64.alo[:, 0, heads], n64.qa[:, 0, heads], n64.ahi[:, 0, heads].bitcast(F32),
                                        ALU.subtract).then_inc(S.qlo_ready, 1)
                dve.wait_ge(S.hi_ready, HI_BASE[1] + 6 + 2 * hh)
                nc.vector.tensor_tensor(n64.blo[0:CB, 0, heads], n64.qb[0:CB, 0, heads],
                                        n64.bhi[0:CB, 0, heads].bitcast(F32), ALU.subtract).then_inc(S.qlo_ready, 1)

            def context_back(u):
                b, hp = u // 8, u % 8
                nc.vector.tensor_copy(n64.opa[:, b, 2 * hp:2 * hp + 2, :],
                                      ps7[:, 0:P].rearrange("p (h q) -> p h q", h=2))
                return nc.vector.tensor_copy(n64.opb[CB:P, b, 2 * hp:2 * hp + 2, :],
                                             ps7[0:CB, P:2 * P].rearrange("p (h q) -> p h q", h=2))

            attention("l2x", 16, plain_max(20, lambda t: (ps01, ps23)[t % 2][:]), lambda t: n64.pt[:, t % 2, :],
                      lambda u: n64.o[:, u % 2, :], CD, context_back)
            dve.wait_ge(S.ot_psum, 1)
            nc.vector.tensor_copy(n64.ot, ps01[:].rearrange("p (h k) -> p h k", h=8)).then_inc(S.ot_ready, 1)
            residual(4, ps6[:, 0:D], "l2x_bo")
            norm(10, x[:], xh[:])
            tokens_t(7)
            ttt(dve, own, bc, inverse_sqrt)
            residual(5, ps6[:, 0:D], "l2a_pb")
            norm(11, x[:], xh[:])
            tokens_t(8)
            mixture(2)
            norm(12, x[:], xh[:])
            tokens_t(9)
            cross16(1, "l3x", "l3x_bq", "l3x_bv")
            residual(6, ps6[:, 0:D], "l3x_b2")
            norm(13, x[:], xh[:])
            tokens_t(10)
            dve.wait_ge(S.g_psum, 1)
            for c in range(C):
                own(nc.vector.tensor_scalar(gr.t[:, c, :], ps01[:, 512 + c * P:512 + (c + 1) * P], col("l3a_bh", c),
                                            None, ALU.add))
            dve.wait_ge(S.g_z, 1)
            own.wait()
            own(nc.vector.tensor_scalar(gr.a, gr.z, -1.0, 1.0, ALU.mult, ALU.add))
            own(nc.vector.tensor_tensor(gr.b, gr.z, gr.t, ALU.mult))
            own.wait()
            own(nc.vector.tensor_scalar(gr.a, gr.a, 1e-8, None, ALU.add))
            own.wait()
            for c in range(C):
                for b in range(B):
                    k = slice(b * LQ, (b + 1) * LQ)
                    nc.vector.tensor_tensor_scan(gr.h[:, c, k], gr.a[:, c, k], gr.b[:, c, k], 0.0, ALU.mult, ALU.add)\
                        .then_inc(S.g_scan, 1)
            dve.wait_ge(S.g_back, 1)
            own(nc.vector.tensor_tensor(x[:], x[:], ps6[:, 0:D], ALU.add))
            own.wait()
            norm(14, x[:], xh[:])
            tokens_t(11)
            mixture(3)

        def pe_ttt(pe, context16):
            mm = nc.tensor.matmul
            W = lambda name, *shape: weight(wa, L2A, name, *shape)
            gate, val, proj, projt = W("gate", C, 1024), W("val", C, 1024), W("proj", 8, D), W("projt", C, 1024)
            pe.wait_ge(S.in_l2a, 16)
            w = W("qkv", C, 3 * D)
            for n0, n1 in ((0, 512), (512, 768)):
                for c in range(C):
                    ins = mm(ps01[:, n0:n1], xt[:, c, :], w[:, c, n0:n1], start=(c == 0), stop=(c == 1))
            ins.then_inc(S.t_qkv, 1)
            pe.wait_ge(S.in_l3x, 16)
            pe.wait_ge(S.in_ctxt, 32)
            context16(1, range(0, 6))
            pe.wait_ge(S.t_qk, 2)
            for a in range(2):
                for c in range(C):
                    ins = nc.tensor.transpose(ps6[:, (2 * a + c) * P:(2 * a + c + 1) * P],
                                              tt.qkv[:, 1 - a, c * P:(c + 1) * P], ident)
            ins.then_inc(S.t_kqt, 1)
            pe.wait_ge(S.t_kqtc, 1)
            kt, qt = tt.kqt[:, 0], tt.kqt[:, 1]
            for a, r in ((0, kt), (1, qt)):
                for c in range(C):
                    ins = mm(ps7[:, a * P:(a + 1) * P], kt[:, c, :], r[:, c, :], start=(c == 0), stop=(c == 1))
            ins.then_inc(S.t_gram, 1)

            def through(bank, weights, rhs, updates):
                for f in range(8):
                    terms = [(weights[:, c, f * P:(f + 1) * P], rhs[:, c, :]) for c in range(C)]
                    terms += [(d[:, f, :], r) for d, r in updates]
                    for i, (l, r) in enumerate(terms):
                        ins = mm(bank[:, f * P:(f + 1) * P], l, r, start=(i == 0), stop=(i == len(terms) - 1))
                return ins

            def gram(dst, l, r):
                for f in range(l.shape[1]):
                    ins = mm(dst, l[:, f, :], r[:, f, :], start=(f == 0), stop=(f == l.shape[1] - 1))
                return ins

            def back(bank, src):
                for f in range(8):
                    ins = nc.tensor.transpose(bank[:, f * P:(f + 1) * P], src[:, f, :], ident)
                return ins

            for s in range(2):
                if s == 1:
                    pe.wait_ge(S.t_rc, 1)
                if s == 0:
                    pe.wait_ge(S.t_gramc, 1)
                ug = [(tt.dan[:, 0], tt.tmp[:, 0])] if s else []
                uv = [(tt.dbn[0], tt.tmp[:, 1])] if s else []
                through(ps01, gate, kt, ug).then_inc(S.t_a, 1)
                if s == 0:
                    pe.wait_ge(S.c_act, 16 + 6)
                through(ps23, val, kt, uv).then_inc(S.t_b, 1)
                context16(1, range(6 + 2 * s, 7 + 2 * s))
                pe.wait_ge(S.t_h, s + 1)
                h = tt.h[:, s]
                if s == 1:
                    gram(ps7[:, 0:P], tt.h[:, 0], h).then_inc(S.t_x, 1)
                    pe.wait_ge(S.t_xc, 1)
                    mm(ps7[:, P:2 * P], tt.m[0][2][:, 1], tt.tmp[:, 2], start=True, stop=True).then_inc(S.t_z, 1)
                    pe.wait_ge(S.t_zc, 1)
                for f in range(8):
                    ins = mm(ps6[:, 0:D], h[:, f, :], proj[:, f, :], start=(f == 0), stop=(f == 7 and s == 0))
                if s == 1:
                    ins = mm(ps6[:, 0:D], tt.tmp[:, 3], tt.en[:, 0], start=False, stop=True)
                ins.then_inc(S.t_pred, 1)
                pe.wait_ge(S.c_act, 16 + 7 + 2 * s)
                back(ps45, h).then_inc(S.t_back, 1)
                gram(ps7[:, 2 * P:3 * P], h, h)
                pe.wait_ge(S.t_e, s + 1)
                for c in range(C):
                    ins = nc.tensor.transpose(ps6[:, D + c * P:D + (c + 1) * P], tt.en[:, s, c * P:(c + 1) * P], ident)
                ins.then_inc(S.t_et, 1)
                pe.wait_ge(S.t_etc, s + 1)
                et = tt.et[:, s]
                if s == 1:
                    gram(ps7[:, 0:P], tt.et[:, 0], et).then_inc(S.t_x, 1)
                    pe.wait_ge(S.t_xc, 2)
                    mm(ps7[:, P:2 * P], tt.m[0][2][:, 0], tt.tmp[:, 4], start=True, stop=True).then_inc(S.t_z, 1)
                    pe.wait_ge(S.t_zc, 2)
                gram(ps7[:, 3 * P:4 * P], et, et).then_inc(S.t_sh, 1)
                through(ps01, projt, et, [(tt.hn[:, 0], tt.tmp[:, 5])] if s else []).then_inc(S.t_dh, 1)
                context16(1, range(7 + 2 * s, 8 + 2 * s))
                pe.wait_ge(S.t_da, s + 1)
                gram(ps6[:, 0:P], tt.tb, tt.tb)
                gram(ps6[:, P:2 * P], tt.w, tt.w).then_inc(S.t_s, 1)
                pe.wait_ge(S.c_act, 16 + 8 + 2 * s)
                back(ps23, tt.tb).then_inc(S.t_back, 1)
                pe.wait_ge(S.t_backc, 3 * s + 1)
                back(ps45, tt.w).then_inc(S.t_back, 1)
                pe.wait_ge(S.t_tr, s + 1)
                mm(ps7[:, 0:3], ones, tt.tr, start=True, stop=True).then_inc(S.t_trp, 1)
                pe.wait_ge(S.t_backc, 3 * s + 3)
                c_of = (tt.gram[:, 0], tt.gram[:, 0], tt.sh[:, 1])
                s_of = (tt.sgv[:, 0], tt.sgv[:, 1], tt.sh[:, 0])
                n1 = 3 * NS_ITERS * s + 1
                for c in range(3):
                    pe.wait_ge(S.n_wc, n1 + c)
                    mm(halves[c][:, 2 * P:3 * P], tt.wm[c], c_of[c], start=True, stop=True)
                    mm(halves[c][:, 3 * P:4 * P], c_of[c], tt.wm[c], start=True, stop=True).then_inc(S.n_e, 1)
                for c in range(3):
                    pe.wait_ge(S.n_ec, n1 + c)
                    mm(halves[3 + c][:, 0:P], tt.e[c][:, 1], tt.e[c][:, 0], start=True, stop=True)
                    mm(halves[3 + c][:, P:2 * P], tt.e[c][:, 0], tt.e[c][:, 1], start=True, stop=True).then_inc(S.n_p, 1)
                with pe.Fori(0, NS_ITERS - 1) as it:
                    n0 = 3 * (NS_ITERS - 1) * s + 1
                    for c in range(3):
                        pe.wait_ge(S.n_mc, n1 + c + it * 3)
                        mm(halves[c][:, 0:P], s_of[c], tt.m[s][c][:, 1], start=True, stop=True).then_inc(S.n_u, 1)
                    for c in range(3):
                        pe.wait_ge(S.n_uc, n0 + c + it * 3)
                        mm(halves[c][:, P:2 * P], tt.m[s][c][:, 1], tt.u[c], start=True, stop=True).then_inc(S.n_w, 1)
                    for c in range(3):
                        pe.wait_ge(S.n_wc, n1 + 3 + c + it * 3)
                        mm(halves[c][:, 2 * P:3 * P], tt.wm[c], c_of[c], start=True, stop=True)
                        mm(halves[c][:, 3 * P:4 * P], c_of[c], tt.wm[c], start=True, stop=True).then_inc(S.n_e, 1)
                    for c in range(3):
                        pe.wait_ge(S.n_ec, n1 + 3 + c + it * 3)
                        mm(halves[3 + c][:, 0:P], tt.e[c][:, 0], tt.e[c][:, 1], start=True, stop=True).then_inc(S.n_p, 1)
                    for c in range(3):
                        pe.wait_ge(S.n_pc, n0 + c + it * 3)
                        mm(halves[3 + c][:, P:2 * P], tt.pt[c], tt.m[s][c][:, 0], start=True, stop=True)
                        mm(halves[3 + c][:, 2 * P:3 * P], tt.m[s][c][:, 0], tt.pt[c], start=True, stop=True)\
                            .then_inc(S.n_m, 1)
                pe.wait_ge(S.n_mc, 3 * NS_ITERS * (s + 1))
                if s == 0:
                    for c in range(2):
                        ins = mm(ps6[:, c * P:(c + 1) * P], tt.m[0][c][:, 0], tt.gram[:, 0], start=True, stop=True)
                else:
                    for i, (u, c) in enumerate(((0, 0), (0, 1), (1, 0), (1, 1))):
                        ins = mm(ps6[:, i * P:(i + 1) * P], tt.m[u][c][:, 0], tt.gram[:, 1], start=True, stop=True)
                ins.then_inc(S.t_r, 1)
            pe.wait_ge(S.t_rc, 2)
            through(ps01, gate, qt, [(tt.dan[:, 0], tt.tmp[:, 0]), (tt.dan[:, 1], tt.tmp[:, 2])]).then_inc(S.t_a, 1)
            through(ps23, val, qt, [(tt.dbn[0], tt.tmp[:, 1]), (tt.dbn[1], tt.tmp[:, 3])]).then_inc(S.t_b, 1)
            context16(1, range(10, 11))
            pe.wait_ge(S.t_h, 3)
            h = tt.tb
            for u in range(2):
                ins = gram(ps7[:, u * P:(u + 1) * P], tt.h[:, u], h)
            ins.then_inc(S.t_x, 1)
            pe.wait_ge(S.t_xc, 3)
            for u in range(2):
                ins = mm(ps7[:, (2 + u) * P:(3 + u) * P], tt.m[u][2][:, 1], tt.tmp[:, 4 + u], start=True, stop=True)
            ins.then_inc(S.t_z, 1)
            pe.wait_ge(S.t_zc, 3)
            for d in range(C):
                k = slice(d * P, (d + 1) * P)
                terms = [(proj[:, f, k], h[:, f, :]) for f in range(8)]
                terms += [(tt.en[:, u, k], tt.tmp[:, u]) for u in range(2)]
                for i, (l, r) in enumerate(terms):
                    ins = mm(ps45[:, k], l, r, start=(i == 0), stop=(i == len(terms) - 1))
            ins.then_inc(S.t_o, 1)
            pe.wait_ge(S.t_oc, 1)
            w = W("pw", C, D)
            for c in range(C):
                ins = mm(ps6[:, 0:D], tt.et[:, 0, c, :], w[:, c, :], start=(c == 0), stop=(c == 1))
            ins.then_inc(S.out_psum, 1)

        @block.tensor
        def _(pe):
            mm = nc.tensor.matmul

            def keep_warm(n):
                for _ in range(n):
                    mm(halves[2][:, 0:P], ident, ident, start=True, stop=True)

            def tokens_t(stage, norms_done):
                keep_warm(KEEP[stage])
                pe.wait_ge(S.xh_ready, norms_done)
                for c in range(C):
                    ins = nc.tensor.transpose(ps7[:, c * P:(c + 1) * P], xh[:, c * P:(c + 1) * P], ident)
                ins.then_inc(S.xt_psum, 1)
                pe.wait_ge(S.xt_ready, stage + 1)

            def attention(stage, n, scores, pt_of, v_of, width, tiles, post=None):
                base = ATT_BASE[stage]
                for t in range(n + 2 + (post is not None)):
                    if t < n:
                        if stage == "l0x":
                            if t >= 1:
                                pe.wait_ge(S.att_max, t)
                        elif t >= 2:
                            pe.wait_ge(S.att_exp, base + t - 1)
                        scores(t).then_inc(S.att_s, 1)
                    if 1 <= t <= n:
                        u = t - 1
                        pe.wait_ge(S.att_exp, base + t)
                        if u >= 1:
                            pe.wait_ge(S.att_pta, base + u)
                            pe.wait_ge(S.att_ptd, base + u)
                        src = q.sc[:, u % 2, :] if stage == "l0x" else \
                            (n64.p if stage == "l2x" else n16.p)[:, u % 2, :]
                        for k in range(tiles):
                            dst = ps45[:, k * P:(k + 1) * P] if k < 8 else halves[3][:, 0:P]
                            ins = nc.tensor.transpose(dst, src[:, k * P:(k + 1) * P], ident)
                        ins.then_inc(S.att_pt, 1)
                    if post is not None and t >= 3:
                        u = t - 3
                        pe.wait_ge(S.att_on, base + u + 1)
                        if u >= 1:
                            pe.wait_ge(S.opt_ready, OPT_BASE[stage] + u)
                        post(u).then_inc(S.opt_psum, 1)
                    if 2 <= t < n + 2:
                        u = t - 2
                        pe.wait_ge(S.att_pta, base + u + 1)
                        pe.wait_ge(S.att_ptd, base + u + 1)
                        if u >= 1:
                            pe.wait_ge(S.att_on, base + u)
                        for k in range(tiles):
                            ins = mm(ps6[:, 0:width], pt_of(u)[:, k * P:(k + 1) * P],
                                     v_of(u, k), start=(k == 0), stop=(k == tiles - 1))
                        ins.then_inc(S.att_o, 1)

            def mixture(m):
                base, nu = MOE_BASE[m], MOE_UNITS[m]
                if m == 0:
                    pe.wait_ge(S.in_router, 16)
                for c in range(C):
                    ins = mm(ps7[:, 256:264], xt[:, c, :], router[:, (m * C + c) * E:(m * C + c + 1) * E],
                             start=(c == 0), stop=(c == C - 1))
                ins.then_inc(S.router_psum, 1)
                gated = m >= 2
                down_at = (1 + gated) * C * FU

                def up(s, it, first):
                    par = s % 2
                    pe.wait_ge(slot_full[s], 16 * (base // SLOTS + 1) + it * 16)
                    if not (first and s < 2):
                        pe.wait_ge(S.moe_h, base + s - 1 + it * SLOTS)
                    w = ring[:, s, 0:down_at].rearrange("p (g c f) -> p g c f", g=1 + gated, c=C)
                    for g in range(1 + gated):
                        for fc in range(FC):
                            for c in range(C):
                                ins = mm(halves[2 * g + par][:, fc * P:(fc + 1) * P], w[:, g, c, fc * P:(fc + 1) * P],
                                         xt[:, c, :], start=(c == 0), stop=(c == C - 1))
                    ins.then_inc(S.moe_up, 1)

                def down(s, value):
                    par = s % 2
                    pe.wait_ge(S.moe_h, value)
                    if not (isinstance(value, int) and value - 2 <= 0):
                        pe.wait_ge(S.moe_acc, value - 2)
                    for fc in range(FC):
                        ins = mm(halves[4 + par][:, 0:D], mo.h[:, par, fc * P:(fc + 1) * P],
                                 ring[:, s, down_at + fc * D:down_at + (fc + 1) * D],
                                 start=(fc == 0), stop=(fc == FC - 1))
                    ins.then_inc(S.moe_y, 1)

                def lot(it):
                    for s in range(SLOTS):
                        first = isinstance(it, int) and it == 0
                        up(s, it, first)
                        if not (first and s == 0):
                            down((s - 1) % SLOTS, base + s + it * SLOTS)

                lot(0)
                if m in (1, 3):
                    pe.wait_ge(S.comb_ready, m + 1)
                    if m == 1:
                        pe.wait_ge(S.in_e8, 16)
                    nc.tensor.transpose(ps7[0:E, 264:264 + P], mo.comb, ident).then_inc(S.combt_psum, 1)
                    pe.wait_ge(S.combt_ready, m // 2 + 1)
                    mm(ps7[:, 0:D], mo.combt[0:E, :], e8[:, (m // 2) * D:(m // 2 + 1) * D], start=True, stop=True)\
                        .then_inc(S.b2_psum, 1)
                if nu // SLOTS == 2:
                    lot(1)
                else:
                    with pe.Fori(1, nu // SLOTS) as it:
                        lot(it)
                down(SLOTS - 1, base + nu)

            W = lambda name, *shape: weight(wa, L0X, name, *shape)
            pe.wait_ge(S.in_const, 16)
            tokens_t(0, 2)
            pe.wait_ge(S.in_l0x, 16)
            for c in range(C):
                ins = mm(ps6[:, 0:D], xt[:, c, :], W("wq", C, D)[:, c, :], start=(c == 0), stop=(c == 1))
            ins.then_inc(S.q_psum, 1)
            def keys_values(i):
                j = L0X_ORDER[i]
                if j < KT:
                    pe.wait_ge(S.xn_act, j // 4 + 1)
                    pe.wait_ge(S.xn_dve, j // 4 + 1)
                if i >= 2:
                    pe.wait_ge(S.kv_v, i - 1)
                dst, k = halves[2 + i % 2], slice(j * P, (j + 1) * P)
                if j < KT:
                    w = W("wkv", C, 2 * D)
                    mm(dst, xnt[:, 0, k], w[:, 0, :], start=True, stop=False)
                    ins = mm(dst, xnt[0:CB, 1, k], w[0:CB, 1, :], start=False, stop=True)
                else:
                    w = W("wlkv", C, 2 * D)
                    mm(dst, xt[:, 0, :], w[:, 0, :], start=True, stop=False)
                    ins = mm(dst, xt[:, 1, :], w[:, 1, :], start=False, stop=True)
                ins.then_inc(S.kv_psum, 1)

            def rows_t(g):
                pe.wait_ge(S.xn_ready, 4 * g + 4)
                if g >= 1:
                    pe.wait_ge(S.xn_act, g)
                    pe.wait_ge(S.xn_dve, g)
                for i in range(4):
                    xn = q.xn[:, (4 * g + i) % 8, :]
                    nc.tensor.transpose(halves[0][:, i * P:(i + 1) * P], xn[:, 0:P], ident)
                    ins = nc.tensor.transpose(halves[1][0:CB, i * P:(i + 1) * P], xn[:, P:CD], ident)
                ins.then_inc(S.xn_psum, 1)

            rows_t(0)
            keys_values(0)
            for g in range(1, KT // 4):
                rows_t(g)
                for i in range(4 * g - 3, 4 * g + 1):
                    keys_values(i)
            for i in range(KT - 3, KT + 1):
                keys_values(i)
            pe.wait_ge(S.q_norm, 1)
            for c in range(C):
                ins = nc.tensor.transpose(ps6[:, 256 + c * P:256 + (c + 1) * P], xh[:, c * P:(c + 1) * P], ident)
            ins.then_inc(S.qt_psum, 1)
            for g, (first, n) in enumerate(L0X_GROUPS):
                pe.wait_ge(S.khat_ready, 2 * g + 1)
                if g == 8:
                    pe.wait_ge(S.kt_dve, 1)
                elif g >= 2:
                    pe.wait_ge(S.kt_act, g - 1)
                for i in range(n):
                    for c in range(C):
                        ins = nc.tensor.transpose(halves[4 + g % 2][:, (c * n + i) * P:(c * n + i + 1) * P],
                                                  q.knat[:, first + i, c * P:(c + 1) * P], ident)
                ins.then_inc(S.kt_psum, 1)
            pe.wait_ge(S.qbd_ready, 1)
            pe.wait_ge(S.kt_dve, 2)
            pe.wait_ge(S.kt_act, 7)

            def scores_l0x(t):
                b, hp = t // 2, t % 2
                bank = ps01
                mm(bank[:, 0:512], q.qbd[:, b, hp, :], q.kt[:, hp, b * KEYS:b * KEYS + 512], start=True, stop=True)
                mm(bank[:, 512:1024], q.qbd[:, b, hp, :], q.kt[:, hp, b * KEYS + 512:(b + 1) * KEYS], start=True, stop=True)
                return mm(halves[2][:, 0:P], q.qbd[:, b, hp, :], q.kt[:, hp, KT * P:(KT + 1) * P],
                          start=True, stop=True)

            attention("l0x", 4, scores_l0x, lambda u: q.pt[:, u % 2, :],
                      lambda u, k: q.v[:, (u // 2) * KTB + k if k < KTB else KT, (u % 2) * P:(u % 2) * P + P], P, 9,
                      lambda u: nc.tensor.transpose(ps7[:, 0:P], xh[:, (u % 2) * P:(u % 2) * P + P], ident))
            pe.wait_ge(S.opt_ready, 4)
            for c in range(C):
                ins = mm(ps6[:, 0:D], xt[:, c, :], W("wo", C, D)[:, c, :], start=(c == 0), stop=(c == 1))
            ins.then_inc(S.out_psum, 1)

            def context16(i, shares):
                W = lambda name, *shape: weight((wa, wb)[i], (L1X, L3X)[i], name, *shape)
                ct = carve(ctxt, 0, C, B * KEYS)
                if 16 * i + shares[0] > 0:
                    pe.wait_ge(S.c_act, 16 * i + shares[0])
                for j in shares:
                    if j >= shares[0] + 2:
                        pe.wait_ge(S.c_act, 16 * i + j - 1)
                    dst = halves[SHARE_BANKS[i][j]]
                    if j < 8:
                        c, kb = j // 4, j % 4
                        k = slice(kb * 512, (kb + 1) * 512)
                        w = W("wk", C, D)
                        mm(dst, w[:, 0, c * P:(c + 1) * P], ct[:, 0, k], start=True, stop=False)
                        ins = mm(dst, w[0:CB, 1, c * P:(c + 1) * P], ct[0:CB, 1, k], start=False, stop=True)
                    else:
                        w = W("wv", C, D)
                        for a in range(2):
                            kt = 2 * (j - 8) + a
                            k = slice(kt * P, (kt + 1) * P)
                            mm(dst[:, a * D:(a + 1) * D], ct[:, 0, k], w[:, 0, :], start=True, stop=False)
                            ins = mm(dst[:, a * D:(a + 1) * D], ct[0:CB, 1, k], w[0:CB, 1, :], start=False, stop=True)
                    ins.then_inc(S.c_psum, 1)

            W = lambda name, *shape: weight(wb, L0A, name, *shape)
            pe.wait_ge(S.in_l1x, 16)
            pe.wait_ge(S.in_ctxt, 16)
            context16(0, range(0, 5))
            tokens_t(1, 4)
            pe.wait_ge(S.in_l0a, 16)
            for h in range(4):
                for c in range(C):
                    mm(ps01[:, h * P:(h + 1) * P], W("wq", C, 512)[:, c, h * P:(h + 1) * P], xt[:, c, :],
                       start=(c == 0), stop=(c == 1))
            for c in range(C):
                mm(ps23[:, 0:P], W("wk", C, P)[:, c, :], xt[:, c, :], start=(c == 0), stop=(c == 1))
            for c in range(C):
                ins = mm(ps23[:, P:P + 64], xt[:, c, :], W("wv", C, 64)[:, c, :], start=(c == 0), stop=(c == 1))
            ins.then_inc(S.sa_qkv, 1)
            context16(0, range(5, 7))
            pe.wait_ge(S.sa_q, 1)
            for h in range(4):
                for b in range(B):
                    ins = mm(ps45[:, (h * 2 + b) * LQ:(h * 2 + b + 1) * LQ], r0.qbd[:, b, h, :],
                             r0.kt[:, b * LQ:(b + 1) * LQ], start=True, stop=True)
            ins.then_inc(S.sa_s, 1)
            context16(0, range(7, 10))
            pe.wait_ge(S.sa_norm, 1)
            for h in range(4):
                ins = nc.tensor.transpose(ps01[:, h * P:(h + 1) * P], r0.p[:, h].rearrange("p b k -> p (b k)"), ident)
            ins.then_inc(S.sa_pt, 1)
            context16(0, range(10, 11))
            pe.wait_ge(S.sa_ptc, 1)
            for h in range(4):
                for b in range(B):
                    for j in range(2):
                        k = slice(b * LQ, (b + 1) * LQ)
                        ins = mm(halves[2 + b][64 * j:64 * j + 64, h * LQ:(h + 1) * LQ], r0.v[k, :],
                                 r0.pt[k, h, 64 * j:64 * j + 64], start=True, stop=True)
            ins.then_inc(S.sa_ot, 1)
            context16(0, range(11, 12))
            pe.wait_ge(S.sa_otc, 1)
            for h in range(4):
                ins = mm(ps6[:, 0:D], r0.ot[:, h, :], W("wo", 4, D)[:, h, :], start=(h == 0), stop=(h == 3))
            ins.then_inc(S.out_psum, 1)
            context16(0, range(12, 16))
            tokens_t(2, 6)
            pe.wait_ge(S.c_act, 16)
            mixture(0)

            def cross16(i, stage, wt, tab, norms_done):
                W = lambda name, *shape: weight(wt, tab, name, *shape)
                tokens_t((3, 9)[i], norms_done)
                for c in range(C):
                    for cc in range(C):
                        ins = mm(ps6[:, c * P:(c + 1) * P], W("wq", C, D)[:, cc, c * P:(c + 1) * P], xt[:, cc, :],
                                 start=(cc == 0), stop=(cc == 1))
                ins.then_inc(S.q16_psum, 1)
                pe.wait_ge(S.c_act, 16 * i + 16)

                def scores(t):
                    if t % 4 == 0:
                        pe.wait_ge(S.lo_ready, (0, 10)[i] + t // 4 + 1)
                    if t < 4:
                        pe.wait_ge(S.q16_ready, 8 * i + 2 * t + 2)
                        pe.wait_ge(S.q16_low, 8 * i + 2 * t + 2)
                    cb, g = t // 4, t % 4
                    c, b = cb // 2, cb % 2
                    qhi, qlo = (w[:, c, b, 2 * g:2 * g + 2, :].rearrange("p j k -> p (j k)")
                                for w in (n16.qhi, n16.qlo))
                    for k in range(2):
                        dst = (ps01, ps23)[t % 2][:, k * 512:(k + 1) * 512]
                        khi, klo = (w[:, c, b * KEYS + k * 512:b * KEYS + (k + 1) * 512]
                                    for w in (n16.khi, n16.klo))
                        mm(dst, qhi, khi, start=True, stop=False)
                        mm(dst, qlo, khi, start=False, stop=False)
                        ins = mm(dst, qhi, klo, start=False, stop=True)
                    return ins

                def values(u, k):
                    cb, g = u // 4, u % 4
                    at = (cb // 2) * P + 32 * g
                    return n16.v[:, (cb % 2) * KTB + k, at:at + 32]

                attention(stage, 16, scores, lambda u: n16.pt[:, u % 2, :], values, 32, 8)
                pe.wait_ge(S.att_on, ATT_BASE[stage] + 16)
                for c in range(C):
                    for b in range(B):
                        ins = nc.tensor.transpose(ps6[:, (c * 2 + b) * P:(c * 2 + b + 1) * P], n16.o[:, c, b, :], ident)
                ins.then_inc(S.o16_psum, 1)
                pe.wait_ge(S.o16_ready, i + 1)

            cross16(0, "l1x", wa, L1X, 7)
            w = weight(wa, L1X, "wo", C, D)
            for c in range(C):
                ins = mm(ps6[:, 0:D], n16.ot[:, c, :], w[:, c, :], start=(c == 0), stop=(c == 1))
            ins.then_inc(S.out_psum, 1)
            tokens_t(4, 8)
            w = weight(wa, L1X, "l1a_w", C, 32)
            for c in range(C):
                ins = mm(ps6[:, 0:32], xt[:, c, :], w[:, c, :], start=(c == 0), stop=(c == 1))
            ins.then_inc(S.conv_s, 1)
            pe.wait_ge(S.conv_a, 1)
            nc.tensor.transpose(ps6[:, 32:32 + P], cv.full, ident).then_inc(S.conv_at, 1)
            pe.wait_ge(S.conv_atc, 1)
            mm(ps6[:, 256:512], cv.at, xh[:], start=True, stop=True).then_inc(S.conv_y, 1)
            tokens_t(5, 9)
            mixture(1)
            W = lambda name, *shape: weight(wb, L2X, name, *shape)
            tokens_t(6, 10)
            pe.wait_ge(S.in_l2x, 16)
            for h in range(8):
                for c in range(C):
                    ins = mm(ps01[:, h * P:(h + 1) * P], W("wq", C, 1024)[:, c, h * P:(h + 1) * P], xt[:, c, :],
                             start=(c == 0), stop=(c == 1))
            ins.then_inc(S.qa_psum, 1)
            for hh in range(2):
                pe.wait_ge(S.qa_ready, hh + 1)
                if hh == 1:
                    pe.wait_ge(S.h1_dve, B)
                    pe.wait_ge(S.h1_act, B)
                for i in range(4):
                    pair = 4 * hh + i
                    w, two = W("wk", 8, CD)[:, pair, :], n64.qz[:, pair].rearrange("p j k -> p (j k)")
                    dst = slice(i * 2 * P, (i + 1) * 2 * P)
                    mm(ps23[:, dst], w[:, 0:P], two, start=True, stop=True)
                    ins = mm(ps45[0:CB, dst], w[:, P:CD], two, start=True, stop=True)
                ins.then_inc(S.h1_psum, 1)
            pe.wait_ge(S.h1_dve, 2 * B)
            pe.wait_ge(S.h1_act, 2 * B)

            def scores64(t):
                b, hp = t // 8, t % 8
                if t == 0:
                    pe.wait_ge(S.qlo_ready, 2)
                    pe.wait_ge(S.lo_ready, 4 + 2)
                if t == 4:
                    pe.wait_ge(S.qlo_ready, 4)
                if t == 8:
                    pe.wait_ge(S.lo_ready, 4 + 6)
                heads = slice(2 * hp, 2 * hp + 2)
                ahi, alo = (w[:, b, heads, :].rearrange("p h q -> p (h q)") for w in (n64.ahi, n64.alo))
                bhi, blo = (w[0:CB, b, heads, :].rearrange("p h q -> p (h q)") for w in (n64.bhi, n64.blo))
                for k in range(2):
                    keys = slice(b * KEYS + k * 512, b * KEYS + (k + 1) * 512)
                    dst = (ps01, ps23)[t % 2][:, k * 512:(k + 1) * 512]
                    chi, clo = (w[:, 0, keys] for w in (n64.chi, n64.clo))
                    dhi, dlo = (w[0:CB, 1, keys] for w in (n64.chi, n64.clo))
                    mm(dst, ahi, chi, start=True, stop=False)
                    mm(dst, bhi, dhi, start=False, stop=False)
                    mm(dst, alo, chi, start=False, stop=False)
                    mm(dst, blo, dhi, start=False, stop=False)
                    mm(dst, ahi, clo, start=False, stop=False)
                    ins = mm(dst, bhi, dlo, start=False, stop=True)
                return ins

            def context_out(u):
                nc.tensor.transpose(ps7[:, 0:P], n64.o[:, u % 2, 0:P], ident)
                return nc.tensor.transpose(ps7[0:CB, P:2 * P], n64.o[:, u % 2, P:CD], ident)

            attention("l2x", 16, scores64, lambda u: n64.pt[:, u % 2, :],
                      lambda u, k: ctxn[:, ((u // 8) * KTB + k) * CD:((u // 8) * KTB + k + 1) * CD], CD, 8, context_out)
            pe.wait_ge(S.opt_ready, 4 + 16)
            for h in range(16):
                dst = ps01[64 * (h % 2):64 * (h % 2) + 64, (h // 2) * P:(h // 2 + 1) * P]
                w = W("wv", 2, 1024)[:, :, h * 64:(h + 1) * 64]
                mm(dst, w[:, 0, :], n64.opa[:, :, h, :], start=True, stop=False)
                ins = mm(dst, w[CB:P, 1, :], n64.opb[CB:P, :, h, :], start=False, stop=True)
            ins.then_inc(S.ot_psum, 1)
            pe.wait_ge(S.ot_ready, 1)
            for h in range(8):
                ins = mm(ps6[:, 0:D], n64.ot[:, h, :], W("wo", 8, D)[:, h, :], start=(h == 0), stop=(h == 7))
            ins.then_inc(S.out_psum, 1)
            tokens_t(7, 11)
            pe_ttt(pe, context16)
            context16(1, range(11, 14))
            tokens_t(8, 12)
            pe.wait_ge(S.c_act, 16 + 14)
            mixture(2)
            pe.wait_ge(S.moe_acc, MOE_BASE[3])
            context16(1, range(14, 16))
            cross16(1, "l3x", wb, L3X, 13)
            w = weight(wb, L3X, "w1", C, 512)
            for f in range(4):
                for c in range(C):
                    ins = mm(halves[0][:, f * P:(f + 1) * P], w[:, c, f * P:(f + 1) * P], n16.ot[:, c, :],
                             start=(c == 0), stop=(c == 1))
            ins.then_inc(S.m_h, 1)
            pe.wait_ge(S.m_hc, 1)
            w = weight(wb, L3X, "w2", 4, D)
            for f in range(4):
                ins = mm(ps6[:, 0:D], n16.h[:, f, :], w[:, f, :], start=(f == 0), stop=(f == 3))
            ins.then_inc(S.out_psum, 1)
            tokens_t(10, 14)
            pe.wait_ge(S.in_l3a, 16)
            for i, name in enumerate(("wz", "wh")):
                w = weight(wa, L3A, name, C, D)
                for cc in range(C):
                    for c in range(C):
                        ins = mm(ps01[:, i * 512 + cc * P:i * 512 + (cc + 1) * P], w[:, c, cc * P:(cc + 1) * P], xt[:, c, :],
                                 start=(c == 0), stop=(c == 1))
            ins.then_inc(S.g_psum, 1)
            pe.wait_ge(S.g_scan, 4)
            for c in range(C):
                ins = nc.tensor.transpose(ps6[:, c * P:(c + 1) * P], gr.h[:, c, :], ident)
            ins.then_inc(S.g_back, 1)
            tokens_t(11, 15)
            mixture(3)


def chunks(a, np):
    n = -(-a.shape[0] // P)
    if a.shape[0] < n * P:
        full = np.zeros((n * P,) + a.shape[1:], a.dtype)
        full[:a.shape[0]] = a
        a = full
    return a.reshape(n, P, -1).transpose(1, 0, 2).reshape(P, -1)


def pack_units(np, ups, down, per):
    cat = []
    for w in ups:
        cat.append(w.reshape(E, C, P, per, FU).transpose(0, 3, 2, 1, 4).reshape(E * per, P, C * FU))
    cat.append(down.reshape(E, per, FC, P, D).transpose(0, 1, 3, 2, 4).reshape(E * per, P, FC * D))
    return np.ascontiguousarray(np.concatenate(cat, axis=2))


def layout(inp, np):
    g = {k: np.asarray(v) for k, v in inp.items()}
    f = np.float32
    a = {}
    a["x"] = np.ascontiguousarray(g["x"].reshape(P, D))
    rows = g["ctx_768"].reshape(KT * P, CD)
    a["ctx"] = np.ascontiguousarray(rows.reshape(KT, P, CD).transpose(1, 0, 2).reshape(P, KT * CD))
    a["ctxt"] = np.ascontiguousarray(chunks(rows.T, np))
    a["mask"] = np.ascontiguousarray(g["mask_BxS2_bk0"].reshape(B * KEYS))

    def column(v):
        return chunks(v.reshape(-1, 1), np)

    twice = lambda v: np.concatenate([v, v])
    c = {"l0x_lg": g["L0_xattn_ln_l_g"], "l0x_lb": g["L0_xattn_ln_l_b"], "l0x_xg": g["L0_xattn_ln_x_g"],
         "l0x_xb": g["L0_xattn_ln_x_b"], "l0x_qg": twice(g["L0_xattn_qn_g"]), "l0x_kg": twice(g["L0_xattn_kn_g"]),
         "l0a_w": g["L0_attn_norm_w"], "l0a_b": g["L0_attn_norm_b"], "l1x_bq": g["L1_xattn_bq"],
         "l1x_bk": g["L1_xattn_bk"], "l1x_bv": g["L1_xattn_bv"], "l3x_bq": g["L3_xattn_bq"],
         "l3x_bk": g["L3_xattn_bk"], "l3x_bv": g["L3_xattn_bv"], "l3x_b1": g["L3_xattn_b1"],
         "l3a_bz": g["L3_attn_bz"], "l3a_bh": g["L3_attn_bh"], "l1f_b1": g["L1_ffn_b1"].reshape(-1),
         "l3f_b0": g["L3_ffn_b0"].reshape(-1), "l3f_b1": g["L3_ffn_b1"].reshape(-1)}
    a["cols"] = np.ascontiguousarray(np.concatenate([column(c[n]) for n in COLS], axis=1))
    r = {"l0x_bo": "L0_xattn_bo", "l0a_ow": "L0_attn_out_norm_w", "l0a_ob": "L0_attn_out_norm_b",
         "l1x_bo": "L1_xattn_bo", "l1a_b": "L1_attn_b", "l2x_bo": "L2_xattn_b_o", "l2a_pb": "L2_attn_proj_b",
         "l3x_b2": "L3_xattn_b2", "l3f_bg": "L3_ffn_bg"}
    a["rows"] = np.concatenate([g[r[n]] for n in ROWS])
    a["late"] = np.concatenate([g["L2_attn_" + n] for n in ("qkv_b", "qn_scale", "qn_bias", "kn_scale", "kn_bias")])
    a["e8"] = np.ascontiguousarray(np.concatenate([g["L1_ffn_b2"], g["L3_ffn_b2"]], axis=1))
    p = np.arange(P)
    a["const"] = np.concatenate([
        np.eye(P, dtype=f), np.ones((P, P), f), np.broadcast_to(np.arange(E, dtype=f), (P, E)),
        np.stack([(p // 16) % 2 == j for j in range(2)], 1).astype(f),
        np.stack([(p % LQ) >> i & 1 for i in range(6)], 1).astype(f),
        np.full((P, 72), -0.5, f), np.full((P, 32), 0.5, f),
        np.stack([(p // 16) % 8 == j for j in range(8)], 1).astype(f)], axis=1)
    a["router"] = np.ascontiguousarray(np.concatenate(
        [chunks(w, np) for w in (g["L0_ffn_router_w"].T, g["L1_ffn_gate_w"], g["L2_ffn_router_w"].T, g["L3_ffn_Wg"])],
        axis=1))

    def pack(*ws):
        return np.ascontiguousarray(np.concatenate([chunks(w, np) for w in ws], axis=1))

    kv = g["L0_attn_Wkv"]
    a["l0x"] = pack(g["L0_xattn_Wq"].T, g["L0_xattn_Wkv"].T, g["L0_xattn_Wlkv"].T, g["L0_xattn_Wo"].T)
    a["l0a"] = pack(g["L0_attn_Wq"], np.concatenate([kv[:, :64], kv[:, :64]], axis=1), kv[:, 64:], g["L0_attn_Wo"])
    a["l1x"] = pack(g["L1_xattn_Wq"], g["L1_xattn_Wk"], g["L1_xattn_Wv"], g["L1_xattn_Wo"], g["L1_attn_W"].T)
    wv = g["L2_xattn_w_v"]
    low = np.zeros((2 * P, 1024), f)
    low[:P], low[P + CB:] = wv[:P], wv[P:]
    a["l2x"] = pack(g["L2_xattn_w_q"], g["L2_xattn_w_k"].T, low, g["L2_xattn_w_o"])
    a["l2a"] = pack(g["L2_attn_qkv_w"], g["L2_attn_ttt_gate"], g["L2_attn_ttt_val"], g["L2_attn_ttt_proj"],
                    g["L2_attn_ttt_proj"].T, g["L2_attn_proj_w"])
    a["l3x"] = pack(g["L3_xattn_Wq"], g["L3_xattn_Wk"], g["L3_xattn_Wv"], g["L3_xattn_W1"], g["L3_xattn_W2"])
    a["l3a"] = pack(g["L3_attn_Wz"].T, g["L3_attn_Wh"].T)
    a["m0"] = pack_units(np, [g["L0_ffn_w1"]], g["L0_ffn_w2"], 1)
    a["m1"] = pack_units(np, [g["L1_ffn_w1"]], g["L1_ffn_w2"], 2)
    a["m2"] = pack_units(np, [g["L2_ffn_w_gate"].transpose(0, 2, 1), g["L2_ffn_w_up"].transpose(0, 2, 1)],
                         g["L2_ffn_w_down"].transpose(0, 2, 1), 1)
    a["m3"] = pack_units(np, [g["L3_ffn_W1"], g["L3_ffn_W0"]], g["L3_ffn_W2"], 2)
    return a


_ORDER = ["x", "ctx", "ctxt", "mask", "cols", "rows", "late", "e8", "const", "router",
          "l0x", "l0a", "l1x", "l2x", "l2a", "l3x", "l3a", "m0", "m1", "m2", "m3"]


def kernel(**inputs):
    import numpy as _np
    import concourse.bacc as _bacc
    from concourse import mybir as _mybir
    from concourse.bass_utils import run_bass_kernel_spmd as _run

    nc = _bacc.Bacc("TRN2", target_bir_lowering=False, num_devices=1)
    laid = layout(inputs, _np)
    arrays, args = {}, []
    for name in _ORDER:
        arr = laid[name]
        arrays[f"in_{name}_dram"] = arr
        args.append(nc.dram_tensor(f"in_{name}_dram", arr.shape, _mybir.dt.from_np(arr.dtype), kind="ExternalInput").ap())
    args.append(nc.dram_tensor("out_0_dram", (P, D), F32, kind="ExternalOutput").ap())
    perceiver_kernel(nc, *args)
    r = _run(nc, [arrays], core_ids=[0])
    return r.results[0]["out_0_dram"].reshape(B, LQ, D)
```
